# Optimizing a Trainium2 kernel written in Bass

```python
import numpy as np
import jax
import jax.numpy as jnp

def _softmax(x, axis=-1):
    return jax.nn.softmax(x, axis=axis)

def _gelu(x):
    return jax.nn.gelu(x, approximate=True)

def _silu(x):
    return jax.nn.silu(x)

def _sigmoid(x):
    return jax.nn.sigmoid(x)

def _layernorm(x, axis=-1, eps=1e-05):
    m = jnp.mean(x, axis=axis, keepdims=True)
    v = jnp.var(x, axis=axis, keepdims=True)
    return (x - m) / jnp.sqrt(v + eps)

def _scatter_add(tgt, idx, src, axis=0):
    return tgt.at[idx].add(src)

def _segment_sum(src, seg, n):
    return jax.ops.segment_sum(src, seg, n)
kernel_name = 'mk_macaron_d2_jaxref_r8_378aa7'

def setup_inputs(seed: int=0):
    np.random.seed(seed)
    _w = jnp.asarray

    def _L0_attn_setup():
        import jax, jax.numpy as jnp
        import numpy as np
        N_LAYERS = 2
        D_MODEL = 128
        D_INNER = 2 * D_MODEL
        D_STATE = 16
        D_CONV = 4
        DT_RANK = D_MODEL // 16
        B_SZ, L = (1, 256)
        EPS = 1e-05

        def layernorm(x, w, b):
            mu = jnp.mean(x, axis=-1, keepdims=True)
            var = jnp.mean(jnp.square(x - mu), axis=-1, keepdims=True)
            return (x - mu) * jax.lax.rsqrt(var + EPS) * w + b

        def mamba(x, in_w, cw, cb, xp_w, dtp_w, dtp_b, A_log, Dp, out_w):
            Bn, Ln, _ = x.shape
            xz = jnp.einsum('bld,ed->ble', x, in_w)
            xc, z = jnp.split(xz, 2, axis=-1)
            xp = jnp.pad(xc, ((0, 0), (D_CONV - 1, 0), (0, 0)))
            xc = sum((xp[:, k:k + Ln, :] * cw[:, k] for k in range(D_CONV))) + cb
            xc = jax.nn.silu(xc)
            dbl = jnp.einsum('ble,re->blr', xc, xp_w)
            dt, Bm, Cm = jnp.split(dbl, [DT_RANK, DT_RANK + D_STATE], axis=-1)
            dt = jax.nn.softplus(jnp.einsum('blr,er->ble', dt, dtp_w) + dtp_b)
            A = -jnp.exp(A_log)
            dA = jnp.exp(dt[..., None] * A)
            dBu = (dt * xc)[..., None] * Bm[:, :, None, :]

            def step(h, inp):
                dA_t, dBu_t, C_t = inp
                h = dA_t * h + dBu_t
                y = jnp.einsum('ben,bn->be', h, C_t)
                return (h, y)
            h0 = jnp.zeros((Bn, D_INNER, D_STATE), dA.dtype)
            _, ys = jax.lax.scan(step, h0, (dA.transpose(1, 0, 2, 3), dBu.transpose(1, 0, 2, 3), Cm.transpose(1, 0, 2)))
            y = ys.transpose(1, 0, 2) + xc * Dp
            y = y * jax.nn.silu(z)
            return jnp.einsum('ble,de->bld', y, out_w)
        key = jax.random.key(seed)
        ks = jax.random.split(key, 12)
        s = 0.02
        dt_init = np.log(np.expm1(0.01)).astype(np.float32)
        A_row = jnp.log(jnp.arange(1, D_STATE + 1, dtype=jnp.float32))
        return {'x': jax.random.normal(ks[0], (B_SZ, L, D_MODEL), jnp.float32), 'ln_w': jnp.ones((N_LAYERS, D_MODEL), jnp.float32), 'ln_b': jnp.zeros((N_LAYERS, D_MODEL), jnp.float32), 'in_proj_w': jax.random.normal(ks[1], (N_LAYERS, 2 * D_INNER, D_MODEL)) * s, 'conv_w': jax.random.normal(ks[2], (N_LAYERS, D_INNER, D_CONV)) * 0.2, 'conv_b': jnp.zeros((N_LAYERS, D_INNER), jnp.float32), 'x_proj_w': jax.random.normal(ks[3], (N_LAYERS, DT_RANK + 2 * D_STATE, D_INNER)) * s, 'dt_proj_w': jax.random.normal(ks[4], (N_LAYERS, D_INNER, DT_RANK)) * DT_RANK ** (-0.5), 'dt_proj_b': jnp.full((N_LAYERS, D_INNER), dt_init), 'A_log': jnp.broadcast_to(A_row, (N_LAYERS, D_INNER, D_STATE)).copy(), 'D_skip': jnp.ones((N_LAYERS, D_INNER), jnp.float32), 'out_proj_w': jax.random.normal(ks[5], (N_LAYERS, D_MODEL, D_INNER)) * s, 'norm_f_w': jnp.ones((D_MODEL,), jnp.float32), 'norm_f_b': jnp.zeros((D_MODEL,), jnp.float32)}
    _L0_attn_in = _L0_attn_setup()

    def _L0_ffn_setup():
        import jax, jax.numpy as jnp
        import numpy as np
        B, S, H, FFN, E = (2, 256, 128, 512, 8)
        key = jax.random.key(seed)
        k0, k1, k2, k3 = jax.random.split(key, 4)
        return {'hidden_states': jax.random.normal(k0, (B, S, H), dtype=jnp.float32), 'Wr': jax.random.normal(k1, (H, E), dtype=jnp.float32) * 0.02, 'br': jnp.zeros((E,), dtype=jnp.float32), 'W1': jax.random.normal(k2, (E, H, FFN), dtype=jnp.float32) * 0.02, 'W2': jax.random.normal(k3, (E, FFN, H), dtype=jnp.float32) * 0.02}
    _L0_ffn_in = _L0_ffn_setup()

    def _L1_attn_setup():
        import jax, jax.numpy as jnp
        import numpy as np
        NUM_HEADS = 16
        key = jax.random.key(seed)
        ks = jax.random.split(key, 5)
        B, N, C = (4, 256, 128)
        s = 0.02
        return {'x': jax.random.normal(ks[0], (B, N, C), jnp.float32), 'w_qkv': jax.random.normal(ks[1], (C, 3 * C), jnp.float32) * s, 'b_qkv': jnp.zeros((3 * C,), jnp.float32), 'w_proj': jax.random.normal(ks[2], (C, C), jnp.float32) * s, 'b_proj': jnp.zeros((C,), jnp.float32)}
    _L1_attn_in = _L1_attn_setup()

    def _L1_ffn_setup():
        import jax, jax.numpy as jnp
        import numpy as np
        ALPHA = 1.0
        key = jax.random.key(seed)
        ks = jax.random.split(key, 7)
        B, S, IN, OUT = (8, 1024, 128, 128)
        RANK, DDIM, UDIM = (4, 100, 50)
        return {'hidden_states': jax.random.normal(ks[0], (B, S, IN), dtype=jnp.float32), 'W': jax.random.normal(ks[1], (OUT, IN), dtype=jnp.float32) * 0.02, 'b': jax.random.normal(ks[2], (OUT,), dtype=jnp.float32) * 0.02, 'lora_down': jax.random.normal(ks[3], (RANK, DDIM), dtype=jnp.float32) * 0.1, 'lora_up': jax.random.normal(ks[4], (UDIM, RANK), dtype=jnp.float32) * 0.1, 'down_aux': jax.random.normal(ks[5], (DDIM, IN), dtype=jnp.float32) * 0.03, 'up_aux': jax.random.normal(ks[6], (OUT, UDIM), dtype=jnp.float32) * 0.03}
    _L1_ffn_in = _L1_ffn_setup()
    _d = {'L0_attn_x': _L0_attn_in['x'], 'L0_attn_ln_w': _L0_attn_in['ln_w'], 'L0_attn_ln_b': _L0_attn_in['ln_b'], 'L0_attn_in_proj_w': _L0_attn_in['in_proj_w'], 'L0_attn_conv_w': _L0_attn_in['conv_w'], 'L0_attn_conv_b': _L0_attn_in['conv_b'], 'L0_attn_x_proj_w': _L0_attn_in['x_proj_w'], 'L0_attn_dt_proj_w': _L0_attn_in['dt_proj_w'], 'L0_attn_dt_proj_b': _L0_attn_in['dt_proj_b'], 'L0_attn_A_log': _L0_attn_in['A_log'], 'L0_attn_D_skip': _L0_attn_in['D_skip'], 'L0_attn_out_proj_w': _L0_attn_in['out_proj_w'], 'L0_attn_norm_f_w': _L0_attn_in['norm_f_w'], 'L0_attn_norm_f_b': _L0_attn_in['norm_f_b'], 'L0_ffn_Wr': _L0_ffn_in['Wr'], 'L0_ffn_br': _L0_ffn_in['br'], 'L0_ffn_W1': _L0_ffn_in['W1'], 'L0_ffn_W2': _L0_ffn_in['W2'], 'L1_attn_w_qkv': _L1_attn_in['w_qkv'], 'L1_attn_b_qkv': _L1_attn_in['b_qkv'], 'L1_attn_w_proj': _L1_attn_in['w_proj'], 'L1_attn_b_proj': _L1_attn_in['b_proj'], 'L1_ffn_W': _L1_ffn_in['W'], 'L1_ffn_b': _L1_ffn_in['b'], 'L1_ffn_lora_down': _L1_ffn_in['lora_down'], 'L1_ffn_lora_up': _L1_ffn_in['lora_up'], 'L1_ffn_down_aux': _L1_ffn_in['down_aux'], 'L1_ffn_up_aux': _L1_ffn_in['up_aux']}
    _x0 = _d['L0_attn_x']
    _d['L0_attn_x'] = jax.random.normal(jax.random.fold_in(jax.random.key(seed), 1), (4, 1024, 128), dtype=_x0.dtype)
    del _x0
    return _d

def reference(L0_attn_x, L0_attn_ln_w, L0_attn_ln_b, L0_attn_in_proj_w, L0_attn_conv_w, L0_attn_conv_b, L0_attn_x_proj_w, L0_attn_dt_proj_w, L0_attn_dt_proj_b, L0_attn_A_log, L0_attn_D_skip, L0_attn_out_proj_w, L0_attn_norm_f_w, L0_attn_norm_f_b, L0_ffn_Wr, L0_ffn_br, L0_ffn_W1, L0_ffn_W2, L1_attn_w_qkv, L1_attn_b_qkv, L1_attn_w_proj, L1_attn_b_proj, L1_ffn_W, L1_ffn_b, L1_ffn_lora_down, L1_ffn_lora_up, L1_ffn_down_aux, L1_ffn_up_aux):

    def _L0_attn_ref(x, ln_w, ln_b, in_proj_w, conv_w, conv_b, x_proj_w, dt_proj_w, dt_proj_b, A_log, D_skip, out_proj_w, norm_f_w, norm_f_b):
        import jax, jax.numpy as jnp
        import numpy as np
        N_LAYERS = 2
        D_MODEL = 128
        D_INNER = 2 * D_MODEL
        D_STATE = 16
        D_CONV = 4
        DT_RANK = D_MODEL // 16
        B_SZ, L = (1, 256)
        EPS = 1e-05

        def layernorm(x, w, b):
            mu = jnp.mean(x, axis=-1, keepdims=True)
            var = jnp.mean(jnp.square(x - mu), axis=-1, keepdims=True)
            return (x - mu) * jax.lax.rsqrt(var + EPS) * w + b

        def mamba(x, in_w, cw, cb, xp_w, dtp_w, dtp_b, A_log, Dp, out_w):
            Bn, Ln, _ = x.shape
            xz = jnp.einsum('bld,ed->ble', x, in_w)
            xc, z = jnp.split(xz, 2, axis=-1)
            xp = jnp.pad(xc, ((0, 0), (D_CONV - 1, 0), (0, 0)))
            xc = sum((xp[:, k:k + Ln, :] * cw[:, k] for k in range(D_CONV))) + cb
            xc = jax.nn.silu(xc)
            dbl = jnp.einsum('ble,re->blr', xc, xp_w)
            dt, Bm, Cm = jnp.split(dbl, [DT_RANK, DT_RANK + D_STATE], axis=-1)
            dt = jax.nn.softplus(jnp.einsum('blr,er->ble', dt, dtp_w) + dtp_b)
            A = -jnp.exp(A_log)
            dA = jnp.exp(dt[..., None] * A)
            dBu = (dt * xc)[..., None] * Bm[:, :, None, :]

            def step(h, inp):
                dA_t, dBu_t, C_t = inp
                h = dA_t * h + dBu_t
                y = jnp.einsum('ben,bn->be', h, C_t)
                return (h, y)
            h0 = jnp.zeros((Bn, D_INNER, D_STATE), dA.dtype)
            _, ys = jax.lax.scan(step, h0, (dA.transpose(1, 0, 2, 3), dBu.transpose(1, 0, 2, 3), Cm.transpose(1, 0, 2)))
            y = ys.transpose(1, 0, 2) + xc * Dp
            y = y * jax.nn.silu(z)
            return jnp.einsum('ble,de->bld', y, out_w)
        for i in range(N_LAYERS):
            h = layernorm(x, ln_w[i], ln_b[i])
            h = mamba(h, in_proj_w[i], conv_w[i], conv_b[i], x_proj_w[i], dt_proj_w[i], dt_proj_b[i], A_log[i], D_skip[i], out_proj_w[i])
            x = h + x
        return layernorm(x, norm_f_w, norm_f_b)

    def _L0_ffn_ref(hidden_states, Wr, br, W1, W2):
        import jax, jax.numpy as jnp
        import numpy as np
        B, S, H, FFN, E = (2, 256, 128, 512, 8)
        b, s, h = hidden_states.shape
        x = hidden_states.reshape(-1, h)
        route = jax.nn.sigmoid(x @ Wr + br)
        max_prob = jnp.max(route, axis=1, keepdims=True)
        max_ind = jnp.argmax(route, axis=1)
        out = jnp.zeros_like(x)
        n_experts = Wr.shape[1]
        for e in range(n_experts):
            mask = (max_ind == e)[:, None].astype(x.dtype)
            y = jax.nn.gelu(x @ W1[e], approximate=False) @ W2[e]
            out = out + mask * y
        out = out * max_prob
        return out.reshape(b, s, h)

    def _L1_attn_ref(x, w_qkv, b_qkv, w_proj, b_proj):
        import jax, jax.numpy as jnp
        import numpy as np
        NUM_HEADS = 16
        B, N, C = x.shape
        H = NUM_HEADS
        D = C // H
        scale = D ** (-0.5)
        qkv = x @ w_qkv + b_qkv
        qkv = qkv.reshape(B, N, 3, H, D)
        q, k, v = (jnp.moveaxis(qkv, 2, 0)[i] for i in range(3))
        scores = jnp.einsum('bqhd,bkhd->bhqk', q.astype(jnp.float32), k.astype(jnp.float32)) * scale
        attn = jax.nn.softmax(scores, axis=-1).astype(q.dtype)
        out = jnp.einsum('bhqk,bkhd->bqhd', attn, v).reshape(B, N, C)
        return out @ w_proj + b_proj

    def _L1_ffn_ref(hidden_states, W, b, lora_down, lora_up, down_aux, up_aux):
        import jax, jax.numpy as jnp
        import numpy as np
        ALPHA = 1.0
        lilora_weight = up_aux @ (lora_up @ (lora_down @ down_aux))
        base = jnp.einsum('bsi,oi->bso', hidden_states, W) + b
        delta = jnp.einsum('bsi,oi->bso', hidden_states, lilora_weight)
        return base + ALPHA * delta
    x = L0_attn_x
    x = x + 0.5 * _L0_ffn_ref(_layernorm(x, axis=-1), L0_ffn_Wr, L0_ffn_br, L0_ffn_W1, L0_ffn_W2)
    x = x + _L0_attn_ref(_layernorm(x, axis=-1), L0_attn_ln_w, L0_attn_ln_b, L0_attn_in_proj_w, L0_attn_conv_w, L0_attn_conv_b, L0_attn_x_proj_w, L0_attn_dt_proj_w, L0_attn_dt_proj_b, L0_attn_A_log, L0_attn_D_skip, L0_attn_out_proj_w, L0_attn_norm_f_w, L0_attn_norm_f_b)
    x = x + 0.5 * _L0_ffn_ref(_layernorm(x, axis=-1), L0_ffn_Wr, L0_ffn_br, L0_ffn_W1, L0_ffn_W2)
    x = x + 0.5 * _L1_ffn_ref(_layernorm(x, axis=-1), L1_ffn_W, L1_ffn_b, L1_ffn_lora_down, L1_ffn_lora_up, L1_ffn_down_aux, L1_ffn_up_aux)
    x = x + _L1_attn_ref(_layernorm(x, axis=-1), L1_attn_w_qkv, L1_attn_b_qkv, L1_attn_w_proj, L1_attn_b_proj)
    x = x + 0.5 * _L1_ffn_ref(_layernorm(x, axis=-1), L1_ffn_W, L1_ffn_b, L1_ffn_lora_down, L1_ffn_lora_up, L1_ffn_down_aux, L1_ffn_up_aux)
    return x

_drawn_inputs = setup_inputs


def setup_inputs(seed=0):
    import zlib

    import numpy as np

    out = dict(_drawn_inputs(seed))
    spreads = {'L0_attn_ln_w': (1.0, 0.6),
     'L0_attn_ln_b': (0.0, 0.8),
     'L0_attn_conv_b': (0.0, 0.8),
     'L0_attn_dt_proj_b': (-4.600165843963623, 0.6),
     'L0_attn_D_skip': (1.0, 0.6),
     'L0_attn_norm_f_w': (1.0, 0.2),
     'L0_attn_norm_f_b': (0.0, 0.1),
     'L0_ffn_br': (0.0, 0.377),
     'L1_attn_b_qkv': (0.0, 0.689),
     'L1_attn_b_proj': (0.0, 0.8)}
    factors = {'L0_attn_in_proj_w': 8.0,
     'L0_attn_conv_w': 8.0,
     'L0_attn_x_proj_w': 8.0,
     'L0_attn_dt_proj_w': 8.0,
     'L0_attn_A_log': 8.0,
     'L0_attn_out_proj_w': 8.0,
     'L0_ffn_Wr': 2.804,
     'L1_attn_w_qkv': 8.0,
     'L1_attn_w_proj': 4.983,
     'L1_ffn_b': 47.776,
     'L1_ffn_lora_down': 8.0,
     'L1_ffn_lora_up': 8.0,
     'L1_ffn_down_aux': 7.502,
     'L1_ffn_up_aux': 8.0,
     'L1_ffn_W': 8.0}
    for name, (base, spread) in spreads.items():
        noise = np.random.default_rng([zlib.crc32(name.encode()), seed]).standard_normal(out[name].shape)
        drawn = base * np.exp(spread * noise) if base else spread * noise
        out[name] = jnp.asarray(drawn.astype(out[name].dtype))
    for name, factor in factors.items():
        out[name] = (out[name] * factor).astype(out[name].dtype)
    return out
```

```python
from contextlib import ExitStack, contextmanager

import numpy as np

import concourse.bass as bass
from concourse import mybir

ALU = mybir.AluOpType
ACT = mybir.ActivationFunctionType
AX = mybir.AxisListType
F32 = mybir.dt.float32
BF16 = mybir.dt.bfloat16
I32 = mybir.dt.int32
U32 = mybir.dt.uint32

P = 128
C = 128
EPS = 1e-5


class Tally:

    def __init__(self, eng, sem):
        self.eng, self.sem, self.n, self.base = eng, sem, 0, 0

    def count(self, inst):
        inst.then_inc(self.sem, 1)
        self.n += 1

    def wait(self):
        self.eng.wait_ge(self.sem, self.base + self.n)

    def step(self, inst):
        self.count(inst)
        self.wait()

    @contextmanager
    def loop(self, times, each):
        start, outer = self.n, self.base
        with self.eng.Fori(0, times) as i:
            self.base = outer + i * each
            yield i
        assert self.n - start == each, (self.n - start, each)
        self.n, self.base = start + each * times, outer


class Stage:

    def __init__(self, nc, stack, stage):
        self.nc, self.stack, self.stage, self.sems = nc, stack, stage, []
        stack.callback(self.release)

    def sb(self, name, shape, dt=F32):
        return self.stack.enter_context(self.nc.sbuf_tensor(f"{self.stage}_{name}", shape, dt))

    def ps(self, name, shape, dt=F32):
        return self.stack.enter_context(self.nc.psum_tensor(f"{self.stage}_{name}", shape, dt))

    def sem(self, name):
        self.sems.append(self.nc.alloc_semaphore(f"{self.stage}_{name}"))
        return self.sems[-1]

    def release(self):
        if self.sems:
            self.nc.clear_and_free_semaphores(self.sems)
            self.nc.all_engine_barrier()


def norm_buffers(mem, tiles):
    return {
        "bn": mem.sb("bn", [P, tiles, 6]),
        "mean": mem.sb("mean", [P, tiles]),
        "var": mem.sb("var", [P, tiles]),
        "rstd": mem.sb("rstd", [P, tiles]),
        "tmp": mem.sb("tmp", [P, 2, tiles]),
    }


def norm_factors(v, own, b, tiles, first=0):
    s = slice(first, first + tiles)
    bn, mean, var, y = b["bn"][:, s, :], b["mean"][:, s], b["var"][:, s], b["rstd"][:, s]
    t0, t1 = b["tmp"][:, 0, s], b["tmp"][:, 1, s]
    own.wait()
    own.count(v.tensor_tensor(t0, bn[:, :, 1], bn[:, :, 4], ALU.subtract))
    own.count(v.tensor_tensor(t1, bn[:, :, 2], bn[:, :, 5], ALU.add))
    own.step(v.tensor_tensor(mean, bn[:, :, 1], bn[:, :, 4], ALU.add))
    own.count(v.scalar_tensor_tensor(out=t0, in0=t0, scalar=0.25, in1=t0, op0=ALU.mult, op1=ALU.mult))
    own.count(v.tensor_scalar(t1, t1, 1.0 / C, EPS, ALU.mult, ALU.add))
    own.step(v.tensor_scalar(mean, mean, 0.5, None, ALU.mult))
    own.step(v.tensor_tensor(var, t0, t1, ALU.add))
    own.step(v.tensor_scalar(t0.bitcast(I32), var.bitcast(I32), 1, None, ALU.logical_shift_right))
    own.step(v.tensor_scalar(y.bitcast(I32), t0.bitcast(I32), -1, 0x5F3759DF, ALU.mult, ALU.add))
    for _ in range(3):
        own.step(v.tensor_tensor(t0, y, y, ALU.mult))
        own.step(v.scalar_tensor_tensor(out=t0, in0=t0, scalar=-0.5, in1=var, op0=ALU.mult, op1=ALU.mult))
        own.step(v.scalar_tensor_tensor(out=y, in0=t0, scalar=1.5, in1=y, op0=ALU.add, op1=ALU.mult))


NORM_STEPS = 7 + 2 + 9


def load_stage(nc, x_dram, x_tok, ident, tri, ones_bf):
    with ExitStack() as stack:
        mem = Stage(nc, stack, "load")
        x_loaded, cleared, made = mem.sem("x_loaded"), mem.sem("cleared"), mem.sem("made")
        block = stack.enter_context(nc.Block())

        @block.sync
        def _(sp):
            for q in range(4):
                sp.dma_start(x_tok[:, 8 * q:8 * q + 8, :], x_dram[:, 8 * q:8 * q + 8, :]).then_inc(x_loaded, 16)
            sp.wait_ge(x_loaded, 64)

        @block.gpsimd
        def _(pool):
            pool.memset(ident[:], 0.0).then_inc(cleared, 1)
            pool.memset(tri[:], 0.0).then_inc(cleared, 1)
            pool.memset(ones_bf[:], 1.0).then_inc(cleared, 1)
            pool.wait_ge(cleared, 3)
            pool.affine_select(out=ident[:], in_=ident[:], compare_op=ALU.not_equal, fill=1.0, base=0,
                               pattern=[[-1, P]], channel_multiplier=1).then_inc(made, 1)
            pool.affine_select(out=tri[:], in_=tri[:], compare_op=ALU.is_ge, fill=1.0, base=0,
                               pattern=[[-1, P]], channel_multiplier=1).then_inc(made, 1)
            pool.wait_ge(made, 2)


def store_stage(nc, x_tok, out_dram):
    with ExitStack() as stack:
        mem = Stage(nc, stack, "store")
        stored = mem.sem("stored")
        block = stack.enter_context(nc.Block())

        @block.sync
        def _(sp):
            for q in range(4):
                sp.dma_start(out_dram[:, 8 * q:8 * q + 8, :], x_tok[:, 8 * q:8 * q + 8, :]).then_inc(stored, 16)
            sp.wait_ge(stored, 64)


def moe_stage(nc, stage, x_tok, ident, tri, ones_bf, Wr, br, W1, W2, sorted_x, sorted_y, clear_sorted):
    TILES = x_tok.shape[1]
    E = Wr.shape[1]
    F = W1.shape[2]
    FB = F // P
    SLOTS = TILES + E
    GROUPS = TILES // 4
    x_slots = sorted_x.rearrange("(n p) c -> p n c", p=P)
    y_slots = sorted_y.rearrange("(n p) c -> p n c", p=P)
    with ExitStack() as stack:
        mem = Stage(nc, stack, stage)
        w1 = mem.sb("w1", [P, E, F])
        w2 = mem.sb("w2", [P, E, FB, C])
        wr = mem.sb("wr", [P, E])
        br_row = mem.sb("br_row", [P, E])
        nb = norm_buffers(mem, TILES)
        xn = mem.sb("xn", [P, TILES, C])
        xn_ring = mem.sb("xn_ring", [P, 2, 4, C])
        xnT = mem.sb("xnT", [P, 2, 4 * P])
        prob = mem.sb("prob", [P, TILES, E])
        pick = mem.sb("pick", [P, TILES, E])
        work = mem.sb("work", [P, TILES, E])
        best = mem.sb("best", [P, TILES])
        pos = mem.sb("pos", [P, TILES])
        pos_i = mem.sb("pos_i", [P, TILES], U32)
        mask_bf = mem.sb("mask_bf", [P, TILES, E], BF16)
        prefer = mem.sb("prefer", [P, E])
        ones = mem.sb("ones", [P, TILES])
        upto = mem.sb("upto", [P, TILES, E])
        total = mem.sb("total", [P, 4, E])
        total_i = mem.sb("total_i", [P, E], I32)
        slot_no = mem.sb("slot_no", [P, SLOTS, E])
        slot_e = mem.sb("slot_e", [P, SLOTS])
        slot_i = mem.sb("slot_i", [P, SLOTS], I32)
        zero = mem.sb("zero", [P, 4 * C])
        xs = mem.sb("xs", [P, 2, C])
        xsT = mem.sb("xsT", [P, 2, P])
        hs = mem.sb("hs", [P, 2, F])
        hT = mem.sb("hT", [P, 2, FB, P])
        ys = mem.sb("ys", [P, 2, C])
        yg = xn
        s_w, s_wr, s_zero, s_const, s_stored0 = (mem.sem(n) for n in
                                                 ("w_loaded", "wr_loaded", "zeroed", "const", "cleared"))
        s_norm, s_ring, s_T, s_Tc, s_logit = (mem.sem(n) for n in
                                              ("norm", "ring", "xnT", "xnT_copied", "logits"))
        s_v, s_z, s_exp, s_mask, s_pre, s_pos, s_slots = (mem.sem(n) for n in
                                                          ("own", "z", "exp", "mask", "prefix", "pos", "slots"))
        s_scat = mem.sem("scattered")
        s_xs = [mem.sem(f"xs{k}_loaded") for k in range(2)]
        s_out = [mem.sem(f"ys{k}_stored") for k in range(2)]
        s_xsT, s_xsTc, s_up, s_gelu, s_hT, s_hTc, s_down, s_ys, s_gath = (mem.sem(n) for n in (
            "xsT", "xsT_copied", "up", "gelu", "hT", "hT_copied", "down", "ys", "gathered"))

        with ExitStack() as route_stack:
            pmem = Stage(nc, route_stack, stage + "r")
            xnT_ps = pmem.ps("xnT_ps", [P, 2, 4 * P])
            logit_ps = pmem.ps("logit_ps", [P, TILES, E])
            pre_ps = pmem.ps("pre_ps", [P, 2, 512])
            block = route_stack.enter_context(nc.Block())

            @block.sync
            def _(sp):
                sp.dma_start(wr[:], Wr).then_inc(s_wr, 16)
                sp.dma_start(br_row[:], br.rearrange("(a e) -> a e", a=1).broadcast_to([P, E])).then_inc(s_wr, 16)
                for e in range(0, E, 2):
                    sp.dma_start(w1[:, e:e + 2, :], W1[e:e + 2].rearrange("e c f -> c e f")).then_inc(s_w, 16)
                    sp.dma_start(w2[:, e:e + 2, :, :],
                                 W2[e:e + 2].rearrange("e (k f) c -> f e k c", f=P)).then_inc(s_w, 16)
                if clear_sorted:
                    sp.wait_ge(s_zero, 1)
                    for n in range(SLOTS // 4):
                        sp.dma_start(x_slots[:, 4 * n:4 * n + 4, :],
                                     zero[:].rearrange("p (n c) -> p n c", c=C)).then_inc(s_stored0, 16)
                    sp.wait_ge(s_stored0, 16 * (SLOTS // 4))
                sp.wait_ge(s_w, 16 * E)

            @block.gpsimd
            def _(pool):
                pool.memset(zero[:], 0.0).then_inc(s_zero, 1)
                pool.iota(prefer[:], pattern=[[-1, E]], base=E, channel_multiplier=0,
                          allow_small_or_imprecise_dtypes=True).then_inc(s_const, 1)
                pool.iota(slot_no[:], pattern=[[1, SLOTS], [0, E]], base=0, channel_multiplier=0,
                          allow_small_or_imprecise_dtypes=True).then_inc(s_const, 1)
                pool.memset(ones[:], 1.0).then_inc(s_const, 1)
                if clear_sorted:
                    pool.wait_ge(s_stored0, 16 * (SLOTS // 4))
                pool.wait_ge(s_pos, 1)
                for t in range(TILES):
                    pool.indirect_dma_start(sorted_x, bass.IndirectOffsetOnAxis(pos_i[:, t:t + 1], 0), xn[:, t, :],
                                            None).then_inc(s_scat, 16)
                pool.wait_ge(s_scat, 16 * TILES)

            @block.vector
            def _(v):
                own = Tally(v, s_v)
                with own.loop(TILES, 1) as t:
                    own.count(v.bn_stats(nb["bn"][:, bass.ds(t, 1), :], x_tok[:, bass.ds(t, 1), :]))
                norm_factors(v, own, nb, TILES)
                for g in range(GROUPS):
                    for t in range(4 * g, 4 * g + 4):
                        v.tensor_scalar(xn[:, t, :], x_tok[:, t, :], nb["mean"][:, t:t + 1],
                                        nb["rstd"][:, t:t + 1], ALU.subtract, ALU.mult).then_inc(s_norm, 1)
                    if g >= 1:
                        v.wait_ge(s_T, g)
                        if g >= 3:
                            v.wait_ge(s_logit, g - 2)
                        v.tensor_copy(xnT[:, (g - 1) % 2, :], xnT_ps[:, (g - 1) % 2, :]).then_inc(s_Tc, 1)
                v.wait_ge(s_T, GROUPS)
                v.wait_ge(s_logit, GROUPS - 2)
                v.tensor_copy(xnT[:, (GROUPS - 1) % 2, :], xnT_ps[:, (GROUPS - 1) % 2, :]).then_inc(s_Tc, 1)

                v.wait_ge(s_wr, 32)
                v.wait_ge(s_const, 3)
                v.wait_ge(s_logit, GROUPS)

                def over_tiles(row):
                    return row.rearrange("p (a e) -> p a e", a=1).broadcast_to([P, TILES, E])

                def over_experts(col, n=TILES):
                    return col.rearrange("p (t a) -> p t a", a=1).broadcast_to([P, n, E])

                v.tensor_tensor(work[:], logit_ps[:], over_tiles(br_row[:]), ALU.add).then_inc(s_z, 1)
                v.wait_ge(s_exp, 1)
                own.step(v.tensor_scalar(work[:], prob[:], 1.0, None, ALU.add))
                own.step(v.reciprocal(prob[:], work[:]))
                own.step(v.tensor_reduce(best[:], prob[:], AX.X, ALU.max))
                own.step(v.tensor_tensor(pick[:], prob[:], over_experts(best[:]), ALU.is_equal))
                own.step(v.tensor_tensor(work[:], pick[:], over_tiles(prefer[:]), ALU.mult))
                own.step(v.tensor_reduce(pos[:], work[:], AX.X, ALU.max))
                own.step(v.tensor_tensor(pick[:], work[:], over_experts(pos[:]), ALU.is_equal))
                v.tensor_copy(mask_bf[:], pick[:]).then_inc(s_mask, 1)
                own.step(v.tensor_scalar(best[:], best[:], 0.5, None, ALU.mult))
                v.wait_ge(s_pre, 1)
                count = pre_ps[:, 1, 0:TILES * E].rearrange("p (t e) -> p t e", e=E)
                before = pre_ps[:, 0, 0:TILES * E].rearrange("p (t e) -> p t e", e=E)
                own.step(v.tensor_copy(work[:], count))
                for e in range(E):
                    own.count(v.tensor_tensor_scan(upto[:, :, e], ones[:], work[:, :, e], 0.0, ALU.mult, ALU.add))
                own.wait()
                tot, tiles_of, end, start = (total[:, k, :] for k in range(4))
                own.step(v.tensor_scalar(tot, upto[:, TILES - 1, :], float(P - 1), None, ALU.add))
                own.step(v.tensor_copy(total_i[:], tot))
                own.step(v.tensor_scalar(total_i[:], total_i[:], 7, None, ALU.logical_shift_right))
                own.step(v.tensor_copy(tiles_of, total_i[:]))
                own.step(v.tensor_tensor_scan(end, ones[:, 0:E], tiles_of, 0.0, ALU.mult, ALU.add))
                own.step(v.tensor_tensor(start, end, tiles_of, ALU.subtract))
                own.step(v.tensor_scalar(start, start, float(P), None, ALU.mult))
                own.step(v.tensor_tensor(upto[:], upto[:], work[:], ALU.subtract))
                own.step(v.tensor_tensor(upto[:], upto[:], before, ALU.add))
                own.step(v.tensor_tensor(upto[:], upto[:], over_tiles(start), ALU.add))
                own.step(v.tensor_tensor(upto[:], upto[:], pick[:], ALU.mult))
                own.step(v.tensor_reduce(pos[:], upto[:], AX.X, ALU.add))
                v.tensor_copy(pos_i[:], pos[:]).then_inc(s_pos, 1)
                own.step(v.tensor_tensor(slot_no[:], slot_no[:],
                                         end.rearrange("p (a e) -> p a e", a=1).broadcast_to([P, SLOTS, E]),
                                         ALU.is_ge))
                own.step(v.tensor_reduce(slot_e[:], slot_no[:], AX.X, ALU.add))
                own.step(v.tensor_scalar(slot_e[:], slot_e[:], float(E - 1), None, ALU.min))
                own.step(v.tensor_copy(slot_i[:], slot_e[:]))

            @block.scalar
            def _(act):
                for g in range(GROUPS):
                    act.wait_ge(s_norm, 4 * g + 4)
                    if g >= 2:
                        act.wait_ge(s_T, g - 1)
                    act.activation(xn_ring[:, g % 2], xn[:, 4 * g:4 * g + 4, :], ACT.Copy).then_inc(s_ring, 1)
                act.wait_ge(s_z, 1)
                act.activation(prob[:], work[:], ACT.Exp, scale=-1.0).then_inc(s_exp, 1)

            @block.tensor
            def _(pe):
                def logits(g):
                    pe.wait_ge(s_Tc, g + 1)
                    for k in range(4):
                        last = pe.matmul(logit_ps[:, 4 * g + k, :], xnT[:, g % 2, P * k:P * k + P], wr[:],
                                         start=True, stop=True)
                    last.then_inc(s_logit, 1)

                pe.wait_ge(s_wr, 32)
                for g in range(GROUPS):
                    pe.wait_ge(s_ring, g + 1)
                    if g >= 2:
                        pe.wait_ge(s_Tc, g - 1)
                    for k in range(4):
                        last = pe.transpose(xnT_ps[:, g % 2, P * k:P * k + P], xn_ring[:, g % 2, k, :], ident[:])
                    last.then_inc(s_T, 1)
                    if g >= 1:
                        logits(g - 1)
                logits(GROUPS - 1)
                pe.wait_ge(s_mask, 1)
                m = mask_bf[:].rearrange("p t e -> p (t e)")
                pe.matmul(pre_ps[:, 0, 0:TILES * E], tri[:], m, start=True, stop=True)
                pe.matmul(pre_ps[:, 1, 0:TILES * E], ones_bf[:], m, start=True, stop=True).then_inc(s_pre, 1)

        with ExitStack() as expert_stack:
            pmem = Stage(nc, expert_stack, stage + "e")
            xsT_ps = pmem.ps("xsT_ps", [P, 512])
            up_ps = pmem.ps("up_ps", [P, 2, F])
            hT_ps = pmem.ps("hT_ps", [P, 2, FB, P])
            y_ps = pmem.ps("y_ps", [P, 2, 512])
            block = expert_stack.enter_context(nc.Block())
            PAIRS = (SLOTS - 2) // 2

            @block.sync
            def _(sp):
                def load(j, k, n, again):
                    if again:
                        sp.wait_ge(s_xsT, j - 1)
                    sp.dma_start(xs[:, k, :], x_slots[:, bass.ds(j, 1), :]).then_inc(s_xs[k], 16)

                load(0, 0, 0, False)
                load(1, 1, 0, False)
                with sp.Fori(0, PAIRS) as i:
                    for k in range(2):
                        load(2 * i + k + 2, k, i + 1, True)

            @block.scalar
            def _(act):
                def gelu(j, k):
                    act.wait_ge(s_up, j + 1)
                    act.activation(hs[:, k, :], up_ps[:, k, :], ACT.Gelu).then_inc(s_gelu, 1)

                def store(j, k):
                    act.wait_ge(s_ys, j + 1)
                    act.dma_start(y_slots[:, bass.ds(j, 1), :], ys[:, k, :]).then_inc(s_out[k], 16)

                gelu(0, 0)
                gelu(1, 1)
                with act.Fori(0, PAIRS) as i:
                    for k in range(2):
                        gelu(2 * i + k + 2, k)
                        store(2 * i + k, k)
                store(SLOTS - 2, 0)
                store(SLOTS - 1, 1)
                for k in range(2):
                    act.wait_ge(s_out[k], 16 * (SLOTS // 2))

            @block.tensor
            def _(pe):
                def turn_x(k, n):
                    pe.wait_ge(s_xs[k], 16 * (n + 1))
                    pe.transpose(xsT_ps[:, 0:P], xs[:, k, :], ident[:]).then_inc(s_xsT, 1)

                def up(j, k, e):
                    pe.wait_ge(s_xsTc, j + 1)
                    pe.matmul(up_ps[:, k, :], xsT[:, k, :], w1[:, bass.ds(e, 1), :], start=True,
                              stop=True).then_inc(s_up, 1)

                def turn_h(j, k):
                    pe.wait_ge(s_gelu, j + 1)
                    for q in range(FB):
                        last = pe.transpose(hT_ps[:, k, q, :], hs[:, k, P * q:P * q + P], ident[:])
                    last.then_inc(s_hT, 1)

                def down(j, k, e):
                    pe.wait_ge(s_hTc, j + 1)
                    for q in range(FB):
                        last = pe.matmul(y_ps[:, k, 0:C], hT[:, k, q, :], w2[:, bass.ds(e, 1), q, :],
                                         start=(q == 0), stop=(q == FB - 1))
                    last.then_inc(s_down, 1)

                def expert(j):
                    return pe.value_load(slot_i[0:1, bass.ds(j, 1)], min_val=0, max_val=E - 1)

                turn_x(0, 0)
                up(0, 0, expert(0))
                turn_x(1, 0)
                with pe.Fori(0, PAIRS) as i:
                    for k in range(2):
                        j = 2 * i + k + 1
                        turn_h(j - 1, k)
                        up(j, 1 - k, expert(j))
                        turn_x(k, i + 1)
                        down(j - 1, k, expert(j - 1))
                j = SLOTS - 1
                turn_h(j - 1, 0)
                up(j, 1, expert(j))
                down(j - 1, 0, expert(j - 1))
                turn_h(j, 1)
                down(j, 1, expert(j))

            @block.vector
            def _(v):
                def copy_x(j, k):
                    v.wait_ge(s_xsT, j + 1)
                    v.tensor_copy(xsT[:, k, :], xsT_ps[:, 0:P]).then_inc(s_xsTc, 1)

                def copy_h(j, k):
                    v.wait_ge(s_hT, j + 1)
                    v.tensor_copy(hT[:, k], hT_ps[:, k]).then_inc(s_hTc, 1)

                def copy_y(j, k, stored):
                    v.wait_ge(s_down, j + 1)
                    if stored is not None:
                        v.wait_ge(s_out[k], 16 * stored)
                    v.tensor_copy(ys[:, k, :], y_ps[:, k, 0:C]).then_inc(s_ys, 1)

                copy_x(0, 0)
                copy_x(1, 1)
                for k in range(2):
                    copy_h(k, k)
                    copy_x(k + 2, k)
                    copy_y(k, k, None)
                with v.Fori(0, PAIRS - 2) as i:
                    for k in range(2):
                        j = 2 * i + k + 2
                        copy_h(j, k)
                        copy_x(j + 2, k)
                        copy_y(j, k, i + 1)
                for j in range(SLOTS - 4, SLOTS):
                    copy_h(j, j % 2)
                    if j + 2 < SLOTS:
                        copy_x(j + 2, j % 2)
                    copy_y(j, j % 2, j // 2)
                v.wait_ge(s_gath, 16 * TILES)
                for t in range(TILES):
                    v.scalar_tensor_tensor(out=x_tok[:, t, :], in0=yg[:, t, :], scalar=best[:, t:t + 1],
                                           in1=x_tok[:, t, :], op0=ALU.mult, op1=ALU.add)

            @block.gpsimd
            def _(pool):
                for k in range(2):
                    pool.wait_ge(s_out[k], 16 * (SLOTS // 2))
                for t in range(TILES):
                    pool.indirect_dma_start(yg[:, t, :], None, sorted_y,
                                            bass.IndirectOffsetOnAxis(pos_i[:, t:t + 1], 0)).then_inc(s_gath, 16)


_NODES = (np.cos((2 * np.arange(5) + 1) * np.pi / 10) + 1) / 16
LOG1P = [float(c) for c in np.polyfit(_NODES, np.log1p(_NODES) / _NODES, 4)]


def mamba_stage(nc, x_tok, ident, ln_w, ln_b, in_w, conv_w, conv_b, xp_w, dtp_w, dtp_b, A_log, D_skip, out_w,
                nf_w, nf_b):
    LAYERS, DI, N = A_log.shape
    TAPS = conv_w.shape[2]
    R = dtp_w.shape[2]
    HALVES = DI // P
    TILES = x_tok.shape[1]
    BT = 8
    L = BT * P
    BATCHES = TILES // BT
    CH = L // 512
    BC = 2 * N
    ROWS = 3 * BC + R
    with ExitStack() as stack:
        mem = Stage(nc, stack, "mamba")
        r_tok = mem.sb("r_tok", [P, TILES, C])
        nb = norm_buffers(mem, TILES)
        w_in = mem.sb("w_in", [P, 2 * HALVES, C])
        w_tap = mem.sb("w_tap", [P, 2, C])
        wT = mem.sb("wT", [P, HALVES * TAPS + HALVES, P])
        cw = mem.sb("cw", [P, HALVES, TAPS])
        cb = mem.sb("cb", [P, HALVES])
        dtb = mem.sb("dtb", [P, HALVES])
        dsk = mem.sb("dsk", [P, HALVES])
        diag = mem.sb("diag", [P, HALVES, P])
        xp_in = mem.sb("xp_in", [ROWS, DI])
        xpT = mem.sb("xpT", [P, HALVES, ROWS])
        dtp_in = mem.sb("dtp_in", [P, HALVES, ROWS])
        dtpT = mem.sb("dtpT", [ROWS, DI])
        ow_in = mem.sb("ow_in", [P, DI])
        owT = mem.sb("owT", [P, HALVES, C])
        alog = mem.sb("alog", [P, HALVES, N])
        aneg = mem.sb("aneg", [P, HALVES, N])
        lnw = mem.sb("lnw", [P, 2])
        nfw = mem.sb("nfw", [P, 2, C])
        sel = mem.sb("sel", [3 * BC, BC, P], BF16)
        hn = mem.sb("hn", [P, BT, C])
        hT = mem.sb("hT", [P, TAPS - 1 + L])
        xc = mem.sb("xc", [P, HALVES, L])
        zs = mem.sb("zs", [P, HALVES, L])
        dt = mem.sb("dt", [P, HALVES, L])
        u = mem.sb("u", [P, HALVES, L])
        dt8 = mem.sb("dt8", [ROWS, L])
        parts = mem.sb("parts", [3 * BC, L], BF16)
        mid = mem.sb("mid", [3 * BC, L], BF16)
        rest = mem.sb("rest", [3 * BC, L])
        dA = mem.sb("dA", [P, 2, HALVES, L])
        dBu = mem.sb("dBu", [P, 2, HALVES, L])
        Bs = mem.sb("Bs", [P, 2, L])
        hs = mem.sb("hs", [P, HALVES, L])
        hC = mem.sb("hC", [P, 2, HALVES, L])
        e_sp, ln_sp = dA[:, 0], dA[:, 1]
        t_sp = hs
        yz = dBu[:, 0]

        psB = mem.ps("psB", [P, CH, 512])
        psC = mem.ps("psC", [P, CH, 512])
        psY = mem.ps("psY", [P, HALVES, CH, 512])
        flatB = psB[:].rearrange("p a b -> p (a b)")
        flatC = psC[:].rearrange("p a b -> p (a b)")

        names = ("own scan w_copied pool_own w_loaded w_cleared sel_made layer_free w_scaled w_turned w_ready a_exp hn hT hT_copied "
                 "xc_mm z_mm xc_silu z_silu dbl_mm parts dt8 dt_mm softplus u skip_mm B_mm B_copied C_mm "
                 "dA dBu hC y_mm yz out_mm nf_loaded zero_pad").split()
        s = {n: mem.sem(n) for n in names}
        PREP = HALVES * TAPS
        TURNS = PREP + 4 * HALVES
        RING = 2 * HALVES
        block = stack.enter_context(nc.Block())

        @block.sync
        def _(sp):
            for k, w in enumerate((nf_w, nf_b)):
                sp.dma_start(nfw[:, k, :], w.rearrange("(a c) -> a c", a=1).broadcast_to([P, C])).then_inc(s["nf_loaded"], 16)
            sp.wait_ge(s["w_cleared"], 1)
            with sp.Fori(0, LAYERS) as l:
                sp.wait_ge(s["layer_free"], l + 1)
                one = bass.ds(l, 1)
                loads = [
                    (w_in[:], in_w[one].rearrange("a (k p) c -> p (a k) c", p=P)),
                    (cw[:], conv_w[one].rearrange("a (h p) t -> p (a h) t", p=P)),
                    (cb[:], conv_b[one].rearrange("a (h p) -> p (a h)", p=P)),
                    (dtb[:], dtp_b[one].rearrange("a (h p) -> p (a h)", p=P)),
                    (dsk[:], D_skip[one].rearrange("a (h p) -> p (a h)", p=P)),
                    (alog[:], A_log[one].rearrange("a (h p) n -> p (a h) n", p=P)),
                    (lnw[:, 0:1], ln_w[one].rearrange("a c -> c a")),
                    (lnw[:, 1:2], ln_b[one].rearrange("a c -> c a")),
                    (ow_in[:], out_w[one].rearrange("a d e -> d (a e)")),
                    (dtp_in[:, :, 3 * BC:ROWS], dtp_w[one].rearrange("a (h p) r -> p (a h) r", p=P)),
                    (xp_in[3 * BC:ROWS, :], xp_w[one, 0:R].rearrange("a r e -> r (a e)")),
                ] + [(xp_in[BC * k:BC * k + BC, :], xp_w[one, R:R + BC].rearrange("a r e -> r (a e)")) for k in range(3)]
                for dst, src in loads:
                    with nc.allow_non_contiguous_dma(reason="a few hundred values per channel"):
                        sp.dma_start(dst, src).then_inc(s["w_loaded"], 16)
            assert len(loads) == 14

        LOADS = 14

        @block.gpsimd
        def _(pool):
            own = Tally(pool, s["pool_own"])
            pool.memset(dtp_in[:], 0.0).then_inc(s["w_cleared"], 1)
            pool.memset(hT[:, 0:TAPS - 1], 0.0).then_inc(s["zero_pad"], 1)
            own.step(pool.memset(sel[:], 0.0))
            for q in range(3):
                own.step(pool.affine_select(out=sel[:], in_=sel[:], compare_op=ALU.not_equal, fill=1.0,
                                            base=-BC * q, pattern=[[-1, BC], [0, P]], channel_multiplier=1))
            pool.sem_inc(s["sel_made"], 1)
            pool.sem_inc(s["dBu"], RING)
            with pool.Fori(0, LAYERS * BATCHES) as g:
                with pool.Fori(0, N // 2) as i:
                    for k in range(2):
                        pool.wait_ge(s["u"], g + 1)
                        m = g * N + i * 2 + k
                        pool.wait_ge(s["B_copied"], m + 2)
                        for h in range(HALVES):
                            pool.wait_ge(s["scan"], HALVES * m + h + 1)
                            pool.tensor_tensor(dBu[:, k, h, :], u[:, h, :], Bs[:, k, :],
                                               ALU.mult).then_inc(s["dBu"], 1)

        @block.scalar
        def _(act):
            act.sem_inc(s["B_copied"], 1)
            with act.Fori(0, LAYERS) as l:
                act.wait_ge(s["w_loaded"], 16 * LOADS * (l + 1))
                act.activation(aneg[:].rearrange("p h n -> p (h n)"), alog[:].rearrange("p h n -> p (h n)"),
                               ACT.Exp).then_inc(s["a_exp"], 1)
                act.wait_ge(s["w_ready"], l + 1)
                with act.Fori(0, BATCHES) as b:
                    g = l * BATCHES + b
                    act.wait_ge(s["xc_mm"], g + 1)
                    for h in range(HALVES):
                        last = act.activation(xc[:, h, :], psY[:, h].rearrange("p a b -> p (a b)"), ACT.Silu,
                                              bias=cb[:, h:h + 1])
                    last.then_inc(s["xc_silu"], 1)
                    act.wait_ge(s["z_mm"], g + 1)
                    act.activation(zs[:, 0, :], flatC, ACT.Silu)
                    act.activation(zs[:, 1, :], flatB, ACT.Silu).then_inc(s["z_silu"], 1)
                    act.wait_ge(s["dt_mm"], g + 1)
                    for h, ps in ((0, flatC), (1, flatB)):
                        act.activation(dt[:, h, :], ps, ACT.Relu, bias=dtb[:, h:h + 1])
                        act.activation(e_sp[:, h, :], ps, ACT.Abs, bias=dtb[:, h:h + 1]).then_inc(s["softplus"], 1)
                    act.wait_ge(s["softplus"], 4 * g + 2)
                    act.activation(e_sp, e_sp, ACT.Exp, scale=-1.0).then_inc(s["softplus"], 1)
                    act.wait_ge(s["softplus"], 4 * g + 3)
                    act.activation(ln_sp, e_sp, ACT.Ln, bias=1.0).then_inc(s["softplus"], 1)
                    act.wait_ge(s["u"], g + 1)
                    with act.Fori(0, N // 2) as i:
                        for k in range(2):
                            m = g * N + i * 2 + k
                            act.wait_ge(s["dBu"], HALVES * m + HALVES)
                            act.wait_ge(s["B_mm"], m + 1)
                            act.activation(Bs[:, k, :], flatB, ACT.Copy).then_inc(s["B_copied"], 1)
                            for h in range(HALVES):
                                act.wait_ge(s["scan"], HALVES * m + h + 1)
                                act.activation(dA[:, k, h, :], dt[:, h, :], ACT.Exp,
                                               scale=aneg[:, h, bass.ds(i * 2 + k, 1)]).then_inc(s["dA"], 1)

        @block.tensor
        def _(pe):
            pe.sem_inc(s["y_mm"], 2)
            pe.wait_ge(s["sel_made"], 1)
            pe.wait_ge(s["zero_pad"], 1)
            with pe.Fori(0, LAYERS) as l:
                pe.wait_ge(s["w_loaded"], 16 * LOADS * (l + 1))
                turns = 0

                def turn(in_, rows):
                    nonlocal turns
                    out = psY[:, (turns % 4) // 2, turns % 2, 0:P]
                    if turns >= 4:
                        pe.wait_ge(s["w_copied"], l * TURNS + turns - 3)
                    pe.transpose(out[0:rows, 0:in_.shape[0]], in_, ident[0:in_.shape[0], 0:in_.shape[0]]).then_inc(s["w_turned"], 1)
                    turns += 1
                for q in range(PREP):
                    pe.wait_ge(s["w_scaled"], l * PREP + q + 1)
                    turn(w_tap[:, q % 2, :], P)
                for h in range(HALVES):
                    turn(w_in[:, HALVES + h, :], P)
                for h in range(HALVES):
                    turn(xp_in[:, P * h:P * h + P], P)
                for h in range(HALVES):
                    turn(dtp_in[:, h, :], ROWS)
                for h in range(HALVES):
                    turn(ow_in[:, P * h:P * h + P], P)
                assert turns == TURNS
                with pe.Fori(0, BATCHES) as b:
                    g = l * BATCHES + b
                    pe.wait_ge(s["w_ready"], l + 1)
                    pe.wait_ge(s["hn"], g + 1)
                    for t in range(BT):
                        last = pe.transpose(psB[:, t // 4, P * (t % 4):P * (t % 4) + P], hn[:, t, :], ident[:])
                    last.then_inc(s["hT"], 1)
                    pe.wait_ge(s["hT_copied"], g + 1)
                    for h in range(HALVES):
                        for c in range(CH):
                            for k in range(TAPS):
                                last = pe.matmul(psY[:, h, c, :], wT[:, h * TAPS + k, :],
                                                 hT[:, 512 * c + k:512 * c + k + 512], start=(k == 0), stop=(k == TAPS - 1))
                    last.then_inc(s["xc_mm"], 1)
                    for h, ps in ((0, psC), (1, psB)):
                        for c in range(CH):
                            last = pe.matmul(ps[:, c, :], wT[:, PREP + h, :],
                                             hT[:, TAPS - 1 + 512 * c:TAPS - 1 + 512 * c + 512], start=True, stop=True)
                    last.then_inc(s["z_mm"], 1)
                    pe.wait_ge(s["xc_silu"], g + 1)
                    for c in range(CH):
                        for h in range(HALVES):
                            last = pe.matmul(psY[0:ROWS, 0, c, :], xpT[:, h, :], xc[:, h, 512 * c:512 * c + 512],
                                             start=(h == 0), stop=(h == HALVES - 1))
                    last.then_inc(s["dbl_mm"], 1)
                    pe.wait_ge(s["dt8"], g + 1)
                    pe.wait_ge(s["z_silu"], g + 1)
                    for h, ps in ((0, psC), (1, psB)):
                        for c in range(CH):
                            last = pe.matmul(ps[:, c, :], dtpT[3 * BC:ROWS, P * h:P * h + P],
                                             dt8[3 * BC:ROWS, 512 * c:512 * c + 512], start=True, stop=True)
                    last.then_inc(s["dt_mm"], 1)
                    pe.wait_ge(s["parts"], g + 1)
                    for h in range(HALVES):
                        for c in range(CH):
                            pe.matmul(psY[:, h, c, :], diag[:, h, :], xc[:, h, 512 * c:512 * c + 512],
                                      start=True, stop=True)
                    pe.wait_ge(s["u"], g + 1)

                    def spread(ps, row, sem):
                        for c in range(CH):
                            last = pe.matmul(ps[:, c, :], sel[:, bass.ds(row, 1), :],
                                             parts[:, 512 * c:512 * c + 512], start=True, stop=True)
                        last.then_inc(sem, 1)

                    def spread_B(n):
                        pe.wait_ge(s["B_copied"], g * N + n + 1)
                        spread(psB, n, s["B_mm"])

                    def step(n, k, ahead):
                        pe.wait_ge(s["hC"], HALVES * (g * N + n) + HALVES)
                        spread(psC, n + N, s["C_mm"])
                        if ahead:
                            spread_B(n + 2)
                        for h in range(HALVES):
                            pe.wait_ge(s["hC"], HALVES * (g * N + n) + HALVES + h + 1)
                            for c in range(CH):
                                last = pe.matmul(psY[:, h, c, :], ident[:], hC[:, k, h, 512 * c:512 * c + 512],
                                                 start=False, stop=True, skip_group_check=True)
                        last.then_inc(s["y_mm"], 1)

                    spread_B(0)
                    spread_B(1)
                    with pe.Fori(0, N // 2 - 1) as i:
                        for k in range(2):
                            step(i * 2 + k, k, True)
                    for k in range(2):
                        step(N - 2 + k, k, False)
                    pe.wait_ge(s["yz"], g + 1)
                    for t in range(BT):
                        for h in range(HALVES):
                            last = pe.matmul(psB[:, t // 4, P * (t % 4):P * (t % 4) + P], yz[:, h, P * t:P * t + P],
                                             owT[:, h, :], start=(h == 0), stop=(h == HALVES - 1))
                    last.then_inc(s["out_mm"], 1)

        @block.vector
        def _(v):
            own = Tally(v, s["own"])
            with own.loop(TILES, 1) as t:
                own.count(v.bn_stats(nb["bn"][:, bass.ds(t, 1), :], x_tok[:, bass.ds(t, 1), :]))
            norm_factors(v, own, nb, TILES)
            for t in range(TILES):
                own.count(v.tensor_scalar(r_tok[:, t, :], x_tok[:, t, :], nb["mean"][:, t:t + 1],
                                          nb["rstd"][:, t:t + 1], ALU.subtract, ALU.mult))
            own.wait()
            v.sem_inc(s["layer_free"], 1)
            v.sem_inc(s["scan"], RING)
            v.sem_inc(s["hC"], HALVES)
            PER_BATCH = BT + NORM_STEPS + 14
            with own.loop(LAYERS, HALVES + 1 + BATCHES * PER_BATCH) as l:
                v.wait_ge(s["w_loaded"], 16 * LOADS * (l + 1))
                turned = [wT[:, q, :] for q in range(PREP + HALVES)] + [xpT[:, h, :] for h in range(HALVES)] + \
                    [dtpT[3 * BC:ROWS, P * h:P * h + P] for h in range(HALVES)] + [owT[:, h, :] for h in range(HALVES)]

                def copy_turn(q):
                    dst = turned[q]
                    lo, n = (3 * BC, R) if PREP + 2 * HALVES <= q < PREP + 3 * HALVES else (0, P)
                    v.wait_ge(s["w_turned"], l * TURNS + q + 1)
                    v.tensor_copy(dst, psY[lo:lo + n, (q % 4) // 2, q % 2, 0:dst.shape[-1]]).then_inc(s["w_copied"], 1)

                for q in range(PREP):
                    h, k = q // TAPS, q % TAPS
                    if q >= 2:
                        v.wait_ge(s["w_turned"], l * TURNS + q - 1)
                    inst = v.tensor_scalar(w_tap[:, q % 2, :], w_in[:, h, :], cw[:, h, k:k + 1], None, ALU.mult)
                    inst.then_inc(s["w_scaled"], 1)
                    if q >= 2:
                        copy_turn(q - 2)
                for q in range(PREP - 2, TURNS):
                    copy_turn(q)
                for h in range(HALVES):
                    own.count(v.tensor_scalar(diag[:, h, :], ident[:], dsk[:, h:h + 1], None, ALU.mult))
                v.wait_ge(s["a_exp"], l + 1)
                own.count(v.tensor_scalar(aneg[:].rearrange("p h n -> p (h n)"), aneg[:].rearrange("p h n -> p (h n)"),
                                          -1.0, None, ALU.mult))
                own.wait()
                v.wait_ge(s["w_copied"], TURNS * (l + 1))
                v.sem_inc(s["w_ready"], 1)
                with own.loop(BATCHES, PER_BATCH) as b:
                    g = l * BATCHES + b
                    for t in range(BT):
                        own.count(v.bn_stats(nb["bn"][:, t, :], r_tok[:, bass.ds(b * BT + t, 1), :]))
                    norm_factors(v, own, nb, BT)
                    for t in range(BT):
                        last = v.tensor_scalar(hn[:, t, :], r_tok[:, bass.ds(b * BT + t, 1), :], nb["mean"][:, t:t + 1],
                                               nb["rstd"][:, t:t + 1], ALU.subtract, ALU.mult)
                    last.then_inc(s["hn"], 1)
                    v.wait_ge(s["hT"], g + 1)
                    v.tensor_scalar(hT[:, TAPS - 1:], flatB, lnw[:, 0:1], lnw[:, 1:2], ALU.mult,
                                    ALU.add).then_inc(s["hT_copied"], 1)
                    v.wait_ge(s["dbl_mm"], g + 1)
                    dbl = psY[:, 0].rearrange("p a b -> p (a b)")
                    v.tensor_copy(dt8[3 * BC:ROWS, :], dbl[3 * BC:ROWS, :]).then_inc(s["dt8"], 1)
                    J = 3 * BC
                    own.step(v.tensor_copy(parts[:], dbl[0:J, :]))
                    own.step(v.tensor_tensor(rest[:], dbl[0:J, :], parts[:], ALU.subtract))
                    own.step(v.tensor_copy(mid[:], rest[:]))
                    own.step(v.tensor_tensor(rest[:], rest[:], mid[:], ALU.subtract))
                    v.tensor_copy(parts[BC:2 * BC, :], mid[BC:2 * BC, :])
                    v.tensor_copy(parts[2 * BC:J, :], rest[2 * BC:J, :]).then_inc(s["parts"], 1)
                    v.wait_ge(s["softplus"], 4 * g + 4)
                    own.step(v.tensor_scalar(t_sp[:], e_sp, LOG1P[0], LOG1P[1], ALU.mult, ALU.add))
                    own.step(v.tensor_tensor(t_sp[:], t_sp[:], e_sp, ALU.mult))
                    for c in LOG1P[2:]:
                        own.step(v.scalar_tensor_tensor(out=t_sp[:], in0=t_sp[:], scalar=c, in1=e_sp, op0=ALU.add,
                                                        op1=ALU.mult))
                    own.step(v.tensor_tensor(ln_sp, ln_sp, t_sp[:], ALU.subtract))
                    own.step(v.scalar_tensor_tensor(out=ln_sp, in0=e_sp, scalar=0.125, in1=ln_sp, op0=ALU.is_gt,
                                                    op1=ALU.mult))
                    own.step(v.tensor_tensor(t_sp[:], t_sp[:], ln_sp, ALU.add))
                    own.step(v.tensor_tensor(dt[:], dt[:], t_sp[:], ALU.add))
                    v.tensor_tensor(u[:], dt[:], xc[:], ALU.mult).then_inc(s["u"], 1)
                    with v.Fori(0, N // 2) as i:
                        for k in range(2):
                            m = g * N + i * 2 + k
                            for h in range(HALVES):
                                v.wait_ge(s["dA"], HALVES * m + h + 1)
                                v.wait_ge(s["dBu"], HALVES * m + h + 1 + RING)
                                v.wait_ge(s["hC"], HALVES * m + h + 1)
                                v.tensor_tensor_scan(hs[:, h, :], dA[:, k, h, :], dBu[:, k, h, :], 0.0,
                                                     ALU.mult, ALU.add).then_inc(s["scan"], 1)
                            v.wait_ge(s["C_mm"], m + 1)
                            v.wait_ge(s["y_mm"], m + 1)
                            for h in range(HALVES):
                                v.wait_ge(s["scan"], HALVES * m + h + 1 + RING)
                                v.tensor_tensor(hC[:, k, h, :], hs[:, h, :], flatC, ALU.mult).then_inc(s["hC"], 1)
                    v.wait_ge(s["y_mm"], (g + 1) * N + 2)
                    for h in range(HALVES):
                        last = v.tensor_tensor(yz[:, h, :], zs[:, h, :], psY[:, h].rearrange("p a b -> p (a b)"), ALU.mult)
                    last.then_inc(s["yz"], 1)
                    v.wait_ge(s["out_mm"], g + 1)
                    tok = r_tok[:, bass.ds(b * BT, BT), :]
                    own.step(v.tensor_tensor(tok, tok, flatB.rearrange("p (t c) -> p t c", c=C), ALU.add))
                v.sem_inc(s["layer_free"], 1)
            with own.loop(TILES, 1) as t:
                own.count(v.bn_stats(nb["bn"][:, bass.ds(t, 1), :], r_tok[:, bass.ds(t, 1), :]))
            norm_factors(v, own, nb, TILES)
            for t in range(TILES):
                own.count(v.tensor_scalar(r_tok[:, t, :], r_tok[:, t, :], nb["mean"][:, t:t + 1],
                                          nb["rstd"][:, t:t + 1], ALU.subtract, ALU.mult))
            own.wait()
            v.wait_ge(s["nf_loaded"], 32)
            rows = [nfw[:, k:k + 1, :].broadcast_to([P, TILES, C]) for k in range(2)]
            own.step(v.tensor_tensor(r_tok[:], r_tok[:], rows[0], ALU.mult))
            own.step(v.tensor_tensor(r_tok[:], r_tok[:], rows[1], ALU.add))
            own.step(v.tensor_tensor(x_tok[:], x_tok[:], r_tok[:], ALU.add))


def lora_weight_stage(nc, ident, wT, b_row, ones_row, W, b, lora_down, lora_up, down_aux, up_aux):
    RANK, DD = lora_down.shape
    UD = lora_up.shape[0]
    with ExitStack() as stack:
        mem = Stage(nc, stack, "lora")
        w_in = mem.sb("w_in", [P, C])
        ld = mem.sb("ld", [RANK, DD])
        lu = mem.sb("lu", [UD, RANK])
        da = mem.sb("da", [DD, C])
        ua = mem.sb("ua", [P, UD])
        ldT = mem.sb("ldT", [DD, RANK])
        luT = mem.sb("luT", [RANK, UD])
        uaT = mem.sb("uaT", [UD, P])
        m1 = mem.sb("m1", [RANK, C])
        m2 = mem.sb("m2", [UD, C])
        ps = mem.ps("ps", [P, 6, 512])
        loaded, ones_set, done, copied = (mem.sem(n) for n in ("loaded", "ones_set", "mm", "copied"))
        block = stack.enter_context(nc.Block())

        @block.sync
        def _(sp):
            for dst, src in ((w_in, W), (ld, lora_down), (lu, lora_up), (da, down_aux), (ua, up_aux),
                             (b_row, b.rearrange("(a c) -> a c", a=1))):
                sp.dma_start(dst[:], src).then_inc(loaded, 16)

        @block.gpsimd
        def _(pool):
            pool.memset(ones_row[:], 1.0).then_inc(ones_set, 1)
            pool.wait_ge(ones_set, 1)

        @block.tensor
        def _(pe):
            pe.wait_ge(loaded, 96)
            pe.transpose(ps[0:DD, 0, 0:RANK], ld[:], ident[0:RANK, 0:RANK]).then_inc(done, 1)
            pe.transpose(ps[0:RANK, 1, 0:UD], lu[:], ident[0:UD, 0:UD]).then_inc(done, 1)
            pe.transpose(ps[0:UD, 2, 0:P], ua[:], ident[:]).then_inc(done, 1)
            pe.wait_ge(copied, 1)
            pe.matmul(ps[0:RANK, 3, 0:C], ldT[:], da[:], start=True, stop=True).then_inc(done, 1)
            pe.wait_ge(copied, 4)
            pe.matmul(ps[0:UD, 4, 0:C], luT[:], m1[:], start=True, stop=True).then_inc(done, 1)
            pe.wait_ge(copied, 5)
            pe.matmul(ps[:, 5, 0:C], w_in[:], ident[:], start=True, stop=False)
            pe.matmul(ps[:, 5, 0:C], m2[:], uaT[:], start=False, stop=True).then_inc(done, 1)

        @block.vector
        def _(v):
            for n, (dst, src) in enumerate(((ldT, ps[0:DD, 0, 0:RANK]), (luT, ps[0:RANK, 1, 0:UD]),
                                            (uaT, ps[0:UD, 2, 0:P]), (m1, ps[0:RANK, 3, 0:C]),
                                            (m2, ps[0:UD, 4, 0:C]), (wT, ps[:, 5, 0:C]))):
                v.wait_ge(done, n + 1)
                v.tensor_copy(dst[:], src).then_inc(copied, 1)
            v.wait_ge(copied, 6)


def linear_stage(nc, stage, x_tok, ident, wT, b_row, ones_row):
    TILES = x_tok.shape[1]
    GROUPS = TILES // 4
    with ExitStack() as stack:
        mem = Stage(nc, stack, stage)
        nb = norm_buffers(mem, TILES)
        xn = mem.sb("xn", [P, 2, 4, C])
        xnT = mem.sb("xnT", [P, 2, 512])
        ps_T = mem.ps("ps_T", [P, 2, 512])
        ps_y = mem.ps("ps_y", [P, 2, 512])
        s_own, s_xn, s_T, s_Tc, s_y, s_out = (mem.sem(n) for n in ("own", "xn", "turned", "copied", "y", "added"))
        block = stack.enter_context(nc.Block())

        @block.vector
        def _(v):
            own = Tally(v, s_own)
            with own.loop(TILES, 1) as t:
                own.count(v.bn_stats(nb["bn"][:, bass.ds(t, 1), :], x_tok[:, bass.ds(t, 1), :]))
            norm_factors(v, own, nb, TILES)

            def norm(n, k):
                for q in range(4):
                    t = n * 4 + q
                    last = v.tensor_scalar(xn[:, k, q, :], x_tok[:, bass.ds(t, 1), :], nb["mean"][:, bass.ds(t, 1)],
                                           nb["rstd"][:, bass.ds(t, 1)], ALU.subtract, ALU.mult)
                last.then_inc(s_xn, 1)

            def add(n, k):
                v.wait_ge(s_y, n + 1)
                tok = x_tok[:, bass.ds(n * 4, 4), :]
                v.scalar_tensor_tensor(out=tok, in0=ps_y[:, k].rearrange("p (q c) -> p q c", c=C), scalar=0.5,
                                       in1=tok, op0=ALU.mult, op1=ALU.add).then_inc(s_out, 1)

            norm(0, 0)
            norm(1, 1)
            with v.Fori(0, (GROUPS - 2) // 2) as i:
                for k in range(2):
                    add(2 * i + k, k)
                    norm(2 * i + k + 2, k)
            for k in range(2):
                add(GROUPS - 2 + k, k)
            v.wait_ge(s_out, GROUPS)

        @block.scalar
        def _(act):
            with act.Fori(0, GROUPS // 2) as i:
                for k in range(2):
                    act.wait_ge(s_T, 2 * i + k + 1)
                    act.activation(xnT[:, k, :], ps_T[:, k, :], ACT.Copy).then_inc(s_Tc, 1)

        @block.tensor
        def _(pe):
            def turn(n, k):
                pe.wait_ge(s_xn, n + 1)
                for q in range(4):
                    last = pe.transpose(ps_T[:, k, P * q:P * q + P], xn[:, k, q, :], ident[:])
                last.then_inc(s_T, 1)

            def product(n, k, again):
                pe.wait_ge(s_Tc, n + 1)
                if again:
                    pe.wait_ge(s_out, n - 1)
                for q in range(4):
                    o = ps_y[:, k, P * q:P * q + P]
                    pe.matmul(o, xnT[:, k, P * q:P * q + P], wT[:], start=True, stop=False)
                    last = pe.matmul(o, ones_row[:], b_row[:], start=False, stop=True)
                last.then_inc(s_y, 1)

            turn(0, 0)
            turn(1, 1)
            product(0, 0, False)
            turn(2, 0)
            product(1, 1, False)
            with pe.Fori(0, (GROUPS - 4) // 2) as i:
                for k in range(2):
                    turn(2 * i + k + 3, 1 - k)
                    product(2 * i + k + 2, k, True)
            turn(GROUPS - 1, 1)
            product(GROUPS - 2, 0, True)
            product(GROUPS - 1, 1, True)


Q_PARTS = (0, 0, 1, 1, 0, 2)
K_PARTS = (0, 1, 0, 1, 2, 0)
MAX_PARTS = 3


def attention_stage(nc, x_tok, ident, ones_row, w_qkv, b_qkv, w_proj, b_proj, q_dram, k_dram):
    TILES = x_tok.shape[1]
    BT = 8
    L = BT * P
    BATCHES = TILES // BT
    D = 8
    HEADS = C // D
    PAIRS = HEADS // 2
    SCALE = D ** -0.5
    QR = len(Q_PARTS) * D
    KR = QR + MAX_PARTS
    VW = D + 1
    with ExitStack() as stack:
        mem = Stage(nc, stack, "attn")
        v_aug = mem.sb("v_aug", [P, BATCHES, BT, HEADS, VW])
        wqkv = mem.sb("wqkv", [P, 3, C])
        wp = mem.sb("wp", [P, C])
        bqk = mem.sb("bqk", [P, 2])
        bv = mem.sb("bv", [1, C])
        bp = mem.sb("bp", [1, C])

        with ExitStack() as project_stack:
            pm = Stage(nc, project_stack, "qkv")
            nb = norm_buffers(pm, TILES)
            xn = pm.sb("xn", [P, BT, C])
            xnT = pm.sb("xnT", [P, L])
            full = pm.sb("full", [P, 2, L])
            part = pm.sb("part", [P, 2, 3, L], BF16)
            ps_T = pm.ps("ps_T", [P, L])
            ps_q = pm.ps("ps_q", [P, 2, L])
            ps_v = pm.ps("ps_v", [P, BT, C])
            names = "own xn turned copied q_mm v_mm biased split v_copied loaded v_one".split()
            s = {n: pm.sem(n) for n in names}
            stored = [pm.sem(n) for n in ("q_stored", "k_stored")]
            STORES = 16 * len(Q_PARTS)
            block = project_stack.enter_context(nc.Block())

            @block.sync
            def _(sp):
                with nc.allow_non_contiguous_dma(reason="one value per channel"):
                    for dst, src in ((wqkv[:], w_qkv.rearrange("c (k e) -> c k e", k=3)), (wp[:], w_proj),
                                     (bqk[:], b_qkv[0:2 * C].rearrange("(k e) -> e k", k=2)),
                                     (bv[:], b_qkv[2 * C:3 * C].rearrange("(a e) -> a e", a=1)),
                                     (bp[:], b_proj.rearrange("(a e) -> a e", a=1))):
                        sp.dma_start(dst, src).then_inc(s["loaded"], 16)
                for w in range(2):
                    sp.sem_inc(stored[w], STORES)
                with sp.Fori(0, BATCHES) as b:
                    for w, dram, parts_of in ((0, q_dram, Q_PARTS), (1, k_dram, K_PARTS)):
                        sp.wait_ge(s["split"], 2 * b + w + 2)
                        for c, p in enumerate(parts_of):
                            sp.dma_start(dram[bass.ds(b, 1), :, D * c:D * c + D, :].rearrange("a h d t -> (a h) d t"),
                                         part[:, w, p, :]).then_inc(stored[w], 16)
                for w in range(2):
                    sp.wait_ge(stored[w], STORES * (BATCHES + 1))

            @block.gpsimd
            def _(pool):
                pool.memset(v_aug[:, :, :, :, D:VW], 1.0).then_inc(s["v_one"], 1)
                pool.wait_ge(s["v_one"], 1)

            @block.vector
            def _(v):
                own = Tally(v, s["own"])
                with own.loop(TILES, 1) as t:
                    own.count(v.bn_stats(nb["bn"][:, bass.ds(t, 1), :], x_tok[:, bass.ds(t, 1), :]))
                norm_factors(v, own, nb, TILES)
                v.sem_inc(s["split"], 1)
                with own.loop(BATCHES, 6) as b:
                    v.wait_ge(s["split"], 2 * b + 1)
                    for q in range(BT):
                        t = b * BT + q
                        last = v.tensor_scalar(xn[:, q, :], x_tok[:, bass.ds(t, 1), :], nb["mean"][:, bass.ds(t, 1)],
                                               nb["rstd"][:, bass.ds(t, 1)], ALU.subtract, ALU.mult)
                    last.then_inc(s["xn"], 1)
                    v.wait_ge(s["v_mm"], b + 1)
                    v.tensor_copy(v_aug[:, bass.ds(b, 1), :, :, 0:D].rearrange("p a t h d -> p (a t) h d"),
                                  ps_v[:].rearrange("p t (h d) -> p t h d", d=D)).then_inc(s["v_copied"], 1)
                    for w in range(2):
                        v.wait_ge(s["biased"], 2 * b + w + 1)
                        v.wait_ge(stored[w], STORES * (b + 1))
                        own.step(v.tensor_copy(part[:, w, 0, :], full[:, w, :]))
                        own.step(v.tensor_tensor(full[:, w, :], full[:, w, :], part[:, w, 0, :], ALU.subtract))
                        own.step(v.tensor_copy(part[:, w, 1, :], full[:, w, :]))
                        v.tensor_tensor(part[:, w, 2, :], full[:, w, :], part[:, w, 1, :],
                                        ALU.subtract).then_inc(s["split"], 1)
                v.wait_ge(s["v_copied"], BATCHES)

            @block.scalar
            def _(act):
                act.wait_ge(s["loaded"], 80)
                with act.Fori(0, BATCHES) as b:
                    act.wait_ge(s["turned"], b + 1)
                    act.activation(xnT[:], ps_T[:], ACT.Copy).then_inc(s["copied"], 1)
                    for w in range(2):
                        act.wait_ge(s["q_mm"], 2 * b + w + 1)
                        act.activation(full[:, w, :], ps_q[:, w, :], ACT.Identity,
                                       bias=bqk[:, w:w + 1]).then_inc(s["biased"], 1)

            @block.tensor
            def _(pe):
                pe.wait_ge(s["loaded"], 80)
                with pe.Fori(0, BATCHES) as b:
                    pe.wait_ge(s["xn"], b + 1)
                    for q in range(BT):
                        last = pe.transpose(ps_T[:, P * q:P * q + P], xn[:, q, :], ident[:])
                    last.then_inc(s["turned"], 1)
                    pe.wait_ge(s["copied"], b + 1)
                    for q in range(BT):
                        pe.matmul(ps_v[:, q, :], xnT[:, P * q:P * q + P], wqkv[:, 2, :], start=True, stop=False)
                        last = pe.matmul(ps_v[:, q, :], ones_row[:], bv[:], start=False, stop=True)
                    last.then_inc(s["v_mm"], 1)
                    for w in range(2):
                        for c in range(L // 512):
                            last = pe.matmul(ps_q[:, w, 512 * c:512 * c + 512], wqkv[:, w, :],
                                             xnT[:, 512 * c:512 * c + 512], start=True, stop=True)
                        last.then_inc(s["q_mm"], 1)

        with ExitStack() as main_stack:
            mm = Stage(nc, main_stack, "heads")
            q1 = mm.sb("q1", [P, 2, L], BF16)
            k1 = mm.sb("k1", [P, 2, L], BF16)
            q2 = mm.sb("q2", [P, 2, L], BF16)
            k2 = mm.sb("k2", [P, 2, L], BF16)
            ones_bf = mm.sb("ones_bf", [MAX_PARTS, L], BF16)
            top = mm.sb("top", [P, BT, HEADS, 2])
            neg = mm.sb("neg", [P, BT, HEADS])
            neg_part = mm.sb("neg_part", [P, MAX_PARTS, P], BF16)
            neg_rest = mm.sb("neg_rest", [P, P])
            pT = mm.sb("pT", [P, 2, 2, L])
            v_pair = mm.sb("v_pair", [P, BT, 2, 32])
            oT = mm.sb("oT", [P, 512])
            recip = mm.sb("recip", [P, 4, 4])
            o_tok = mm.sb("o_tok", [P, BT, C])
            oTa = mm.sb("oTa", [P, L])
            ps_s = mm.ps("ps_s", [P, 2, L])
            ps_m = mm.ps("ps_m", [P, 2, 512])
            ps_o = mm.ps("ps_o", [P, 512])
            ps_t = mm.ps("ps_t", [P, 4, 4, 32])
            names = ("own first1 k_ones k_ones0 v_zero v_pair s_mm prob pv_step oT o_turned o_norm m_mm top neg neg_turned "
                     "neg_split neg_stored a_turned a_copied out_mm added ones_set").split()
            s = {n: mm.sem(n) for n in names}
            first = [mm.sem(f"first{k}_loaded") for k in range(2)]
            second = [mm.sem(f"second{k}_loaded") for k in range(2)]
            block = main_stack.enter_context(nc.Block())
            MAXES = 4 * BT
            NEG_STORES = 16 * MAX_PARTS
            UNITS = 2 * BT

            def phases(eng, prologue, both, epilogue):
                prologue()
                with eng.Fori(0, BATCHES - 1) as b:
                    both(b)
                epilogue(BATCHES - 1)

            def over_pairs(eng, body):
                with eng.Fori(0, PAIRS // 2) as i:
                    for k in range(2):
                        body(i * 2 + k, i, k)

            @block.sync
            def _(sp):
                def rows(dram, b, pair, j, n):
                    return dram[bass.ds(b, 1), bass.ds(pair * 2 + j, 1), 0:n, :].rearrange("a h r t -> (a h r) t")

                def first_pass(b, pair, k):
                    g = b * PAIRS + pair
                    sp.wait_ge(s["m_mm"], MAXES * (g + 1))
                    for j in range(2):
                        sp.dma_start(q1[64 * j:64 * j + QR, k, :], rows(q_dram, b, pair, j, QR)).then_inc(first[k], 16)
                        sp.dma_start(k1[64 * j:64 * j + QR, k, :], rows(k_dram, b, pair, j, QR)).then_inc(first[k], 16)

                def second_pass(b, pair, k):
                    g = b * PAIRS + pair
                    sp.wait_ge(s["neg_stored"], NEG_STORES * (b + 1))
                    sp.wait_ge(s["s_mm"], UNITS * (g + 1))
                    for j in range(2):
                        sp.dma_start(q2[64 * j:64 * j + KR, k, :], rows(q_dram, b, pair, j, KR)).then_inc(second[k], 16)
                        sp.dma_start(k2[64 * j:64 * j + QR, k, :], rows(k_dram, b, pair, j, QR)).then_inc(second[k], 16)

                def prologue():
                    sp.wait_ge(s["ones_set"], 1)
                    for k in range(2):
                        for j in range(2):
                            sp.dma_start(k2[64 * j + QR:64 * j + KR, k, :], ones_bf[:]).then_inc(s["k_ones"], 16)
                    over_pairs(sp, lambda pair, i, k: first_pass(0, pair, k))

                def both(b):
                    over_pairs(sp, lambda pair, i, k: (second_pass(b, pair, k), first_pass(b + 1, pair, k)))

                def epilogue(b):
                    over_pairs(sp, lambda pair, i, k: second_pass(b, pair, k))
                phases(sp, prologue, both, epilogue)

            @block.gpsimd
            def _(pool):
                pool.memset(ones_bf[:], 1.0).then_inc(s["ones_set"], 1)
                pool.memset(v_pair[:], 0.0).then_inc(s["v_zero"], 1)
                pool.wait_ge(s["v_zero"], 1)

                def store_max(b):
                    pool.wait_ge(s["neg_split"], b + 1)
                    for n in range(MAX_PARTS):
                        pool.dma_start(q_dram[bass.ds(b, 1), :, QR + n:QR + n + 1, :]
                                       .rearrange("a h r (q t) -> q (a h r) t", t=P),
                                       neg_part[:, n, :]).then_inc(s["neg_stored"], 16)

                def pairs(b):
                    with pool.Fori(0, PAIRS) as pair:
                        pool.wait_ge(s["pv_step"], BT * (b * PAIRS + pair) + 2)
                        pool.tensor_copy(v_pair[:, :, :, 0:VW],
                                         v_aug[:, bass.ds(b, 1), :, bass.ds(pair * 2, 2), :]
                                         .rearrange("p a t h d -> p (a t) h d")).then_inc(s["v_pair"], 1)

                store_max(0)
                with pool.Fori(0, BATCHES - 1) as b:
                    pairs(b)
                    store_max(b + 1)
                pairs(BATCHES - 1)
                pool.wait_ge(s["neg_stored"], NEG_STORES * BATCHES)

            @block.scalar
            def _(act):
                def exps(b, pair, k):
                    g = b * PAIRS + pair
                    for t in range(BT):
                        for j in range(2):
                            u = 2 * t + j
                            act.wait_ge(s["s_mm"], UNITS * (g + 2) + u + 1)
                            act.wait_ge(s["pv_step"], BT * g + t + 1)
                            act.activation(pT[:, t % 2, j, :], ps_s[:, j, :], ACT.Exp, scale=SCALE).then_inc(s["prob"], 1)

                def out(b):
                    act.wait_ge(s["a_turned"], b + 1)
                    act.activation(oTa[:], ps_s[:, 0, :], ACT.Copy).then_inc(s["a_copied"], 1)

                def second(b):
                    over_pairs(act, lambda pair, i, k: exps(b, pair, k))
                    out(b)
                with act.Fori(0, BATCHES) as b:
                    second(b)

            @block.tensor
            def _(pe):
                pe.sem_inc(s["m_mm"], 2 * MAXES)
                pe.sem_inc(s["s_mm"], 2 * UNITS)
                pe.sem_inc(s["pv_step"], 2)

                def max_unit(b, pair, k, n):
                    q, j, c = n // 4, (n // 2) % 2, n % 2
                    g = b * PAIRS + pair
                    pe.wait_ge(s["top"], MAXES * g + n + 1)
                    r = slice(64 * j, 64 * j + QR)
                    pe.matmul(ps_m[:, c, :], q1[r, k, P * q:P * q + P], k1[r, k, 512 * c:512 * c + 512], start=True,
                              stop=True).then_inc(s["m_mm"], 1)

                def max_units(b, pair, k, lo, hi):
                    for n in range(lo, hi):
                        max_unit(b, pair, k, n)

                def score(b, pair, k, t, j):
                    g = b * PAIRS + pair
                    pe.wait_ge(s["prob"], UNITS * g + 2 * t + j + 1)
                    r = slice(64 * j, 64 * j + KR)
                    for c in range(L // 512):
                        last = pe.matmul(ps_s[:, j, 512 * c:512 * c + 512], k2[r, k, P * t:P * t + P],
                                         q2[r, k, 512 * c:512 * c + 512], start=True, stop=True)
                    last.then_inc(s["s_mm"], 1)

                def values(b, pair, t):
                    g = b * PAIRS + pair
                    pe.wait_ge(s["prob"], UNITS * g + 2 * t + 2 + 2)
                    if t == 0:
                        pe.wait_ge(s["v_pair"], g + 1)
                        pe.wait_ge(s["oT"], g + 1)
                    for j in range(2):
                        for c in range(2):
                            o = 32 * (2 * j + c)
                            last = pe.matmul(ps_o[o:o + 32, :], v_pair[:, t, j, :], pT[:, t % 2, j, 512 * c:512 * c + 512],
                                             start=(t == 0), stop=(t == BT - 1))
                    last.then_inc(s["pv_step"], 1)

                def turn_out(b, pair):
                    g = b * PAIRS + pair
                    pe.wait_ge(s["oT"], g + 2)
                    pe.wait_ge(s["o_norm"], g + 1)
                    for q in range(4):
                        last = pe.transpose(ps_t[:, q].rearrange("p a d -> p (a d)"), oT[:, P * q:P * q + P], ident[:])
                    last.then_inc(s["o_turned"], 1)

                def second_pass(b, pair, i, k, with_first):
                    g = b * PAIRS + pair
                    share = [0, 2, 4, 6, 8, 10, 12, 14, 16, 18, 20, 22, 24, 25, 26, 27, 28, 32]
                    pe.wait_ge(second[k], 64 * (b * (PAIRS // 2) + i + 1))
                    if with_first:
                        pe.wait_ge(first[k], 64 * ((b + 1) * (PAIRS // 2) + i + 1))
                    for t in range(BT):
                        score(b, pair, k, t, 0)
                        if with_first:
                            max_units(b + 1, pair, k, share[2 * t], share[2 * t + 1])
                        if t:
                            values(b, pair, t - 1)
                        score(b, pair, k, t, 1)
                        if with_first:
                            max_units(b + 1, pair, k, share[2 * t + 1], share[2 * t + 2])
                    values(b, pair, BT - 1)
                    if with_first:
                        max_units(b + 1, pair, k, share[-2], share[-1])
                    turn_out(b, pair)

                def first_pass(b, pair, i, k):
                    pe.wait_ge(first[k], 64 * (b * (PAIRS // 2) + i + 1))
                    max_units(b, pair, k, 0, MAXES)

                def turn_max(b):
                    pe.wait_ge(s["neg"], b + 1)
                    pe.transpose(ps_t[:].rearrange("p a b d -> p (a b d)")[:, 0:P],
                                 neg[:].rearrange("p t h -> p (t h)"), ident[:]).then_inc(s["neg_turned"], 1)

                def out(b):
                    pe.wait_ge(s["o_norm"], (b + 1) * PAIRS + 1)
                    for q in range(BT):
                        last = pe.transpose(ps_s[:, 0, P * q:P * q + P], o_tok[:, q, :], ident[:])
                    last.then_inc(s["a_turned"], 1)
                    pe.wait_ge(s["a_copied"], b + 1)
                    for q in range(BT):
                        o = ps_s[:, 1, P * q:P * q + P]
                        pe.matmul(o, oTa[:, P * q:P * q + P], wp[:], start=True, stop=False)
                        last = pe.matmul(o, ones_row[:], bp[:], start=False, stop=True)
                    last.then_inc(s["out_mm"], 1)
                    pe.wait_ge(s["added"], b + 1)

                def prologue():
                    over_pairs(pe, lambda pair, i, k: first_pass(0, pair, i, k))
                    turn_max(0)
                    pe.wait_ge(s["k_ones"], 64)

                def both(b):
                    over_pairs(pe, lambda pair, i, k: second_pass(b, pair, i, k, True))
                    turn_max(b + 1)
                    out(b)

                def epilogue(b):
                    over_pairs(pe, lambda pair, i, k: second_pass(b, pair, i, k, False))
                    out(b)
                phases(pe, prologue, both, epilogue)

            @block.vector
            def _(v):
                own = Tally(v, s["own"])
                v.sem_inc(s["top"], 2)
                v.sem_inc(s["prob"], 2)
                v.sem_inc(s["oT"], 1)
                v.sem_inc(s["o_norm"], 1)

                def maxima(b, pair, lo, hi):
                    g = b * PAIRS + pair
                    for n in range(lo, hi):
                        q, j, c = n // 4, (n // 2) % 2, n % 2
                        v.wait_ge(s["m_mm"], MAXES * (g + 2) + n + 1)
                        v.tensor_reduce(top[:, q, bass.ds(pair * 2 + j, 1), c], ps_m[:, c, :], AX.X,
                                        ALU.max).then_inc(s["top"], 1)

                def negate(b, again):
                    v.wait_ge(s["top"], MAXES * PAIRS * (b + 1) + 2)
                    own.step(v.tensor_tensor(neg[:], top[:, :, :, 0], top[:, :, :, 1], ALU.max))
                    v.tensor_scalar(neg[:], neg[:], -1.0, None, ALU.mult).then_inc(s["neg"], 1)
                    v.wait_ge(s["neg_turned"], b + 1)
                    if again:
                        v.wait_ge(s["neg_stored"], NEG_STORES * b)
                    turned = ps_t[:].rearrange("p a b d -> p (a b d)")[:, 0:P]
                    own.step(v.tensor_copy(neg_part[:, 0, :], turned))
                    own.step(v.tensor_tensor(neg_rest[:], turned, neg_part[:, 0, :], ALU.subtract))
                    own.step(v.tensor_copy(neg_part[:, 1, :], neg_rest[:]))
                    v.tensor_tensor(neg_part[:, 2, :], neg_rest[:], neg_part[:, 1, :],
                                    ALU.subtract).then_inc(s["neg_split"], 1)

                def copy_sums(b, pair):
                    g = b * PAIRS + pair
                    v.wait_ge(s["pv_step"], BT * (g + 1) + 2)
                    v.wait_ge(s["o_turned"], g + 1)
                    v.tensor_copy(oT[:], ps_o[:]).then_inc(s["oT"], 1)

                def divide(b, pair):
                    g = b * PAIRS + pair
                    v.wait_ge(s["o_turned"], g + 2)
                    own.step(v.reciprocal(recip[:], ps_t[:, :, :, D]))
                    for j in range(2):
                        for c in range(2):
                            last = v.tensor_tensor(
                                o_tok[:, 4 * c:4 * c + 4, bass.ds(pair * 2 * D + j * D, D)],
                                ps_t[:, :, 2 * j + c, 0:D],
                                recip[:, :, 2 * j + c:2 * j + c + 1].broadcast_to([P, 4, D]), ALU.mult)
                    last.then_inc(s["o_norm"], 1)

                def second(b, pair, with_first):
                    if with_first:
                        maxima(b + 1, pair, 0, 28)
                    copy_sums(b, pair)
                    if with_first:
                        maxima(b + 1, pair, 28, MAXES)
                    divide(b, pair)

                def add(b):
                    v.wait_ge(s["out_mm"], b + 1)
                    tok = x_tok[:, bass.ds(b * BT, BT), :]
                    v.tensor_tensor(tok, tok, ps_s[:, 1, :].rearrange("p (t c) -> p t c", c=C),
                                    ALU.add).then_inc(s["added"], 1)

                v.sem_inc(s["o_turned"], 1)
                with v.Fori(0, PAIRS) as pair:
                    maxima(0, pair, 0, MAXES)
                negate(0, False)
                with own.loop(BATCHES - 1, PAIRS + 4) as b:
                    with own.loop(PAIRS, 1) as pair:
                        second(b, pair, True)
                    negate(b + 1, True)
                    add(b)
                with own.loop(PAIRS, 1) as pair:
                    second(BATCHES - 1, pair, False)
                add(BATCHES - 1)
                v.wait_ge(s["added"], BATCHES)


def build_program(nc, x, ln_w, ln_b, in_w, conv_w, conv_b, xp_w, dtp_w, dtp_b, A_log, D_skip, out_w, nf_w, nf_b,
                  Wr, br, W1, W2, w_qkv, b_qkv, w_proj, b_proj, W, b, lora_down, lora_up, down_aux, up_aux, out):
    B, L, _ = x.shape
    TILES = B * L // P
    E = Wr.shape[1]
    HEADS, D = 16, C // 16
    with ExitStack() as stack:
        x_tok = stack.enter_context(nc.sbuf_tensor("x_tok", [P, TILES, C], F32))
        ident = stack.enter_context(nc.sbuf_tensor("ident", [P, P], F32))
        tri = stack.enter_context(nc.sbuf_tensor("tri", [P, P], BF16))
        ones_bf = stack.enter_context(nc.sbuf_tensor("ones_bf", [P, P], BF16))
        wT = stack.enter_context(nc.sbuf_tensor("wT", [P, C], F32))
        b_row = stack.enter_context(nc.sbuf_tensor("b_row", [1, C], F32))
        ones_row = stack.enter_context(nc.sbuf_tensor("ones_row", [1, C], F32))
        sorted_x = nc.dram_tensor("sorted_x", [(TILES + E) * P, C], F32, kind="Internal").ap()
        sorted_y = nc.dram_tensor("sorted_y", [(TILES + E) * P, C], F32, kind="Internal").ap()
        q_rows = nc.dram_tensor("q_rows", [B, HEADS, len(Q_PARTS) * D + MAX_PARTS, L], BF16, kind="Internal").ap()
        k_rows = nc.dram_tensor("k_rows", [B, HEADS, len(K_PARTS) * D, L], BF16, kind="Internal").ap()
        tokens = "b (t p) c -> p (b t) c"
        load_stage(nc, x.rearrange(tokens, p=P), x_tok, ident, tri, ones_bf)
        moe_stage(nc, "moe0", x_tok, ident, tri, ones_bf, Wr, br, W1, W2, sorted_x, sorted_y, True)
        mamba_stage(nc, x_tok, ident, ln_w, ln_b, in_w, conv_w, conv_b, xp_w, dtp_w, dtp_b, A_log, D_skip, out_w,
                    nf_w, nf_b)
        moe_stage(nc, "moe1", x_tok, ident, tri, ones_bf, Wr, br, W1, W2, sorted_x, sorted_y, False)
        lora_weight_stage(nc, ident, wT, b_row, ones_row, W, b, lora_down, lora_up, down_aux, up_aux)
        linear_stage(nc, "linear0", x_tok, ident, wT, b_row, ones_row)
        attention_stage(nc, x_tok, ident, ones_row, w_qkv, b_qkv, w_proj, b_proj, q_rows, k_rows)
        linear_stage(nc, "linear1", x_tok, ident, wT, b_row, ones_row)
        store_stage(nc, x_tok, out.rearrange(tokens, p=P))


_INS = ["L0_attn_x", "L0_attn_ln_w", "L0_attn_ln_b", "L0_attn_in_proj_w", "L0_attn_conv_w", "L0_attn_conv_b",
        "L0_attn_x_proj_w", "L0_attn_dt_proj_w", "L0_attn_dt_proj_b", "L0_attn_A_log", "L0_attn_D_skip",
        "L0_attn_out_proj_w", "L0_attn_norm_f_w", "L0_attn_norm_f_b", "L0_ffn_Wr", "L0_ffn_br", "L0_ffn_W1",
        "L0_ffn_W2", "L1_attn_w_qkv", "L1_attn_b_qkv", "L1_attn_w_proj", "L1_attn_b_proj", "L1_ffn_W", "L1_ffn_b",
        "L1_ffn_lora_down", "L1_ffn_lora_up", "L1_ffn_down_aux", "L1_ffn_up_aux"]
_OUTS = [((4, 1024, 128), "float32")]


def kernel(**inputs):
    import numpy as _np
    import concourse.bacc as _bacc
    from concourse import mybir as _mybir
    from concourse.bass_utils import run_bass_kernel_spmd as _run

    nc = _bacc.Bacc("TRN2", target_bir_lowering=False, num_devices=1)
    arrays, args = {}, []
    for name in _INS:
        a = _np.ascontiguousarray(inputs[name])
        arrays[f"in_{name}_dram"] = a
        args.append(nc.dram_tensor(f"in_{name}_dram", a.shape, _mybir.dt.from_np(a.dtype), kind="ExternalInput").ap())
    for i, (shape, dtype) in enumerate(_OUTS):
        dt = _mybir.dt.from_np(_np.dtype(dtype))
        args.append(nc.dram_tensor(f"out_{i}_dram", shape, dt, kind="ExternalOutput").ap())
    build_program(nc, *args)
    r = _run(nc, [arrays], core_ids=[0])
    got = tuple(r.results[0][f"out_{i}_dram"] for i in range(len(_OUTS)))
    return got[0]
```

```python
from contextlib import ExitStack, contextmanager

import numpy as np

import concourse.bass as bass
from concourse import mybir

ALU = mybir.AluOpType
ACT = mybir.ActivationFunctionType
AX = mybir.AxisListType
F32 = mybir.dt.float32
BF16 = mybir.dt.bfloat16
I32 = mybir.dt.int32
U32 = mybir.dt.uint32

P = 128
C = 128
EPS = 1e-5


class Tally:

    def __init__(self, eng, sem):
        self.eng, self.sem, self.n, self.base = eng, sem, 0, 0

    def count(self, inst):
        inst.then_inc(self.sem, 1)
        self.n += 1

    def wait(self):
        self.eng.wait_ge(self.sem, self.base + self.n)

    def step(self, inst):
        self.count(inst)
        self.wait()

    @contextmanager
    def loop(self, times, each):
        start, outer = self.n, self.base
        with self.eng.Fori(0, times) as i:
            self.base = outer + i * each
            yield i
        assert self.n - start == each, (self.n - start, each)
        self.n, self.base = start + each * times, outer


class Stage:

    def __init__(self, nc, stack, stage):
        self.nc, self.stack, self.stage, self.sems = nc, stack, stage, []
        stack.callback(self.release)

    def sb(self, name, shape, dt=F32):
        return self.stack.enter_context(self.nc.sbuf_tensor(f"{self.stage}_{name}", shape, dt))

    def ps(self, name, shape, dt=F32):
        return self.stack.enter_context(self.nc.psum_tensor(f"{self.stage}_{name}", shape, dt))

    def sem(self, name):
        self.sems.append(self.nc.alloc_semaphore(f"{self.stage}_{name}"))
        return self.sems[-1]

    def release(self):
        if self.sems:
            self.nc.clear_and_free_semaphores(self.sems)
            self.nc.all_engine_barrier()


def norm_buffers(mem, tiles):
    return {
        "bn": mem.sb("bn", [P, tiles, 6]),
        "mean": mem.sb("mean", [P, tiles]),
        "var": mem.sb("var", [P, tiles]),
        "rstd": mem.sb("rstd", [P, tiles]),
        "tmp": mem.sb("tmp", [P, 2, tiles]),
    }


def norm_factors(v, own, b, tiles, first=0):
    s = slice(first, first + tiles)
    bn, mean, var, y = b["bn"][:, s, :], b["mean"][:, s], b["var"][:, s], b["rstd"][:, s]
    t0, t1 = b["tmp"][:, 0, s], b["tmp"][:, 1, s]
    own.wait()
    own.count(v.tensor_tensor(t0, bn[:, :, 1], bn[:, :, 4], ALU.subtract))
    own.count(v.tensor_tensor(t1, bn[:, :, 2], bn[:, :, 5], ALU.add))
    own.step(v.tensor_tensor(mean, bn[:, :, 1], bn[:, :, 4], ALU.add))
    own.count(v.scalar_tensor_tensor(out=t0, in0=t0, scalar=0.25, in1=t0, op0=ALU.mult, op1=ALU.mult))
    own.count(v.tensor_scalar(t1, t1, 1.0 / C, EPS, ALU.mult, ALU.add))
    own.step(v.tensor_scalar(mean, mean, 0.5, None, ALU.mult))
    own.step(v.tensor_tensor(var, t0, t1, ALU.add))
    own.step(v.tensor_scalar(t0.bitcast(I32), var.bitcast(I32), 1, None, ALU.logical_shift_right))
    own.step(v.tensor_scalar(y.bitcast(I32), t0.bitcast(I32), -1, 0x5F3759DF, ALU.mult, ALU.add))
    for _ in range(3):
        own.step(v.tensor_tensor(t0, y, y, ALU.mult))
        own.step(v.scalar_tensor_tensor(out=t0, in0=t0, scalar=-0.5, in1=var, op0=ALU.mult, op1=ALU.mult))
        own.step(v.scalar_tensor_tensor(out=y, in0=t0, scalar=1.5, in1=y, op0=ALU.add, op1=ALU.mult))


NORM_STEPS = 7 + 2 + 9


def load_stage(nc, x_dram, x_tok, ident, tri, ones_bf):
    with ExitStack() as stack:
        mem = Stage(nc, stack, "load")
        x_loaded, cleared, made = mem.sem("x_loaded"), mem.sem("cleared"), mem.sem("made")
        block = stack.enter_context(nc.Block())

        @block.sync
        def _(sp):
            for q in range(4):
                sp.dma_start(x_tok[:, 8 * q:8 * q + 8, :], x_dram[:, 8 * q:8 * q + 8, :]).then_inc(x_loaded, 16)
            sp.wait_ge(x_loaded, 64)

        @block.gpsimd
        def _(pool):
            pool.memset(ident[:], 0.0).then_inc(cleared, 1)
            pool.memset(tri[:], 0.0).then_inc(cleared, 1)
            pool.memset(ones_bf[:], 1.0).then_inc(cleared, 1)
            pool.wait_ge(cleared, 3)
            pool.affine_select(out=ident[:], in_=ident[:], compare_op=ALU.not_equal, fill=1.0, base=0,
                               pattern=[[-1, P]], channel_multiplier=1).then_inc(made, 1)
            pool.affine_select(out=tri[:], in_=tri[:], compare_op=ALU.is_ge, fill=1.0, base=0,
                               pattern=[[-1, P]], channel_multiplier=1).then_inc(made, 1)
            pool.wait_ge(made, 2)


def store_stage(nc, x_tok, out_dram):
    with ExitStack() as stack:
        mem = Stage(nc, stack, "store")
        stored = mem.sem("stored")
        block = stack.enter_context(nc.Block())

        @block.sync
        def _(sp):
            for q in range(4):
                sp.dma_start(out_dram[:, 8 * q:8 * q + 8, :], x_tok[:, 8 * q:8 * q + 8, :]).then_inc(stored, 16)
            sp.wait_ge(stored, 64)


def moe_stage(nc, stage, x_tok, ident, tri, ones_bf, Wr, br, W1, W2, sorted_x, sorted_y, clear_sorted):
    TILES = x_tok.shape[1]
    E = Wr.shape[1]
    F = W1.shape[2]
    FB = F // P
    SLOTS = TILES + E
    GROUPS = TILES // 4
    x_slots = sorted_x.rearrange("(n p) c -> p n c", p=P)
    y_slots = sorted_y.rearrange("(n p) c -> p n c", p=P)
    with ExitStack() as stack:
        mem = Stage(nc, stack, stage)
        w1 = mem.sb("w1", [P, E, F])
        w2 = mem.sb("w2", [P, E, FB, C])
        wr = mem.sb("wr", [P, E])
        br_row = mem.sb("br_row", [P, E])
        nb = norm_buffers(mem, TILES)
        xn = mem.sb("xn", [P, TILES, C])
        xn_ring = mem.sb("xn_ring", [P, 2, 4, C])
        xnT = mem.sb("xnT", [P, 2, 4 * P])
        prob = mem.sb("prob", [P, TILES, E])
        pick = mem.sb("pick", [P, TILES, E])
        work = mem.sb("work", [P, TILES, E])
        best = mem.sb("best", [P, TILES])
        pos = mem.sb("pos", [P, TILES])
        pos_i = mem.sb("pos_i", [P, TILES], U32)
        mask_bf = mem.sb("mask_bf", [P, TILES, E], BF16)
        prefer = mem.sb("prefer", [P, E])
        ones = mem.sb("ones", [P, TILES])
        upto = mem.sb("upto", [P, TILES, E])
        total = mem.sb("total", [P, 4, E])
        total_i = mem.sb("total_i", [P, E], I32)
        slot_no = mem.sb("slot_no", [P, SLOTS, E])
        slot_e = mem.sb("slot_e", [P, SLOTS])
        slot_i = mem.sb("slot_i", [P, SLOTS], I32)
        zero = mem.sb("zero", [P, 4 * C])
        xs = mem.sb("xs", [P, 2, C])
        xsT = mem.sb("xsT", [P, 2, P])
        hs = mem.sb("hs", [P, 2, F])
        hT = mem.sb("hT", [P, 2, FB, P])
        ys = mem.sb("ys", [P, 2, C])
        yg = xn
        s_w, s_wr, s_zero, s_const, s_stored0 = (mem.sem(n) for n in
                                                 ("w_loaded", "wr_loaded", "zeroed", "const", "cleared"))
        s_norm, s_ring, s_T, s_Tc, s_logit = (mem.sem(n) for n in
                                              ("norm", "ring", "xnT", "xnT_copied", "logits"))
        s_v, s_z, s_exp, s_mask, s_pre, s_pos, s_slots = (mem.sem(n) for n in
                                                          ("own", "z", "exp", "mask", "prefix", "pos", "slots"))
        s_scat = mem.sem("scattered")
        s_xs = [mem.sem(f"xs{k}_loaded") for k in range(2)]
        s_out = [mem.sem(f"ys{k}_stored") for k in range(2)]
        s_xsT, s_xsTc, s_up, s_gelu, s_hT, s_hTc, s_down, s_ys, s_gath = (mem.sem(n) for n in (
            "xsT", "xsT_copied", "up", "gelu", "hT", "hT_copied", "down", "ys", "gathered"))

        with ExitStack() as route_stack:
            pmem = Stage(nc, route_stack, stage + "r")
            xnT_ps = pmem.ps("xnT_ps", [P, 2, 4 * P])
            logit_ps = pmem.ps("logit_ps", [P, TILES, E])
            pre_ps = pmem.ps("pre_ps", [P, 2, 512])
            block = route_stack.enter_context(nc.Block())

            @block.sync
            def _(sp):
                sp.dma_start(wr[:], Wr).then_inc(s_wr, 16)
                sp.dma_start(br_row[:], br.rearrange("(a e) -> a e", a=1).broadcast_to([P, E])).then_inc(s_wr, 16)
                for e in range(0, E, 2):
                    sp.dma_start(w1[:, e:e + 2, :], W1[e:e + 2].rearrange("e c f -> c e f")).then_inc(s_w, 16)
                    sp.dma_start(w2[:, e:e + 2, :, :],
                                 W2[e:e + 2].rearrange("e (k f) c -> f e k c", f=P)).then_inc(s_w, 16)
                if clear_sorted:
                    sp.wait_ge(s_zero, 1)
                    for n in range(SLOTS // 4):
                        sp.dma_start(x_slots[:, 4 * n:4 * n + 4, :],
                                     zero[:].rearrange("p (n c) -> p n c", c=C)).then_inc(s_stored0, 16)
                    sp.wait_ge(s_stored0, 16 * (SLOTS // 4))
                sp.wait_ge(s_w, 16 * E)

            @block.gpsimd
            def _(pool):
                pool.memset(zero[:], 0.0).then_inc(s_zero, 1)
                pool.iota(prefer[:], pattern=[[-1, E]], base=E, channel_multiplier=0,
                          allow_small_or_imprecise_dtypes=True).then_inc(s_const, 1)
                pool.iota(slot_no[:], pattern=[[1, SLOTS], [0, E]], base=0, channel_multiplier=0,
                          allow_small_or_imprecise_dtypes=True).then_inc(s_const, 1)
                pool.memset(ones[:], 1.0).then_inc(s_const, 1)
                if clear_sorted:
                    pool.wait_ge(s_stored0, 16 * (SLOTS // 4))
                pool.wait_ge(s_pos, 1)
                for t in range(TILES):
                    pool.indirect_dma_start(sorted_x, bass.IndirectOffsetOnAxis(pos_i[:, t:t + 1], 0), xn[:, t, :],
                                            None).then_inc(s_scat, 16)
                pool.wait_ge(s_scat, 16 * TILES)

            @block.vector
            def _(v):
                own = Tally(v, s_v)
                with own.loop(TILES, 1) as t:
                    own.count(v.bn_stats(nb["bn"][:, bass.ds(t, 1), :], x_tok[:, bass.ds(t, 1), :]))
                norm_factors(v, own, nb, TILES)
                for g in range(GROUPS):
                    for t in range(4 * g, 4 * g + 4):
                        v.tensor_scalar(xn[:, t, :], x_tok[:, t, :], nb["mean"][:, t:t + 1],
                                        nb["rstd"][:, t:t + 1], ALU.subtract, ALU.mult).then_inc(s_norm, 1)
                    if g >= 1:
                        v.wait_ge(s_T, g)
                        if g >= 3:
                            v.wait_ge(s_logit, g - 2)
                        v.tensor_copy(xnT[:, (g - 1) % 2, :], xnT_ps[:, (g - 1) % 2, :]).then_inc(s_Tc, 1)
                v.wait_ge(s_T, GROUPS)
                v.wait_ge(s_logit, GROUPS - 2)
                v.tensor_copy(xnT[:, (GROUPS - 1) % 2, :], xnT_ps[:, (GROUPS - 1) % 2, :]).then_inc(s_Tc, 1)

                v.wait_ge(s_wr, 32)
                v.wait_ge(s_const, 3)
                v.wait_ge(s_logit, GROUPS)

                def over_tiles(row):
                    return row.rearrange("p (a e) -> p a e", a=1).broadcast_to([P, TILES, E])

                def over_experts(col, n=TILES):
                    return col.rearrange("p (t a) -> p t a", a=1).broadcast_to([P, n, E])

                v.tensor_tensor(work[:], logit_ps[:], over_tiles(br_row[:]), ALU.add).then_inc(s_z, 1)
                v.wait_ge(s_exp, 1)
                own.step(v.tensor_scalar(work[:], prob[:], 1.0, None, ALU.add))
                own.step(v.reciprocal(prob[:], work[:]))
                own.step(v.tensor_reduce(best[:], prob[:], AX.X, ALU.max))
                own.step(v.tensor_tensor(pick[:], prob[:], over_experts(best[:]), ALU.is_equal))
                own.step(v.tensor_tensor(work[:], pick[:], over_tiles(prefer[:]), ALU.mult))
                own.step(v.tensor_reduce(pos[:], work[:], AX.X, ALU.max))
                own.step(v.tensor_tensor(pick[:], work[:], over_experts(pos[:]), ALU.is_equal))
                v.tensor_copy(mask_bf[:], pick[:]).then_inc(s_mask, 1)
                own.step(v.tensor_scalar(best[:], best[:], 0.5, None, ALU.mult))
                v.wait_ge(s_pre, 1)
                count = pre_ps[:, 1, 0:TILES * E].rearrange("p (t e) -> p t e", e=E)
                before = pre_ps[:, 0, 0:TILES * E].rearrange("p (t e) -> p t e", e=E)
                own.step(v.tensor_copy(work[:], count))
                for e in range(E):
                    own.count(v.tensor_tensor_scan(upto[:, :, e], ones[:], work[:, :, e], 0.0, ALU.mult, ALU.add))
                own.wait()
                tot, tiles_of, end, start = (total[:, k, :] for k in range(4))
                own.step(v.tensor_scalar(tot, upto[:, TILES - 1, :], float(P - 1), None, ALU.add))
                own.step(v.tensor_copy(total_i[:], tot))
                own.step(v.tensor_scalar(total_i[:], total_i[:], 7, None, ALU.logical_shift_right))
                own.step(v.tensor_copy(tiles_of, total_i[:]))
                own.step(v.tensor_tensor_scan(end, ones[:, 0:E], tiles_of, 0.0, ALU.mult, ALU.add))
                own.step(v.tensor_tensor(start, end, tiles_of, ALU.subtract))
                own.step(v.tensor_scalar(start, start, float(P), None, ALU.mult))
                own.step(v.tensor_tensor(upto[:], upto[:], work[:], ALU.subtract))
                own.step(v.tensor_tensor(upto[:], upto[:], before, ALU.add))
                own.step(v.tensor_tensor(upto[:], upto[:], over_tiles(start), ALU.add))
                own.step(v.tensor_tensor(upto[:], upto[:], pick[:], ALU.mult))
                own.step(v.tensor_reduce(pos[:], upto[:], AX.X, ALU.add))
                v.tensor_copy(pos_i[:], pos[:]).then_inc(s_pos, 1)
                own.step(v.tensor_tensor(slot_no[:], slot_no[:],
                                         end.rearrange("p (a e) -> p a e", a=1).broadcast_to([P, SLOTS, E]),
                                         ALU.is_ge))
                own.step(v.tensor_reduce(slot_e[:], slot_no[:], AX.X, ALU.add))
                own.step(v.tensor_scalar(slot_e[:], slot_e[:], float(E - 1), None, ALU.min))
                own.step(v.tensor_copy(slot_i[:], slot_e[:]))

            @block.scalar
            def _(act):
                for g in range(GROUPS):
                    act.wait_ge(s_norm, 4 * g + 4)
                    if g >= 2:
                        act.wait_ge(s_T, g - 1)
                    act.activation(xn_ring[:, g % 2], xn[:, 4 * g:4 * g + 4, :], ACT.Copy).then_inc(s_ring, 1)
                act.wait_ge(s_z, 1)
                act.activation(prob[:], work[:], ACT.Exp, scale=-1.0).then_inc(s_exp, 1)

            @block.tensor
            def _(pe):
                def logits(g):
                    pe.wait_ge(s_Tc, g + 1)
                    for k in range(4):
                        last = pe.matmul(logit_ps[:, 4 * g + k, :], xnT[:, g % 2, P * k:P * k + P], wr[:],
                                         start=True, stop=True)
                    last.then_inc(s_logit, 1)

                pe.wait_ge(s_wr, 32)
                for g in range(GROUPS):
                    pe.wait_ge(s_ring, g + 1)
                    if g >= 2:
                        pe.wait_ge(s_Tc, g - 1)
                    for k in range(4):
                        last = pe.transpose(xnT_ps[:, g % 2, P * k:P * k + P], xn_ring[:, g % 2, k, :], ident[:])
                    last.then_inc(s_T, 1)
                    if g >= 1:
                        logits(g - 1)
                logits(GROUPS - 1)
                pe.wait_ge(s_mask, 1)
                m = mask_bf[:].rearrange("p t e -> p (t e)")
                pe.matmul(pre_ps[:, 0, 0:TILES * E], tri[:], m, start=True, stop=True)
                pe.matmul(pre_ps[:, 1, 0:TILES * E], ones_bf[:], m, start=True, stop=True).then_inc(s_pre, 1)

        with ExitStack() as expert_stack:
            pmem = Stage(nc, expert_stack, stage + "e")
            xsT_ps = pmem.ps("xsT_ps", [P, 512])
            up_ps = pmem.ps("up_ps", [P, 2, F])
            hT_ps = pmem.ps("hT_ps", [P, 2, FB, P])
            y_ps = pmem.ps("y_ps", [P, 2, 512])
            block = expert_stack.enter_context(nc.Block())
            PAIRS = (SLOTS - 2) // 2

            @block.sync
            def _(sp):
                def load(j, k, n, again):
                    if again:
                        sp.wait_ge(s_xsT, j - 1)
                    sp.dma_start(xs[:, k, :], x_slots[:, bass.ds(j, 1), :]).then_inc(s_xs[k], 16)

                load(0, 0, 0, False)
                load(1, 1, 0, False)
                with sp.Fori(0, PAIRS) as i:
                    for k in range(2):
                        load(2 * i + k + 2, k, i + 1, True)

            @block.scalar
            def _(act):
                def gelu(j, k):
                    act.wait_ge(s_up, j + 1)
                    act.activation(hs[:, k, :], up_ps[:, k, :], ACT.Gelu).then_inc(s_gelu, 1)

                def store(j, k):
                    act.wait_ge(s_ys, j + 1)
                    act.dma_start(y_slots[:, bass.ds(j, 1), :], ys[:, k, :]).then_inc(s_out[k], 16)

                gelu(0, 0)
                gelu(1, 1)
                with act.Fori(0, PAIRS) as i:
                    for k in range(2):
                        gelu(2 * i + k + 2, k)
                        store(2 * i + k, k)
                store(SLOTS - 2, 0)
                store(SLOTS - 1, 1)
                for k in range(2):
                    act.wait_ge(s_out[k], 16 * (SLOTS // 2))

            @block.tensor
            def _(pe):
                def turn_x(k, n):
                    pe.wait_ge(s_xs[k], 16 * (n + 1))
                    pe.transpose(xsT_ps[:, 0:P], xs[:, k, :], ident[:]).then_inc(s_xsT, 1)

                def up(j, k, e):
                    pe.wait_ge(s_xsTc, j + 1)
                    pe.matmul(up_ps[:, k, :], xsT[:, k, :], w1[:, bass.ds(e, 1), :], start=True,
                              stop=True).then_inc(s_up, 1)

                def turn_h(j, k):
                    pe.wait_ge(s_gelu, j + 1)
                    for q in range(FB):
                        last = pe.transpose(hT_ps[:, k, q, :], hs[:, k, P * q:P * q + P], ident[:])
                    last.then_inc(s_hT, 1)

                def down(j, k, e):
                    pe.wait_ge(s_hTc, j + 1)
                    for q in range(FB):
                        last = pe.matmul(y_ps[:, k, 0:C], hT[:, k, q, :], w2[:, bass.ds(e, 1), q, :],
                                         start=(q == 0), stop=(q == FB - 1))
                    last.then_inc(s_down, 1)

                def expert(j):
                    return pe.value_load(slot_i[0:1, bass.ds(j, 1)], min_val=0, max_val=E - 1)

                turn_x(0, 0)
                up(0, 0, expert(0))
                turn_x(1, 0)
                with pe.Fori(0, PAIRS) as i:
                    for k in range(2):
                        j = 2 * i + k + 1
                        turn_h(j - 1, k)
                        up(j, 1 - k, expert(j))
                        turn_x(k, i + 1)
                        down(j - 1, k, expert(j - 1))
                j = SLOTS - 1
                turn_h(j - 1, 0)
                up(j, 1, expert(j))
                down(j - 1, 0, expert(j - 1))
                turn_h(j, 1)
                down(j, 1, expert(j))

            @block.vector
            def _(v):
                def copy_x(j, k):
                    v.wait_ge(s_xsT, j + 1)
                    v.tensor_copy(xsT[:, k, :], xsT_ps[:, 0:P]).then_inc(s_xsTc, 1)

                def copy_h(j, k):
                    v.wait_ge(s_hT, j + 1)
                    v.tensor_copy(hT[:, k], hT_ps[:, k]).then_inc(s_hTc, 1)

                def copy_y(j, k, stored):
                    v.wait_ge(s_down, j + 1)
                    if stored is not None:
                        v.wait_ge(s_out[k], 16 * stored)
                    v.tensor_copy(ys[:, k, :], y_ps[:, k, 0:C]).then_inc(s_ys, 1)

                copy_x(0, 0)
                copy_x(1, 1)
                for k in range(2):
                    copy_h(k, k)
                    copy_x(k + 2, k)
                    copy_y(k, k, None)
                with v.Fori(0, PAIRS - 2) as i:
                    for k in range(2):
                        j = 2 * i + k + 2
                        copy_h(j, k)
                        copy_x(j + 2, k)
                        copy_y(j, k, i + 1)
                for j in range(SLOTS - 4, SLOTS):
                    copy_h(j, j % 2)
                    if j + 2 < SLOTS:
                        copy_x(j + 2, j % 2)
                    copy_y(j, j % 2, j // 2)
                v.wait_ge(s_gath, 16 * TILES)
                for t in range(TILES):
                    v.scalar_tensor_tensor(out=x_tok[:, t, :], in0=yg[:, t, :], scalar=best[:, t:t + 1],
                                           in1=x_tok[:, t, :], op0=ALU.mult, op1=ALU.add)

            @block.gpsimd
            def _(pool):
                for k in range(2):
                    pool.wait_ge(s_out[k], 16 * (SLOTS // 2))
                for t in range(TILES):
                    pool.indirect_dma_start(yg[:, t, :], None, sorted_y,
                                            bass.IndirectOffsetOnAxis(pos_i[:, t:t + 1], 0)).then_inc(s_gath, 16)


_NODES = (np.cos((2 * np.arange(5) + 1) * np.pi / 10) + 1) / 16
LOG1P = [float(c) for c in np.polyfit(_NODES, np.log1p(_NODES) / _NODES, 4)]


def mamba_stage(nc, x_tok, ident, ln_w, ln_b, in_w, conv_w, conv_b, xp_w, dtp_w, dtp_b, A_log, D_skip, out_w,
                nf_w, nf_b):
    LAYERS, DI, N = A_log.shape
    TAPS = conv_w.shape[2]
    R = dtp_w.shape[2]
    HALVES = DI // P
    TILES = x_tok.shape[1]
    BT = 8
    L = BT * P
    BATCHES = TILES // BT
    CH = L // 512
    BC = 2 * N
    ROWS = 3 * BC + R
    with ExitStack() as stack:
        mem = Stage(nc, stack, "mamba")
        r_tok = mem.sb("r_tok", [P, TILES, C])
        nb = norm_buffers(mem, TILES)
        w_in = mem.sb("w_in", [P, 2 * HALVES, C])
        w_tap = mem.sb("w_tap", [P, 2, C])
        wT = mem.sb("wT", [P, HALVES * TAPS + HALVES, P])
        cw = mem.sb("cw", [P, HALVES, TAPS])
        cb = mem.sb("cb", [P, HALVES])
        dtb = mem.sb("dtb", [P, HALVES])
        dsk = mem.sb("dsk", [P, HALVES])
        diag = mem.sb("diag", [P, HALVES, P])
        xp_in = mem.sb("xp_in", [ROWS, DI])
        xpT = mem.sb("xpT", [P, HALVES, ROWS])
        dtp_in = mem.sb("dtp_in", [P, HALVES, ROWS])
        dtpT = mem.sb("dtpT", [ROWS, DI])
        ow_in = mem.sb("ow_in", [P, DI])
        owT = mem.sb("owT", [P, HALVES, C])
        alog = mem.sb("alog", [P, HALVES, N])
        aneg = mem.sb("aneg", [P, HALVES, N])
        lnw = mem.sb("lnw", [P, 2])
        nfw = mem.sb("nfw", [P, 2, C])
        sel = mem.sb("sel", [3 * BC, BC, P], BF16)
        hn = mem.sb("hn", [P, BT, C])
        hT = mem.sb("hT", [P, TAPS - 1 + L])
        xc = mem.sb("xc", [P, HALVES, L])
        zs = mem.sb("zs", [P, HALVES, L])
        dt = mem.sb("dt", [P, HALVES, L])
        u = mem.sb("u", [P, HALVES, L])
        dt8 = mem.sb("dt8", [ROWS, L])
        parts = mem.sb("parts", [3 * BC, L], BF16)
        mid = mem.sb("mid", [3 * BC, L], BF16)
        rest = mem.sb("rest", [3 * BC, L])
        dA = mem.sb("dA", [P, 2, HALVES, L])
        dBu = mem.sb("dBu", [P, 2, HALVES, L])
        Bs = mem.sb("Bs", [P, 2, L])
        hs = mem.sb("hs", [P, HALVES, L])
        hC = mem.sb("hC", [P, 2, HALVES, L])
        e_sp, ln_sp = dA[:, 0], dA[:, 1]
        t_sp = hs
        yz = dBu[:, 0]

        psB = mem.ps("psB", [P, CH, 512])
        psC = mem.ps("psC", [P, CH, 512])
        psY = mem.ps("psY", [P, HALVES, CH, 512])
        flatB = psB[:].rearrange("p a b -> p (a b)")
        flatC = psC[:].rearrange("p a b -> p (a b)")

        names = ("own scan w_copied pool_own w_loaded w_cleared sel_made layer_free w_scaled w_turned w_ready a_exp hn hT hT_copied "
                 "xc_mm z_mm xc_silu z_silu dbl_mm parts dt8 dt_mm softplus u skip_mm B_mm B_copied C_mm "
                 "dA dBu hC y_mm yz out_mm nf_loaded zero_pad").split()
        s = {n: mem.sem(n) for n in names}
        PREP = HALVES * TAPS
        TURNS = PREP + 4 * HALVES
        RING = 2 * HALVES
        block = stack.enter_context(nc.Block())

        @block.sync
        def _(sp):
            for k, w in enumerate((nf_w, nf_b)):
                sp.dma_start(nfw[:, k, :], w.rearrange("(a c) -> a c", a=1).broadcast_to([P, C])).then_inc(s["nf_loaded"], 16)
            sp.wait_ge(s["w_cleared"], 1)
            with sp.Fori(0, LAYERS) as l:
                sp.wait_ge(s["layer_free"], l + 1)
                one = bass.ds(l, 1)
                loads = [
                    (w_in[:], in_w[one].rearrange("a (k p) c -> p (a k) c", p=P)),
                    (cw[:], conv_w[one].rearrange("a (h p) t -> p (a h) t", p=P)),
                    (cb[:], conv_b[one].rearrange("a (h p) -> p (a h)", p=P)),
                    (dtb[:], dtp_b[one].rearrange("a (h p) -> p (a h)", p=P)),
                    (dsk[:], D_skip[one].rearrange("a (h p) -> p (a h)", p=P)),
                    (alog[:], A_log[one].rearrange("a (h p) n -> p (a h) n", p=P)),
                    (lnw[:, 0:1], ln_w[one].rearrange("a c -> c a")),
                    (lnw[:, 1:2], ln_b[one].rearrange("a c -> c a")),
                    (ow_in[:], out_w[one].rearrange("a d e -> d (a e)")),
                    (dtp_in[:, :, 3 * BC:ROWS], dtp_w[one].rearrange("a (h p) r -> p (a h) r", p=P)),
                    (xp_in[3 * BC:ROWS, :], xp_w[one, 0:R].rearrange("a r e -> r (a e)")),
                ] + [(xp_in[BC * k:BC * k + BC, :], xp_w[one, R:R + BC].rearrange("a r e -> r (a e)")) for k in range(3)]
                for dst, src in loads:
                    with nc.allow_non_contiguous_dma(reason="a few hundred values per channel"):
                        sp.dma_start(dst, src).then_inc(s["w_loaded"], 16)
            assert len(loads) == 14

        LOADS = 14

        @block.gpsimd
        def _(pool):
            own = Tally(pool, s["pool_own"])
            pool.memset(dtp_in[:], 0.0).then_inc(s["w_cleared"], 1)
            pool.memset(hT[:, 0:TAPS - 1], 0.0).then_inc(s["zero_pad"], 1)
            own.step(pool.memset(sel[:], 0.0))
            for q in range(3):
                own.step(pool.affine_select(out=sel[:], in_=sel[:], compare_op=ALU.not_equal, fill=1.0,
                                            base=-BC * q, pattern=[[-1, BC], [0, P]], channel_multiplier=1))
            pool.sem_inc(s["sel_made"], 1)
            pool.sem_inc(s["dBu"], RING)
            with pool.Fori(0, LAYERS * BATCHES) as g:
                with pool.Fori(0, N // 2) as i:
                    for k in range(2):
                        pool.wait_ge(s["u"], g + 1)
                        m = g * N + i * 2 + k
                        pool.wait_ge(s["B_copied"], m + 2)
                        for h in range(HALVES):
                            pool.wait_ge(s["scan"], HALVES * m + h + 1)
                            pool.tensor_tensor(dBu[:, k, h, :], u[:, h, :], Bs[:, k, :],
                                               ALU.mult).then_inc(s["dBu"], 1)

        @block.scalar
        def _(act):
            act.sem_inc(s["B_copied"], 1)
            with act.Fori(0, LAYERS) as l:
                act.wait_ge(s["w_loaded"], 16 * LOADS * (l + 1))
                act.activation(aneg[:].rearrange("p h n -> p (h n)"), alog[:].rearrange("p h n -> p (h n)"),
                               ACT.Exp).then_inc(s["a_exp"], 1)
                act.wait_ge(s["w_ready"], l + 1)
                with act.Fori(0, BATCHES) as b:
                    g = l * BATCHES + b
                    act.wait_ge(s["xc_mm"], g + 1)
                    for h in range(HALVES):
                        last = act.activation(xc[:, h, :], psY[:, h].rearrange("p a b -> p (a b)"), ACT.Silu,
                                              bias=cb[:, h:h + 1])
                    last.then_inc(s["xc_silu"], 1)
                    act.wait_ge(s["z_mm"], g + 1)
                    act.activation(zs[:, 0, :], flatC, ACT.Silu)
                    act.activation(zs[:, 1, :], flatB, ACT.Silu).then_inc(s["z_silu"], 1)
                    act.wait_ge(s["dt_mm"], g + 1)
                    for h, ps in ((0, flatC), (1, flatB)):
                        act.activation(dt[:, h, :], ps, ACT.Relu, bias=dtb[:, h:h + 1])
                        act.activation(e_sp[:, h, :], ps, ACT.Abs, bias=dtb[:, h:h + 1]).then_inc(s["softplus"], 1)
                    act.wait_ge(s["softplus"], 4 * g + 2)
                    act.activation(e_sp, e_sp, ACT.Exp, scale=-1.0).then_inc(s["softplus"], 1)
                    act.wait_ge(s["softplus"], 4 * g + 3)
                    act.activation(ln_sp, e_sp, ACT.Ln, bias=1.0).then_inc(s["softplus"], 1)
                    act.wait_ge(s["u"], g + 1)
                    with act.Fori(0, N // 2) as i:
                        for k in range(2):
                            m = g * N + i * 2 + k
                            act.wait_ge(s["dBu"], HALVES * m + HALVES)
                            act.wait_ge(s["B_mm"], m + 1)
                            act.activation(Bs[:, k, :], flatB, ACT.Copy).then_inc(s["B_copied"], 1)
                            for h in range(HALVES):
                                act.wait_ge(s["scan"], HALVES * m + h + 1)
                                act.activation(dA[:, k, h, :], dt[:, h, :], ACT.Exp,
                                               scale=aneg[:, h, bass.ds(i * 2 + k, 1)]).then_inc(s["dA"], 1)

        @block.tensor
        def _(pe):
            pe.sem_inc(s["y_mm"], 2)
            pe.wait_ge(s["sel_made"], 1)
            pe.wait_ge(s["zero_pad"], 1)
            with pe.Fori(0, LAYERS) as l:
                pe.wait_ge(s["w_loaded"], 16 * LOADS * (l + 1))
                turns = 0

                def turn(in_, rows):
                    nonlocal turns
                    out = psY[:, (turns % 4) // 2, turns % 2, 0:P]
                    if turns >= 4:
                        pe.wait_ge(s["w_copied"], l * TURNS + turns - 3)
                    pe.transpose(out[0:rows, 0:in_.shape[0]], in_, ident[0:in_.shape[0], 0:in_.shape[0]]).then_inc(s["w_turned"], 1)
                    turns += 1
                for q in range(PREP):
                    pe.wait_ge(s["w_scaled"], l * PREP + q + 1)
                    turn(w_tap[:, q % 2, :], P)
                for h in range(HALVES):
                    turn(w_in[:, HALVES + h, :], P)
                for h in range(HALVES):
                    turn(xp_in[:, P * h:P * h + P], P)
                for h in range(HALVES):
                    turn(dtp_in[:, h, :], ROWS)
                for h in range(HALVES):
                    turn(ow_in[:, P * h:P * h + P], P)
                assert turns == TURNS
                with pe.Fori(0, BATCHES) as b:
                    g = l * BATCHES + b
                    pe.wait_ge(s["w_ready"], l + 1)
                    pe.wait_ge(s["hn"], g + 1)
                    for t in range(BT):
                        last = pe.transpose(psB[:, t // 4, P * (t % 4):P * (t % 4) + P], hn[:, t, :], ident[:])
                    last.then_inc(s["hT"], 1)
                    pe.wait_ge(s["hT_copied"], g + 1)
                    for h in range(HALVES):
                        for c in range(CH):
                            for k in range(TAPS):
                                last = pe.matmul(psY[:, h, c, :], wT[:, h * TAPS + k, :],
                                                 hT[:, 512 * c + k:512 * c + k + 512], start=(k == 0), stop=(k == TAPS - 1))
                    last.then_inc(s["xc_mm"], 1)
                    for h, ps in ((0, psC), (1, psB)):
                        for c in range(CH):
                            last = pe.matmul(ps[:, c, :], wT[:, PREP + h, :],
                                             hT[:, TAPS - 1 + 512 * c:TAPS - 1 + 512 * c + 512], start=True, stop=True)
                    last.then_inc(s["z_mm"], 1)
                    pe.wait_ge(s["xc_silu"], g + 1)
                    for c in range(CH):
                        for h in range(HALVES):
                            last = pe.matmul(psY[0:ROWS, 0, c, :], xpT[:, h, :], xc[:, h, 512 * c:512 * c + 512],
                                             start=(h == 0), stop=(h == HALVES - 1))
                    last.then_inc(s["dbl_mm"], 1)
                    pe.wait_ge(s["dt8"], g + 1)
                    pe.wait_ge(s["z_silu"], g + 1)
                    for h, ps in ((0, psC), (1, psB)):
                        for c in range(CH):
                            last = pe.matmul(ps[:, c, :], dtpT[3 * BC:ROWS, P * h:P * h + P],
                                             dt8[3 * BC:ROWS, 512 * c:512 * c + 512], start=True, stop=True)
                    last.then_inc(s["dt_mm"], 1)
                    pe.wait_ge(s["parts"], g + 1)
                    for h in range(HALVES):
                        for c in range(CH):
                            pe.matmul(psY[:, h, c, :], diag[:, h, :], xc[:, h, 512 * c:512 * c + 512],
                                      start=True, stop=True)
                    pe.wait_ge(s["u"], g + 1)

                    def spread(ps, row, sem):
                        for c in range(CH):
                            last = pe.matmul(ps[:, c, :], sel[:, bass.ds(row, 1), :],
                                             parts[:, 512 * c:512 * c + 512], start=True, stop=True)
                        last.then_inc(sem, 1)

                    def spread_B(n):
                        pe.wait_ge(s["B_copied"], g * N + n + 1)
                        spread(psB, n, s["B_mm"])

                    def step(n, k, ahead):
                        pe.wait_ge(s["hC"], HALVES * (g * N + n) + HALVES)
                        spread(psC, n + N, s["C_mm"])
                        if ahead:
                            spread_B(n + 2)
                        for h in range(HALVES):
                            pe.wait_ge(s["hC"], HALVES * (g * N + n) + HALVES + h + 1)
                            for c in range(CH):
                                last = pe.matmul(psY[:, h, c, :], ident[:], hC[:, k, h, 512 * c:512 * c + 512],
                                                 start=False, stop=True, skip_group_check=True)
                        last.then_inc(s["y_mm"], 1)

                    spread_B(0)
                    spread_B(1)
                    with pe.Fori(0, N // 2 - 1) as i:
                        for k in range(2):
                            step(i * 2 + k, k, True)
                    for k in range(2):
                        step(N - 2 + k, k, False)
                    pe.wait_ge(s["yz"], g + 1)
                    for t in range(BT):
                        for h in range(HALVES):
                            last = pe.matmul(psB[:, t // 4, P * (t % 4):P * (t % 4) + P], yz[:, h, P * t:P * t + P],
                                             owT[:, h, :], start=(h == 0), stop=(h == HALVES - 1))
                    last.then_inc(s["out_mm"], 1)

        @block.vector
        def _(v):
            own = Tally(v, s["own"])
            with own.loop(TILES, 1) as t:
                own.count(v.bn_stats(nb["bn"][:, bass.ds(t, 1), :], x_tok[:, bass.ds(t, 1), :]))
            norm_factors(v, own, nb, TILES)
            for t in range(TILES):
                own.count(v.tensor_scalar(r_tok[:, t, :], x_tok[:, t, :], nb["mean"][:, t:t + 1],
                                          nb["rstd"][:, t:t + 1], ALU.subtract, ALU.mult))
            own.wait()
            v.sem_inc(s["layer_free"], 1)
            v.sem_inc(s["scan"], RING)
            v.sem_inc(s["hC"], HALVES)
            PER_BATCH = BT + NORM_STEPS + 14
            with own.loop(LAYERS, HALVES + 1 + BATCHES * PER_BATCH) as l:
                v.wait_ge(s["w_loaded"], 16 * LOADS * (l + 1))
                turned = [wT[:, q, :] for q in range(PREP + HALVES)] + [xpT[:, h, :] for h in range(HALVES)] + \
                    [dtpT[3 * BC:ROWS, P * h:P * h + P] for h in range(HALVES)] + [owT[:, h, :] for h in range(HALVES)]

                def copy_turn(q):
                    dst = turned[q]
                    lo, n = (3 * BC, R) if PREP + 2 * HALVES <= q < PREP + 3 * HALVES else (0, P)
                    v.wait_ge(s["w_turned"], l * TURNS + q + 1)
                    v.tensor_copy(dst, psY[lo:lo + n, (q % 4) // 2, q % 2, 0:dst.shape[-1]]).then_inc(s["w_copied"], 1)

                for q in range(PREP):
                    h, k = q // TAPS, q % TAPS
                    if q >= 2:
                        v.wait_ge(s["w_turned"], l * TURNS + q - 1)
                    inst = v.tensor_scalar(w_tap[:, q % 2, :], w_in[:, h, :], cw[:, h, k:k + 1], None, ALU.mult)
                    inst.then_inc(s["w_scaled"], 1)
                    if q >= 2:
                        copy_turn(q - 2)
                for q in range(PREP - 2, TURNS):
                    copy_turn(q)
                for h in range(HALVES):
                    own.count(v.tensor_scalar(diag[:, h, :], ident[:], dsk[:, h:h + 1], None, ALU.mult))
                v.wait_ge(s["a_exp"], l + 1)
                own.count(v.tensor_scalar(aneg[:].rearrange("p h n -> p (h n)"), aneg[:].rearrange("p h n -> p (h n)"),
                                          -1.0, None, ALU.mult))
                own.wait()
                v.wait_ge(s["w_copied"], TURNS * (l + 1))
                v.sem_inc(s["w_ready"], 1)
                with own.loop(BATCHES, PER_BATCH) as b:
                    g = l * BATCHES + b
                    for t in range(BT):
                        own.count(v.bn_stats(nb["bn"][:, t, :], r_tok[:, bass.ds(b * BT + t, 1), :]))
                    norm_factors(v, own, nb, BT)
                    for t in range(BT):
                        last = v.tensor_scalar(hn[:, t, :], r_tok[:, bass.ds(b * BT + t, 1), :], nb["mean"][:, t:t + 1],
                                               nb["rstd"][:, t:t + 1], ALU.subtract, ALU.mult)
                    last.then_inc(s["hn"], 1)
                    v.wait_ge(s["hT"], g + 1)
                    v.tensor_scalar(hT[:, TAPS - 1:], flatB, lnw[:, 0:1], lnw[:, 1:2], ALU.mult,
                                    ALU.add).then_inc(s["hT_copied"], 1)
                    v.wait_ge(s["dbl_mm"], g + 1)
                    dbl = psY[:, 0].rearrange("p a b -> p (a b)")
                    v.tensor_copy(dt8[3 * BC:ROWS, :], dbl[3 * BC:ROWS, :]).then_inc(s["dt8"], 1)
                    J = 3 * BC
                    own.step(v.tensor_copy(parts[:], dbl[0:J, :]))
                    own.step(v.tensor_tensor(rest[:], dbl[0:J, :], parts[:], ALU.subtract))
                    own.step(v.tensor_copy(mid[:], rest[:]))
                    own.step(v.tensor_tensor(rest[:], rest[:], mid[:], ALU.subtract))
                    v.tensor_copy(parts[BC:2 * BC, :], mid[BC:2 * BC, :])
                    v.tensor_copy(parts[2 * BC:J, :], rest[2 * BC:J, :]).then_inc(s["parts"], 1)
                    v.wait_ge(s["softplus"], 4 * g + 4)
                    own.step(v.tensor_scalar(t_sp[:], e_sp, LOG1P[0], LOG1P[1], ALU.mult, ALU.add))
                    own.step(v.tensor_tensor(t_sp[:], t_sp[:], e_sp, ALU.mult))
                    for c in LOG1P[2:]:
                        own.step(v.scalar_tensor_tensor(out=t_sp[:], in0=t_sp[:], scalar=c, in1=e_sp, op0=ALU.add,
                                                        op1=ALU.mult))
                    own.step(v.tensor_tensor(ln_sp, ln_sp, t_sp[:], ALU.subtract))
                    own.step(v.scalar_tensor_tensor(out=ln_sp, in0=e_sp, scalar=0.125, in1=ln_sp, op0=ALU.is_gt,
                                                    op1=ALU.mult))
                    own.step(v.tensor_tensor(t_sp[:], t_sp[:], ln_sp, ALU.add))
                    own.step(v.tensor_tensor(dt[:], dt[:], t_sp[:], ALU.add))
                    v.tensor_tensor(u[:], dt[:], xc[:], ALU.mult).then_inc(s["u"], 1)
                    with v.Fori(0, N // 2) as i:
                        for k in range(2):
                            m = g * N + i * 2 + k
                            for h in range(HALVES):
                                v.wait_ge(s["dA"], HALVES * m + h + 1)
                                v.wait_ge(s["dBu"], HALVES * m + h + 1 + RING)
                                v.wait_ge(s["hC"], HALVES * m + h + 1)
                                v.tensor_tensor_scan(hs[:, h, :], dA[:, k, h, :], dBu[:, k, h, :], 0.0,
                                                     ALU.mult, ALU.add).then_inc(s["scan"], 1)
                            v.wait_ge(s["C_mm"], m + 1)
                            v.wait_ge(s["y_mm"], m + 1)
                            for h in range(HALVES):
                                v.wait_ge(s["scan"], HALVES * m + h + 1 + RING)
                                v.tensor_tensor(hC[:, k, h, :], hs[:, h, :], flatC, ALU.mult).then_inc(s["hC"], 1)
                    v.wait_ge(s["y_mm"], (g + 1) * N + 2)
                    for h in range(HALVES):
                        last = v.tensor_tensor(yz[:, h, :], zs[:, h, :], psY[:, h].rearrange("p a b -> p (a b)"), ALU.mult)
                    last.then_inc(s["yz"], 1)
                    v.wait_ge(s["out_mm"], g + 1)
                    tok = r_tok[:, bass.ds(b * BT, BT), :]
                    own.step(v.tensor_tensor(tok, tok, flatB.rearrange("p (t c) -> p t c", c=C), ALU.add))
                v.sem_inc(s["layer_free"], 1)
            with own.loop(TILES, 1) as t:
                own.count(v.bn_stats(nb["bn"][:, bass.ds(t, 1), :], r_tok[:, bass.ds(t, 1), :]))
            norm_factors(v, own, nb, TILES)
            for t in range(TILES):
                own.count(v.tensor_scalar(r_tok[:, t, :], r_tok[:, t, :], nb["mean"][:, t:t + 1],
                                          nb["rstd"][:, t:t + 1], ALU.subtract, ALU.mult))
            own.wait()
            v.wait_ge(s["nf_loaded"], 32)
            rows = [nfw[:, k:k + 1, :].broadcast_to([P, TILES, C]) for k in range(2)]
            own.step(v.tensor_tensor(r_tok[:], r_tok[:], rows[0], ALU.mult))
            own.step(v.tensor_tensor(r_tok[:], r_tok[:], rows[1], ALU.add))
            own.step(v.tensor_tensor(x_tok[:], x_tok[:], r_tok[:], ALU.add))


def lora_weight_stage(nc, ident, wT, b_row, ones_row, W, b, lora_down, lora_up, down_aux, up_aux):
    RANK, DD = lora_down.shape
    UD = lora_up.shape[0]
    with ExitStack() as stack:
        mem = Stage(nc, stack, "lora")
        w_in = mem.sb("w_in", [P, C])
        ld = mem.sb("ld", [RANK, DD])
        lu = mem.sb("lu", [UD, RANK])
        da = mem.sb("da", [DD, C])
        ua = mem.sb("ua", [P, UD])
        ldT = mem.sb("ldT", [DD, RANK])
        luT = mem.sb("luT", [RANK, UD])
        uaT = mem.sb("uaT", [UD, P])
        m1 = mem.sb("m1", [RANK, C])
        m2 = mem.sb("m2", [UD, C])
        ps = mem.ps("ps", [P, 6, 512])
        loaded, ones_set, done, copied = (mem.sem(n) for n in ("loaded", "ones_set", "mm", "copied"))
        block = stack.enter_context(nc.Block())

        @block.sync
        def _(sp):
            for dst, src in ((w_in, W), (ld, lora_down), (lu, lora_up), (da, down_aux), (ua, up_aux),
                             (b_row, b.rearrange("(a c) -> a c", a=1))):
                sp.dma_start(dst[:], src).then_inc(loaded, 16)

        @block.gpsimd
        def _(pool):
            pool.memset(ones_row[:], 1.0).then_inc(ones_set, 1)
            pool.wait_ge(ones_set, 1)

        @block.tensor
        def _(pe):
            pe.wait_ge(loaded, 96)
            pe.transpose(ps[0:DD, 0, 0:RANK], ld[:], ident[0:RANK, 0:RANK]).then_inc(done, 1)
            pe.transpose(ps[0:RANK, 1, 0:UD], lu[:], ident[0:UD, 0:UD]).then_inc(done, 1)
            pe.transpose(ps[0:UD, 2, 0:P], ua[:], ident[:]).then_inc(done, 1)
            pe.wait_ge(copied, 1)
            pe.matmul(ps[0:RANK, 3, 0:C], ldT[:], da[:], start=True, stop=True).then_inc(done, 1)
            pe.wait_ge(copied, 4)
            pe.matmul(ps[0:UD, 4, 0:C], luT[:], m1[:], start=True, stop=True).then_inc(done, 1)
            pe.wait_ge(copied, 5)
            pe.matmul(ps[:, 5, 0:C], w_in[:], ident[:], start=True, stop=False)
            pe.matmul(ps[:, 5, 0:C], m2[:], uaT[:], start=False, stop=True).then_inc(done, 1)

        @block.vector
        def _(v):
            for n, (dst, src) in enumerate(((ldT, ps[0:DD, 0, 0:RANK]), (luT, ps[0:RANK, 1, 0:UD]),
                                            (uaT, ps[0:UD, 2, 0:P]), (m1, ps[0:RANK, 3, 0:C]),
                                            (m2, ps[0:UD, 4, 0:C]), (wT, ps[:, 5, 0:C]))):
                v.wait_ge(done, n + 1)
                v.tensor_copy(dst[:], src).then_inc(copied, 1)
            v.wait_ge(copied, 6)


def linear_stage(nc, stage, x_tok, ident, wT, b_row, ones_row):
    TILES = x_tok.shape[1]
    GROUPS = TILES // 4
    with ExitStack() as stack:
        mem = Stage(nc, stack, stage)
        nb = norm_buffers(mem, TILES)
        xn = mem.sb("xn", [P, 2, 4, C])
        xnT = mem.sb("xnT", [P, 2, 512])
        ps_T = mem.ps("ps_T", [P, 2, 512])
        ps_y = mem.ps("ps_y", [P, 2, 512])
        s_own, s_xn, s_T, s_Tc, s_y, s_out = (mem.sem(n) for n in ("own", "xn", "turned", "copied", "y", "added"))
        block = stack.enter_context(nc.Block())

        @block.vector
        def _(v):
            own = Tally(v, s_own)
            with own.loop(TILES, 1) as t:
                own.count(v.bn_stats(nb["bn"][:, bass.ds(t, 1), :], x_tok[:, bass.ds(t, 1), :]))
            norm_factors(v, own, nb, TILES)

            def norm(n, k):
                for q in range(4):
                    t = n * 4 + q
                    last = v.tensor_scalar(xn[:, k, q, :], x_tok[:, bass.ds(t, 1), :], nb["mean"][:, bass.ds(t, 1)],
                                           nb["rstd"][:, bass.ds(t, 1)], ALU.subtract, ALU.mult)
                last.then_inc(s_xn, 1)

            def add(n, k):
                v.wait_ge(s_y, n + 1)
                tok = x_tok[:, bass.ds(n * 4, 4), :]
                v.scalar_tensor_tensor(out=tok, in0=ps_y[:, k].rearrange("p (q c) -> p q c", c=C), scalar=0.5,
                                       in1=tok, op0=ALU.mult, op1=ALU.add).then_inc(s_out, 1)

            norm(0, 0)
            norm(1, 1)
            with v.Fori(0, (GROUPS - 2) // 2) as i:
                for k in range(2):
                    add(2 * i + k, k)
                    norm(2 * i + k + 2, k)
            for k in range(2):
                add(GROUPS - 2 + k, k)
            v.wait_ge(s_out, GROUPS)

        @block.scalar
        def _(act):
            with act.Fori(0, GROUPS // 2) as i:
                for k in range(2):
                    act.wait_ge(s_T, 2 * i + k + 1)
                    act.activation(xnT[:, k, :], ps_T[:, k, :], ACT.Copy).then_inc(s_Tc, 1)

        @block.tensor
        def _(pe):
            def turn(n, k):
                pe.wait_ge(s_xn, n + 1)
                for q in range(4):
                    last = pe.transpose(ps_T[:, k, P * q:P * q + P], xn[:, k, q, :], ident[:])
                last.then_inc(s_T, 1)

            def product(n, k, again):
                pe.wait_ge(s_Tc, n + 1)
                if again:
                    pe.wait_ge(s_out, n - 1)
                for q in range(4):
                    o = ps_y[:, k, P * q:P * q + P]
                    pe.matmul(o, xnT[:, k, P * q:P * q + P], wT[:], start=True, stop=False)
                    last = pe.matmul(o, ones_row[:], b_row[:], start=False, stop=True)
                last.then_inc(s_y, 1)

            turn(0, 0)
            turn(1, 1)
            product(0, 0, False)
            turn(2, 0)
            product(1, 1, False)
            with pe.Fori(0, (GROUPS - 4) // 2) as i:
                for k in range(2):
                    turn(2 * i + k + 3, 1 - k)
                    product(2 * i + k + 2, k, True)
            turn(GROUPS - 1, 1)
            product(GROUPS - 2, 0, True)
            product(GROUPS - 1, 1, True)


Q_PARTS = (0, 0, 1, 1, 0, 2)
K_PARTS = (0, 1, 0, 1, 2, 0)
MAX_PARTS = 3


def attention_stage(nc, x_tok, ident, ones_row, w_qkv, b_qkv, w_proj, b_proj, q_dram, k_dram):
    TILES = x_tok.shape[1]
    BT = 8
    L = BT * P
    BATCHES = TILES // BT
    D = 8
    HEADS = C // D
    PAIRS = HEADS // 2
    SCALE = D ** -0.5
    QR = len(Q_PARTS) * D
    KR = QR + MAX_PARTS
    MAX_BANKS = 3
    VW = D + 1
    with ExitStack() as stack:
        mem = Stage(nc, stack, "attn")
        v_aug = mem.sb("v_aug", [P, BATCHES, BT, HEADS, VW])
        wqkv = mem.sb("wqkv", [P, 3, C])
        wp = mem.sb("wp", [P, C])
        bqk = mem.sb("bqk", [P, 2])
        bv = mem.sb("bv", [1, C])
        bp = mem.sb("bp", [1, C])

        with ExitStack() as project_stack:
            pm = Stage(nc, project_stack, "qkv")
            nb = norm_buffers(pm, TILES)
            xn = pm.sb("xn", [P, BT, C])
            xnT = pm.sb("xnT", [P, L])
            full = pm.sb("full", [P, 2, L])
            part = pm.sb("part", [P, 2, 3, L], BF16)
            ps_T = pm.ps("ps_T", [P, L])
            ps_q = pm.ps("ps_q", [P, 2, L])
            ps_v = pm.ps("ps_v", [P, BT, C])
            names = "own xn turned copied q_mm v_mm biased split v_copied loaded v_one".split()
            s = {n: pm.sem(n) for n in names}
            stored = [pm.sem(n) for n in ("q_stored", "k_stored")]
            STORES = 16 * len(Q_PARTS)
            block = project_stack.enter_context(nc.Block())

            @block.sync
            def _(sp):
                with nc.allow_non_contiguous_dma(reason="one value per channel"):
                    for dst, src in ((wqkv[:], w_qkv.rearrange("c (k e) -> c k e", k=3)), (wp[:], w_proj),
                                     (bqk[:], b_qkv[0:2 * C].rearrange("(k e) -> e k", k=2)),
                                     (bv[:], b_qkv[2 * C:3 * C].rearrange("(a e) -> a e", a=1)),
                                     (bp[:], b_proj.rearrange("(a e) -> a e", a=1))):
                        sp.dma_start(dst, src).then_inc(s["loaded"], 16)
                for w in range(2):
                    sp.sem_inc(stored[w], STORES)
                with sp.Fori(0, BATCHES) as b:
                    for w, dram, parts_of in ((0, q_dram, Q_PARTS), (1, k_dram, K_PARTS)):
                        sp.wait_ge(s["split"], 2 * b + w + 2)
                        for c, p in enumerate(parts_of):
                            sp.dma_start(dram[bass.ds(b, 1), :, D * c:D * c + D, :].rearrange("a h d t -> (a h) d t"),
                                         part[:, w, p, :]).then_inc(stored[w], 16)
                for w in range(2):
                    sp.wait_ge(stored[w], STORES * (BATCHES + 1))

            @block.gpsimd
            def _(pool):
                pool.memset(v_aug[:, :, :, :, D:VW], 1.0).then_inc(s["v_one"], 1)
                pool.wait_ge(s["v_one"], 1)

            @block.vector
            def _(v):
                own = Tally(v, s["own"])
                with own.loop(TILES, 1) as t:
                    own.count(v.bn_stats(nb["bn"][:, bass.ds(t, 1), :], x_tok[:, bass.ds(t, 1), :]))
                norm_factors(v, own, nb, TILES)
                v.sem_inc(s["split"], 1)
                with own.loop(BATCHES, 6) as b:
                    v.wait_ge(s["split"], 2 * b + 1)
                    for q in range(BT):
                        t = b * BT + q
                        last = v.tensor_scalar(xn[:, q, :], x_tok[:, bass.ds(t, 1), :], nb["mean"][:, bass.ds(t, 1)],
                                               nb["rstd"][:, bass.ds(t, 1)], ALU.subtract, ALU.mult)
                    last.then_inc(s["xn"], 1)
                    v.wait_ge(s["v_mm"], b + 1)
                    v.tensor_copy(v_aug[:, bass.ds(b, 1), :, :, 0:D].rearrange("p a t h d -> p (a t) h d"),
                                  ps_v[:].rearrange("p t (h d) -> p t h d", d=D)).then_inc(s["v_copied"], 1)
                    for w in range(2):
                        v.wait_ge(s["biased"], 2 * b + w + 1)
                        v.wait_ge(stored[w], STORES * (b + 1))
                        own.step(v.tensor_copy(part[:, w, 0, :], full[:, w, :]))
                        own.step(v.tensor_tensor(full[:, w, :], full[:, w, :], part[:, w, 0, :], ALU.subtract))
                        own.step(v.tensor_copy(part[:, w, 1, :], full[:, w, :]))
                        v.tensor_tensor(part[:, w, 2, :], full[:, w, :], part[:, w, 1, :],
                                        ALU.subtract).then_inc(s["split"], 1)
                v.wait_ge(s["v_copied"], BATCHES)

            @block.scalar
            def _(act):
                act.wait_ge(s["loaded"], 80)
                with act.Fori(0, BATCHES) as b:
                    act.wait_ge(s["turned"], b + 1)
                    act.activation(xnT[:], ps_T[:], ACT.Copy).then_inc(s["copied"], 1)
                    for w in range(2):
                        act.wait_ge(s["q_mm"], 2 * b + w + 1)
                        act.activation(full[:, w, :], ps_q[:, w, :], ACT.Identity,
                                       bias=bqk[:, w:w + 1]).then_inc(s["biased"], 1)

            @block.tensor
            def _(pe):
                pe.wait_ge(s["loaded"], 80)
                with pe.Fori(0, BATCHES) as b:
                    pe.wait_ge(s["xn"], b + 1)
                    for q in range(BT):
                        last = pe.transpose(ps_T[:, P * q:P * q + P], xn[:, q, :], ident[:])
                    last.then_inc(s["turned"], 1)
                    pe.wait_ge(s["copied"], b + 1)
                    for q in range(BT):
                        pe.matmul(ps_v[:, q, :], xnT[:, P * q:P * q + P], wqkv[:, 2, :], start=True, stop=False)
                        last = pe.matmul(ps_v[:, q, :], ones_row[:], bv[:], start=False, stop=True)
                    last.then_inc(s["v_mm"], 1)
                    for w in range(2):
                        for c in range(L // 512):
                            last = pe.matmul(ps_q[:, w, 512 * c:512 * c + 512], wqkv[:, w, :],
                                             xnT[:, 512 * c:512 * c + 512], start=True, stop=True)
                        last.then_inc(s["q_mm"], 1)

        with ExitStack() as main_stack:
            mm = Stage(nc, main_stack, "heads")
            q1 = mm.sb("q1", [P, 2, 2, L], BF16)
            k1 = mm.sb("k1", [P, 2, L], BF16)
            q2 = mm.sb("q2", [P, 2, L], BF16)
            k2 = mm.sb("k2", [P, 2, 2, L], BF16)
            top = mm.sb("top", [P, 2, 2, BT, 2])
            neg = mm.sb("neg", [P, 2, BT])
            neg_row = mm.sb("neg_row", [2 * BT, P])
            ones = mm.sb("ones", [2 * BT, P])
            neg_part = mm.sb("neg_part", [2 * BT, MAX_PARTS, P], BF16)
            pT = mm.sb("pT", [P, 2, 2, L])
            v_pair = mm.sb("v_pair", [P, BT, 2, 32])
            oT = mm.sb("oT", [P, 512])
            recip = mm.sb("recip", [P, 4, 4])
            o_tok = mm.sb("o_tok", [P, BT, C])
            oTa = mm.sb("oTa", [P, L])
            ps_s = mm.ps("ps_s", [P, 2, L])
            ps_m = mm.ps("ps_m", [P, MAX_BANKS, 512])
            ps_o = mm.ps("ps_o", [P, 512])
            ps_t = ps_o[:].rearrange("p (q a d) -> p q a d", q=4, a=4)
            names = ("own v_zero v_pair s_mm prob pv_step oT o_turned o_norm m_mm top neg neg_turned neg_copied "
                     "neg_work neg_split neg_stored a_turned a_copied out_mm added rows_set").split()
            s = {n: mm.sem(n) for n in names}
            first = [mm.sem(f"first{k}_loaded") for k in range(2)]
            second = [mm.sem(f"second{k}_loaded") for k in range(2)]
            block = main_stack.enter_context(nc.Block())
            MAXES = 4 * BT
            UNITS = 2 * BT
            LEAD = 2
            NEG_BANK = 2
            UNCOVERED = (0, 8, 16, 24, 31)
            NEG_STORES = 16 * 2

            def each_pair(loop, step, batch_end=None):
                def pairs(b, rounds):
                    with loop(rounds, 2) as i:
                        for k in range(2):
                            step(b * PAIRS + i * 2 + k, b, i * 2 + k, k, True)

                with loop(BATCHES - 1, PAIRS) as b:
                    pairs(b, PAIRS // 2)
                    if batch_end:
                        batch_end(b)
                b = BATCHES - 1
                pairs(b, (PAIRS - LEAD) // 2)
                for k in range(2):
                    pair = PAIRS - LEAD + k
                    step(b * PAIRS + pair, b, pair, k, False)
                if batch_end:
                    batch_end(b)

            @block.sync
            def _(sp):
                def rows(dram, g, n):
                    of_pair = dram.rearrange("b h r t -> (b h) r t")[bass.ds(g * 2, 2), 0:n, :]
                    return [of_pair[j] for j in range(2)]

                def load_first(g, k):
                    q_rows, k_rows = rows(q_dram, g, QR), rows(k_dram, g, QR)
                    sp.wait_ge(s["m_mm"], MAXES * (g + 1))
                    for j in range(2):
                        sp.dma_start(q1[64 * j:64 * j + QR, k, j, :], q_rows[j]).then_inc(first[k], 16)
                        sp.dma_start(k1[64 * j:64 * j + QR, k, :], k_rows[j]).then_inc(first[k], 16)

                def step(g, b, pair, k, with_first):
                    if with_first:
                        load_first(g + LEAD, k)

                    def head_rows(dram, j, n):
                        return dram[bass.ds(b, 1), bass.ds(pair * 2 + j, 1), 0:n, :].rearrange("b h r t -> (b h r) t")
                    sp.wait_ge(s["s_mm"], UNITS * (g + 1))
                    sp.wait_ge(s["neg_split"], g + 1)
                    for j in range(2):
                        sp.dma_start(head_rows(q_dram, j, KR)[QR:KR, :].rearrange("n (t c) -> t n c", c=P),
                                     neg_part[BT * j:BT * j + BT]).then_inc(s["neg_stored"], 16)
                    sp.wait_ge(s["neg_stored"], NEG_STORES * (g + 2))
                    for j in range(2):
                        sp.dma_start(k2[64 * j:64 * j + QR, k, j, :], head_rows(k_dram, j, QR)).then_inc(second[k], 16)
                    for j in range(2):
                        sp.dma_start(q2[64 * j:64 * j + KR, k, :], head_rows(q_dram, j, KR)).then_inc(second[k], 16)

                sp.wait_ge(s["rows_set"], 6)
                for k in range(LEAD):
                    load_first(k, k)
                each_pair(lambda n, pairs: sp.Fori(0, n), step)

            @block.gpsimd
            def _(pool):
                for n, rows in enumerate((q1, k1, q2, k2)):
                    pool.memset(rows[:], 0.0).then_inc(s["rows_set"], 1)
                    pool.wait_ge(s["rows_set"], n + 1)
                for j in range(2):
                    pool.memset(k2[64 * j + 32:64 * j + 64, :, j, :], 1.0).then_inc(s["rows_set"], 1)
                    pool.wait_ge(s["rows_set"], 5 + j)
                pool.memset(v_pair[:], 0.0).then_inc(s["v_zero"], 1)
                pool.wait_ge(s["v_zero"], 1)
                pool.memset(ones[:], 1.0).then_inc(s["v_zero"], 1)
                pool.wait_ge(s["v_zero"], 2)

                def split_neg(g):
                    pool.wait_ge(s["neg_stored"], NEG_STORES * (g + 1))
                    pool.wait_ge(s["neg_copied"], g + 1)
                    work = s["neg_work"]
                    pool.tensor_tensor(neg_part[:, 0, :], neg_row[:], ones[:], ALU.mult).then_inc(work, 1)
                    pool.wait_ge(work, 3 * g + 1)
                    pool.tensor_tensor(neg_row[:], neg_row[:], neg_part[:, 0, :], ALU.subtract).then_inc(work, 1)
                    pool.wait_ge(work, 3 * g + 2)
                    pool.tensor_tensor(neg_part[:, 1, :], neg_row[:], ones[:], ALU.mult).then_inc(work, 1)
                    pool.wait_ge(work, 3 * g + 3)
                    pool.tensor_tensor(neg_part[:, 2, :], neg_row[:], neg_part[:, 1, :],
                                       ALU.subtract).then_inc(s["neg_split"], 1)

                def step(g, b, pair, k, with_first):
                    pool.wait_ge(s["pv_step"], BT * g + 2)
                    pool.tensor_copy(v_pair[:, :, :, 0:VW],
                                     v_aug[:, bass.ds(b, 1), :, bass.ds(pair * 2, 2), :]
                                     .rearrange("p a t h d -> p (a t) h d")).then_inc(s["v_pair"], 1)
                    if with_first or k == 0:
                        split_neg(g + 1)

                pool.sem_inc(s["neg_stored"], NEG_STORES)
                split_neg(0)
                each_pair(lambda n, pairs: pool.Fori(0, n), step)

            @block.scalar
            def _(act):
                def step(g, b, pair, k, with_first):
                    for t in range(BT):
                        for j in range(2):
                            act.wait_ge(s["s_mm"], UNITS * (g + 2) + 2 * t + j + 1)
                            act.wait_ge(s["pv_step"], BT * g + t + 1)
                            act.activation(pT[:, t % 2, j, :], ps_s[:, j, :], ACT.Exp, scale=SCALE).then_inc(s["prob"], 1)
                    act.wait_ge(s["pv_step"], BT * (g + 1) + 2)
                    act.wait_ge(s["o_turned"], g + 1)
                    act.activation(oT[:], ps_o[:], ACT.Copy).then_inc(s["oT"], 1)

                def out(b):
                    act.wait_ge(s["a_turned"], b + 1)
                    act.activation(oTa[:], ps_s[:, 0, :], ACT.Copy).then_inc(s["a_copied"], 1)
                each_pair(lambda n, pairs: act.Fori(0, n), step, out)

            @block.tensor
            def _(pe):
                pe.sem_inc(s["m_mm"], 2 * MAXES)
                pe.sem_inc(s["s_mm"], 2 * UNITS)
                pe.sem_inc(s["pv_step"], 2)

                def max_unit(g, k, n, turned):
                    q, j, c = n // 4, (n // 2) % 2, n % 2
                    pe.wait_ge(s["top"], MAXES * g + (n if n >= MAX_BANKS else min(n + 1, 2)))
                    if n == NEG_BANK and turned:
                        pe.wait_ge(s["neg_copied"], g)
                    pe.matmul(ps_m[:, n % MAX_BANKS, :], q1[:, k, j, P * q:P * q + P], k1[:, k, 512 * c:512 * c + 512],
                              start=True, stop=True).then_inc(s["m_mm"], 1)

                def turn_neg(g):
                    pe.wait_ge(s["neg"], g + 1)
                    pe.transpose(ps_m[0:2 * BT, NEG_BANK, 0:P], neg[:].rearrange("p j t -> p (j t)"),
                                 ident[:]).then_inc(s["neg_turned"], 1)

                def score(g, k, t, j, c):
                    if c == 0:
                        pe.wait_ge(s["prob"], UNITS * g + 2 * t + j + 1)
                    product = pe.matmul(ps_s[:, j, 512 * c:512 * c + 512], k2[:, k, j, P * t:P * t + P],
                                        q2[:, k, 512 * c:512 * c + 512], start=True, stop=True)
                    if c == L // 512 - 1:
                        product.then_inc(s["s_mm"], 1)

                def values(g, t):
                    pe.wait_ge(s["prob"], UNITS * g + 2 * t + 2 + 2)
                    if t == 0:
                        pe.wait_ge(s["v_pair"], g + 1)
                        pe.wait_ge(s["o_norm"], g + 1)
                    for j in range(2):
                        for c in range(2):
                            o = 32 * (2 * j + c)
                            last = pe.matmul(ps_o[o:o + 32, :], v_pair[:, t, j, :], pT[:, t % 2, j, 512 * c:512 * c + 512],
                                             start=(t == 0), stop=(t == BT - 1))
                    last.then_inc(s["pv_step"], 1)

                def step(g, b, pair, k, with_first):
                    units = iter(range(MAXES))

                    def cover(product=None):
                        if with_first and product not in UNCOVERED:
                            max_unit(g + LEAD, k, next(units), True)
                    pe.wait_ge(second[k], 32 * (g - k + 2))
                    if with_first:
                        pe.wait_ge(first[k], 32 * (g - k + LEAD + 2))
                    for t in range(BT):
                        for j in range(2):
                            score(g, k, t, j, 0)
                            cover(4 * t + 2 * j)
                            if j == 0 and t == 0 and (with_first or k == 0):
                                turn_neg(g + 1)
                            score(g, k, t, j, 1)
                            cover(4 * t + 2 * j + 1)
                            if j == 1 and t:
                                values(g, t - 1)
                    cover()
                    cover()
                    values(g, BT - 1)
                    for _ in UNCOVERED[2:]:
                        cover()
                    pe.wait_ge(s["oT"], g + 1)
                    for q in range(4):
                        last = pe.transpose(ps_o[:, P * q:P * q + P], oT[:, P * q:P * q + P], ident[:])
                    last.then_inc(s["o_turned"], 1)

                def out(b):
                    pe.wait_ge(s["o_norm"], (b + 1) * PAIRS + 1)
                    for q in range(BT):
                        last = pe.transpose(ps_s[:, 0, P * q:P * q + P], o_tok[:, q, :], ident[:])
                    last.then_inc(s["a_turned"], 1)
                    pe.wait_ge(s["a_copied"], b + 1)
                    for q in range(BT):
                        o = ps_s[:, 1, P * q:P * q + P]
                        pe.matmul(o, oTa[:, P * q:P * q + P], wp[:], start=True, stop=False)
                        last = pe.matmul(o, ones_row[:], bp[:], start=False, stop=True)
                    last.then_inc(s["out_mm"], 1)
                    pe.wait_ge(s["added"], b + 1)

                for k in range(LEAD):
                    pe.wait_ge(first[k], 64)
                    if k:
                        turn_neg(k - 1)
                    for n in range(MAXES):
                        max_unit(k, k, n, k > 0)
                each_pair(lambda n, pairs: pe.Fori(0, n), step, out)

            @block.vector
            def _(v):
                own = Tally(v, s["own"])
                v.sem_inc(s["top"], 2)
                v.sem_inc(s["prob"], 2)
                v.sem_inc(s["o_norm"], 1)
                v.sem_inc(s["o_turned"], 1)

                def negate(g, k):
                    v.wait_ge(s["top"], MAXES * (g + 1) + 2)
                    own.step(v.tensor_tensor(neg[:], top[:, k, :, :, 0], top[:, k, :, :, 1], ALU.max))
                    v.tensor_scalar(neg[:], neg[:], -1.0, None, ALU.mult).then_inc(s["neg"], 1)

                def copy_neg(g, again):
                    v.wait_ge(s["neg_turned"], g + 1)
                    if again:
                        v.wait_ge(s["neg_split"], g)
                    v.tensor_copy(neg_row[:], ps_m[0:2 * BT, NEG_BANK, 0:P]).then_inc(s["neg_copied"], 1)

                def first_pass(g, k, turn, again):
                    if turn:
                        copy_neg(g - 1, again)
                    for n in range(MAXES):
                        q, j, c = n // 4, (n // 2) % 2, n % 2
                        v.wait_ge(s["m_mm"], MAXES * (g + 2) + n + 1)
                        v.tensor_reduce(top[:, k, j, q, c:c + 1], ps_m[:, n % MAX_BANKS, :], AX.X,
                                        ALU.max).then_inc(s["top"], 1)
                    negate(g, k)

                def step(g, b, pair, k, with_first):
                    if with_first:
                        first_pass(g + LEAD, k, True, True)
                    elif k == 0:
                        copy_neg(g + 1, True)
                    v.wait_ge(s["o_turned"], g + 2)
                    own.step(v.reciprocal(recip[:], ps_t[:, :, :, D]))
                    for j in range(2):
                        for c in range(2):
                            last = v.tensor_tensor(
                                o_tok[:, 4 * c:4 * c + 4, bass.ds(pair * 2 * D + j * D, D)],
                                ps_t[:, :, 2 * j + c, 0:D],
                                recip[:, :, 2 * j + c:2 * j + c + 1].broadcast_to([P, 4, D]), ALU.mult)
                    last.then_inc(s["o_norm"], 1)

                def add(b):
                    v.wait_ge(s["out_mm"], b + 1)
                    tok = x_tok[:, bass.ds(b * BT, BT), :]
                    v.tensor_tensor(tok, tok, ps_s[:, 1, :].rearrange("p (t c) -> p t c", c=C),
                                    ALU.add).then_inc(s["added"], 1)

                for k in range(LEAD):
                    first_pass(k, k, k > 0, False)
                each_pair(lambda n, pairs: own.loop(n, 2 * pairs), step, add)
                v.wait_ge(s["added"], BATCHES)


def build_program(nc, x, ln_w, ln_b, in_w, conv_w, conv_b, xp_w, dtp_w, dtp_b, A_log, D_skip, out_w, nf_w, nf_b,
                  Wr, br, W1, W2, w_qkv, b_qkv, w_proj, b_proj, W, b, lora_down, lora_up, down_aux, up_aux, out):
    B, L, _ = x.shape
    TILES = B * L // P
    E = Wr.shape[1]
    HEADS, D = 16, C // 16
    with ExitStack() as stack:
        x_tok = stack.enter_context(nc.sbuf_tensor("x_tok", [P, TILES, C], F32))
        ident = stack.enter_context(nc.sbuf_tensor("ident", [P, P], F32))
        tri = stack.enter_context(nc.sbuf_tensor("tri", [P, P], BF16))
        ones_bf = stack.enter_context(nc.sbuf_tensor("ones_bf", [P, P], BF16))
        wT = stack.enter_context(nc.sbuf_tensor("wT", [P, C], F32))
        b_row = stack.enter_context(nc.sbuf_tensor("b_row", [1, C], F32))
        ones_row = stack.enter_context(nc.sbuf_tensor("ones_row", [1, C], F32))
        sorted_x = nc.dram_tensor("sorted_x", [(TILES + E) * P, C], F32, kind="Internal").ap()
        sorted_y = nc.dram_tensor("sorted_y", [(TILES + E) * P, C], F32, kind="Internal").ap()
        q_rows = nc.dram_tensor("q_rows", [B, HEADS, len(Q_PARTS) * D + MAX_PARTS, L], BF16, kind="Internal").ap()
        k_rows = nc.dram_tensor("k_rows", [B, HEADS, len(K_PARTS) * D, L], BF16, kind="Internal").ap()
        tokens = "b (t p) c -> p (b t) c"
        load_stage(nc, x.rearrange(tokens, p=P), x_tok, ident, tri, ones_bf)
        moe_stage(nc, "moe0", x_tok, ident, tri, ones_bf, Wr, br, W1, W2, sorted_x, sorted_y, True)
        mamba_stage(nc, x_tok, ident, ln_w, ln_b, in_w, conv_w, conv_b, xp_w, dtp_w, dtp_b, A_log, D_skip, out_w,
                    nf_w, nf_b)
        moe_stage(nc, "moe1", x_tok, ident, tri, ones_bf, Wr, br, W1, W2, sorted_x, sorted_y, False)
        lora_weight_stage(nc, ident, wT, b_row, ones_row, W, b, lora_down, lora_up, down_aux, up_aux)
        linear_stage(nc, "linear0", x_tok, ident, wT, b_row, ones_row)
        attention_stage(nc, x_tok, ident, ones_row, w_qkv, b_qkv, w_proj, b_proj, q_rows, k_rows)
        linear_stage(nc, "linear1", x_tok, ident, wT, b_row, ones_row)
        store_stage(nc, x_tok, out.rearrange(tokens, p=P))


_INS = ["L0_attn_x", "L0_attn_ln_w", "L0_attn_ln_b", "L0_attn_in_proj_w", "L0_attn_conv_w", "L0_attn_conv_b",
        "L0_attn_x_proj_w", "L0_attn_dt_proj_w", "L0_attn_dt_proj_b", "L0_attn_A_log", "L0_attn_D_skip",
        "L0_attn_out_proj_w", "L0_attn_norm_f_w", "L0_attn_norm_f_b", "L0_ffn_Wr", "L0_ffn_br", "L0_ffn_W1",
        "L0_ffn_W2", "L1_attn_w_qkv", "L1_attn_b_qkv", "L1_attn_w_proj", "L1_attn_b_proj", "L1_ffn_W", "L1_ffn_b",
        "L1_ffn_lora_down", "L1_ffn_lora_up", "L1_ffn_down_aux", "L1_ffn_up_aux"]
_OUTS = [((4, 1024, 128), "float32")]


def kernel(**inputs):
    import numpy as _np
    import concourse.bacc as _bacc
    from concourse import mybir as _mybir
    from concourse.bass_utils import run_bass_kernel_spmd as _run

    nc = _bacc.Bacc("TRN2", target_bir_lowering=False, num_devices=1)
    arrays, args = {}, []
    for name in _INS:
        a = _np.ascontiguousarray(inputs[name])
        arrays[f"in_{name}_dram"] = a
        args.append(nc.dram_tensor(f"in_{name}_dram", a.shape, _mybir.dt.from_np(a.dtype), kind="ExternalInput").ap())
    for i, (shape, dtype) in enumerate(_OUTS):
        dt = _mybir.dt.from_np(_np.dtype(dtype))
        args.append(nc.dram_tensor(f"out_{i}_dram", shape, dt, kind="ExternalOutput").ap())
    build_program(nc, *args)
    r = _run(nc, [arrays], core_ids=[0])
    got = tuple(r.results[0][f"out_{i}_dram"] for i in range(len(_OUTS)))
    return got[0]
```

```python
from contextlib import ExitStack, contextmanager

import numpy as np

import concourse.bass as bass
from concourse import mybir

ALU = mybir.AluOpType
ACT = mybir.ActivationFunctionType
AX = mybir.AxisListType
F32 = mybir.dt.float32
BF16 = mybir.dt.bfloat16
I32 = mybir.dt.int32
U32 = mybir.dt.uint32

P = 128
C = 128
EPS = 1e-5


class Tally:

    def __init__(self, eng, sem):
        self.eng, self.sem, self.n, self.base = eng, sem, 0, 0

    def count(self, inst):
        inst.then_inc(self.sem, 1)
        self.n += 1

    def wait(self):
        self.eng.wait_ge(self.sem, self.base + self.n)

    def step(self, inst):
        self.count(inst)
        self.wait()

    @contextmanager
    def loop(self, times, each):
        start, outer = self.n, self.base
        with self.eng.Fori(0, times) as i:
            self.base = outer + i * each
            yield i
        assert self.n - start == each, (self.n - start, each)
        self.n, self.base = start + each * times, outer


class Stage:

    def __init__(self, nc, stack, stage):
        self.nc, self.stack, self.stage, self.sems = nc, stack, stage, []
        stack.callback(self.release)

    def sb(self, name, shape, dt=F32):
        return self.stack.enter_context(self.nc.sbuf_tensor(f"{self.stage}_{name}", shape, dt))

    def ps(self, name, shape, dt=F32):
        return self.stack.enter_context(self.nc.psum_tensor(f"{self.stage}_{name}", shape, dt))

    def sem(self, name):
        self.sems.append(self.nc.alloc_semaphore(f"{self.stage}_{name}"))
        return self.sems[-1]

    def release(self):
        if self.sems:
            self.nc.clear_and_free_semaphores(self.sems)
            self.nc.all_engine_barrier()


def norm_buffers(mem, tiles):
    return {
        "bn": mem.sb("bn", [P, tiles, 6]),
        "mean": mem.sb("mean", [P, tiles]),
        "var": mem.sb("var", [P, tiles]),
        "rstd": mem.sb("rstd", [P, tiles]),
        "tmp": mem.sb("tmp", [P, 2, tiles]),
    }


def norm_factors(v, own, b, tiles, first=0):
    s = slice(first, first + tiles)
    bn, mean, var, y = b["bn"][:, s, :], b["mean"][:, s], b["var"][:, s], b["rstd"][:, s]
    t0, t1 = b["tmp"][:, 0, s], b["tmp"][:, 1, s]
    own.wait()
    own.count(v.tensor_tensor(t0, bn[:, :, 1], bn[:, :, 4], ALU.subtract))
    own.count(v.tensor_tensor(t1, bn[:, :, 2], bn[:, :, 5], ALU.add))
    own.step(v.tensor_tensor(mean, bn[:, :, 1], bn[:, :, 4], ALU.add))
    own.count(v.scalar_tensor_tensor(out=t0, in0=t0, scalar=0.25, in1=t0, op0=ALU.mult, op1=ALU.mult))
    own.count(v.tensor_scalar(t1, t1, 1.0 / C, EPS, ALU.mult, ALU.add))
    own.step(v.tensor_scalar(mean, mean, 0.5, None, ALU.mult))
    own.step(v.tensor_tensor(var, t0, t1, ALU.add))
    own.step(v.tensor_scalar(t0.bitcast(I32), var.bitcast(I32), 1, None, ALU.logical_shift_right))
    own.step(v.tensor_scalar(y.bitcast(I32), t0.bitcast(I32), -1, 0x5F3759DF, ALU.mult, ALU.add))
    for _ in range(3):
        own.step(v.tensor_tensor(t0, y, y, ALU.mult))
        own.step(v.scalar_tensor_tensor(out=t0, in0=t0, scalar=-0.5, in1=var, op0=ALU.mult, op1=ALU.mult))
        own.step(v.scalar_tensor_tensor(out=y, in0=t0, scalar=1.5, in1=y, op0=ALU.add, op1=ALU.mult))


NORM_STEPS = 7 + 2 + 9


def token_stats(v, own, nb, tok, tiles):
    STEP = 8
    with own.loop(tiles // STEP, STEP) as i:
        for k in range(STEP):
            t = bass.ds(i * STEP + k, 1)
            own.count(v.bn_stats(nb["bn"][:, t, :], tok[:, t, :]))


def load_stage(nc, x_dram, x_tok, ident, tri, ones_bf):
    with ExitStack() as stack:
        mem = Stage(nc, stack, "load")
        x_loaded, cleared, made = mem.sem("x_loaded"), mem.sem("cleared"), mem.sem("made")
        block = stack.enter_context(nc.Block())

        @block.sync
        def _(sp):
            for q in range(4):
                sp.dma_start(x_tok[:, 8 * q:8 * q + 8, :], x_dram[:, 8 * q:8 * q + 8, :]).then_inc(x_loaded, 16)
            sp.wait_ge(x_loaded, 64)

        @block.gpsimd
        def _(pool):
            pool.memset(ident[:], 0.0).then_inc(cleared, 1)
            pool.memset(tri[:], 0.0).then_inc(cleared, 1)
            pool.memset(ones_bf[:], 1.0).then_inc(cleared, 1)
            pool.wait_ge(cleared, 3)
            pool.affine_select(out=ident[:], in_=ident[:], compare_op=ALU.not_equal, fill=1.0, base=0,
                               pattern=[[-1, P]], channel_multiplier=1).then_inc(made, 1)
            pool.affine_select(out=tri[:], in_=tri[:], compare_op=ALU.is_ge, fill=1.0, base=0,
                               pattern=[[-1, P]], channel_multiplier=1).then_inc(made, 1)
            pool.wait_ge(made, 2)


def store_stage(nc, x_tok, out_dram):
    with ExitStack() as stack:
        mem = Stage(nc, stack, "store")
        stored = mem.sem("stored")
        block = stack.enter_context(nc.Block())

        @block.sync
        def _(sp):
            for q in range(4):
                sp.dma_start(out_dram[:, 8 * q:8 * q + 8, :], x_tok[:, 8 * q:8 * q + 8, :]).then_inc(stored, 16)
            sp.wait_ge(stored, 64)


def moe_stage(nc, stage, x_tok, ident, tri, ones_bf, Wr, br, W1, W2, sorted_x, sorted_y, clear_sorted):
    TILES = x_tok.shape[1]
    E = Wr.shape[1]
    F = W1.shape[2]
    FB = F // P
    SLOTS = TILES + E
    GROUPS = TILES // 4
    x_slots = sorted_x.rearrange("(n p) c -> p n c", p=P)
    y_slots = sorted_y.rearrange("(n p) c -> p n c", p=P)
    with ExitStack() as stack:
        mem = Stage(nc, stack, stage)
        w1 = mem.sb("w1", [P, E, F])
        w2 = mem.sb("w2", [P, E, FB, C])
        wr = mem.sb("wr", [P, E])
        br_row = mem.sb("br_row", [P, E])
        nb = norm_buffers(mem, TILES)
        xn = mem.sb("xn", [P, TILES, C])
        xn_ring = mem.sb("xn_ring", [P, 2, 4, C])
        xnT = mem.sb("xnT", [P, 2, 4 * P])
        prob = mem.sb("prob", [P, TILES, E])
        pick = mem.sb("pick", [P, TILES, E])
        work = mem.sb("work", [P, TILES, E])
        best = mem.sb("best", [P, TILES])
        pos = mem.sb("pos", [P, TILES])
        pos_i = mem.sb("pos_i", [P, TILES], U32)
        mask_bf = mem.sb("mask_bf", [P, TILES, E], BF16)
        prefer = mem.sb("prefer", [P, E])
        ones = mem.sb("ones", [P, TILES])
        upto = mem.sb("upto", [P, TILES, E])
        total = mem.sb("total", [P, 4, E])
        total_i = mem.sb("total_i", [P, E], I32)
        slot_no = mem.sb("slot_no", [P, SLOTS, E])
        slot_e = mem.sb("slot_e", [P, SLOTS])
        slot_i = mem.sb("slot_i", [P, SLOTS], I32)
        zero = mem.sb("zero", [P, 4 * C])
        xs = mem.sb("xs", [P, 2, C])
        xsT = mem.sb("xsT", [P, 2, P])
        w1s = mem.sb("w1s", [P, 2, F])
        hT = mem.sb("hT", [P, 2, FB, P])
        ys = mem.sb("ys", [P, 2, C])
        yg = xn
        s_w, s_wr, s_zero, s_const, s_stored0 = (mem.sem(n) for n in
                                                 ("w_loaded", "wr_loaded", "zeroed", "const", "cleared"))
        s_norm, s_ring, s_T, s_Tc, s_logit = (mem.sem(n) for n in
                                              ("norm", "ring", "xnT", "xnT_copied", "logits"))
        s_v, s_z, s_exp, s_mask, s_pre, s_pos, s_slots = (mem.sem(n) for n in
                                                          ("own", "z", "exp", "mask", "prefix", "pos", "slots"))
        s_scat = mem.sem("scattered")
        s_xs = [mem.sem(f"xs{k}_loaded") for k in range(2)]
        s_out = [mem.sem(f"ys{k}_stored") for k in range(2)]
        s_xsT, s_xsTc, s_w1, s_up, s_gelu, s_down, s_ys = (mem.sem(n) for n in (
            "xsT", "xsT_copied", "w1_copied", "up", "gelu", "down", "ys"))
        s_gath = [mem.sem(f"gathered{q}") for q in range(4)]

        with ExitStack() as route_stack:
            pmem = Stage(nc, route_stack, stage + "r")
            xnT_ps = pmem.ps("xnT_ps", [P, 2, 4 * P])
            logit_ps = pmem.ps("logit_ps", [P, TILES, E])
            pre_ps = pmem.ps("pre_ps", [P, 2, 512])
            block = route_stack.enter_context(nc.Block())

            @block.sync
            def _(sp):
                sp.dma_start(wr[:], Wr).then_inc(s_wr, 16)
                sp.dma_start(br_row[:], br.rearrange("(a e) -> a e", a=1).broadcast_to([P, E])).then_inc(s_wr, 16)
                for e in range(0, E, 2):
                    sp.dma_start(w1[:, e:e + 2, :], W1[e:e + 2].rearrange("e c f -> c e f")).then_inc(s_w, 16)
                    sp.dma_start(w2[:, e:e + 2, :, :],
                                 W2[e:e + 2].rearrange("e (k f) c -> f e k c", f=P)).then_inc(s_w, 16)
                if clear_sorted:
                    sp.wait_ge(s_zero, 1)
                    for n in range(SLOTS // 4):
                        sp.dma_start(x_slots[:, 4 * n:4 * n + 4, :],
                                     zero[:].rearrange("p (n c) -> p n c", c=C)).then_inc(s_stored0, 16)
                    sp.wait_ge(s_stored0, 16 * (SLOTS // 4))
                sp.wait_ge(s_w, 16 * E)

            @block.gpsimd
            def _(pool):
                pool.memset(zero[:], 0.0).then_inc(s_zero, 1)
                pool.iota(prefer[:], pattern=[[-1, E]], base=E, channel_multiplier=0,
                          allow_small_or_imprecise_dtypes=True).then_inc(s_const, 1)
                pool.iota(slot_no[:], pattern=[[1, SLOTS], [0, E]], base=0, channel_multiplier=0,
                          allow_small_or_imprecise_dtypes=True).then_inc(s_const, 1)
                pool.memset(ones[:], 1.0).then_inc(s_const, 1)
                if clear_sorted:
                    pool.wait_ge(s_stored0, 16 * (SLOTS // 4))
                pool.wait_ge(s_pos, 1)
                for t in range(TILES):
                    pool.indirect_dma_start(sorted_x, bass.IndirectOffsetOnAxis(pos_i[:, t:t + 1], 0), xn[:, t, :],
                                            None).then_inc(s_scat, 16)
                pool.wait_ge(s_scat, 16 * TILES)

            @block.vector
            def _(v):
                own = Tally(v, s_v)
                token_stats(v, own, nb, x_tok, TILES)
                norm_factors(v, own, nb, TILES)
                for g in range(GROUPS):
                    for t in range(4 * g, 4 * g + 4):
                        v.tensor_scalar(xn[:, t, :], x_tok[:, t, :], nb["mean"][:, t:t + 1],
                                        nb["rstd"][:, t:t + 1], ALU.subtract, ALU.mult).then_inc(s_norm, 1)
                    if g >= 1:
                        v.wait_ge(s_T, g)
                        if g >= 3:
                            v.wait_ge(s_logit, g - 2)
                        v.tensor_copy(xnT[:, (g - 1) % 2, :], xnT_ps[:, (g - 1) % 2, :]).then_inc(s_Tc, 1)
                v.wait_ge(s_T, GROUPS)
                v.wait_ge(s_logit, GROUPS - 2)
                v.tensor_copy(xnT[:, (GROUPS - 1) % 2, :], xnT_ps[:, (GROUPS - 1) % 2, :]).then_inc(s_Tc, 1)

                v.wait_ge(s_wr, 32)
                v.wait_ge(s_const, 3)
                v.wait_ge(s_logit, GROUPS)

                def over_tiles(row):
                    return row.rearrange("p (a e) -> p a e", a=1).broadcast_to([P, TILES, E])

                def over_experts(col, n=TILES):
                    return col.rearrange("p (t a) -> p t a", a=1).broadcast_to([P, n, E])

                v.tensor_tensor(work[:], logit_ps[:], over_tiles(br_row[:]), ALU.add).then_inc(s_z, 1)
                v.wait_ge(s_exp, 1)
                own.step(v.tensor_scalar(work[:], prob[:], 1.0, None, ALU.add))
                own.step(v.reciprocal(prob[:], work[:]))
                own.step(v.tensor_reduce(best[:], prob[:], AX.X, ALU.max))
                own.step(v.tensor_tensor(pick[:], prob[:], over_experts(best[:]), ALU.is_equal))
                own.step(v.tensor_tensor(work[:], pick[:], over_tiles(prefer[:]), ALU.mult))
                own.step(v.tensor_reduce(pos[:], work[:], AX.X, ALU.max))
                own.step(v.tensor_tensor(pick[:], work[:], over_experts(pos[:]), ALU.is_equal))
                v.tensor_copy(mask_bf[:], pick[:]).then_inc(s_mask, 1)
                own.step(v.tensor_scalar(best[:], best[:], 0.5, None, ALU.mult))
                v.wait_ge(s_pre, 1)
                count = pre_ps[:, 1, 0:TILES * E].rearrange("p (t e) -> p t e", e=E)
                before = pre_ps[:, 0, 0:TILES * E].rearrange("p (t e) -> p t e", e=E)
                own.step(v.tensor_copy(work[:], count))
                for e in range(E):
                    own.count(v.tensor_tensor_scan(upto[:, :, e], ones[:], work[:, :, e], 0.0, ALU.mult, ALU.add))
                own.wait()
                tot, tiles_of, end, start = (total[:, k, :] for k in range(4))
                own.step(v.tensor_scalar(tot, upto[:, TILES - 1, :], float(P - 1), None, ALU.add))
                own.step(v.tensor_copy(total_i[:], tot))
                own.step(v.tensor_scalar(total_i[:], total_i[:], 7, None, ALU.logical_shift_right))
                own.step(v.tensor_copy(tiles_of, total_i[:]))
                own.step(v.tensor_tensor_scan(end, ones[:, 0:E], tiles_of, 0.0, ALU.mult, ALU.add))
                own.step(v.tensor_tensor(start, end, tiles_of, ALU.subtract))
                own.step(v.tensor_scalar(start, start, float(P), None, ALU.mult))
                own.step(v.tensor_tensor(upto[:], upto[:], work[:], ALU.subtract))
                own.step(v.tensor_tensor(upto[:], upto[:], before, ALU.add))
                own.step(v.tensor_tensor(upto[:], upto[:], over_tiles(start), ALU.add))
                own.step(v.tensor_tensor(upto[:], upto[:], pick[:], ALU.mult))
                own.step(v.tensor_reduce(pos[:], upto[:], AX.X, ALU.add))
                v.tensor_copy(pos_i[:], pos[:]).then_inc(s_pos, 1)
                own.step(v.tensor_tensor(slot_no[:], slot_no[:],
                                         end.rearrange("p (a e) -> p a e", a=1).broadcast_to([P, SLOTS, E]),
                                         ALU.is_ge))
                own.step(v.tensor_reduce(slot_e[:], slot_no[:], AX.X, ALU.add))
                own.step(v.tensor_scalar(slot_e[:], slot_e[:], float(E - 1), None, ALU.min))
                own.step(v.tensor_copy(slot_i[:], slot_e[:]))

            @block.scalar
            def _(act):
                for g in range(GROUPS):
                    act.wait_ge(s_norm, 4 * g + 4)
                    if g >= 2:
                        act.wait_ge(s_T, g - 1)
                    act.activation(xn_ring[:, g % 2], xn[:, 4 * g:4 * g + 4, :], ACT.Copy).then_inc(s_ring, 1)
                act.wait_ge(s_z, 1)
                act.activation(prob[:], work[:], ACT.Exp, scale=-1.0).then_inc(s_exp, 1)

            @block.tensor
            def _(pe):
                def logits(g):
                    pe.wait_ge(s_Tc, g + 1)
                    for k in range(4):
                        last = pe.matmul(logit_ps[:, 4 * g + k, :], xnT[:, g % 2, P * k:P * k + P], wr[:],
                                         start=True, stop=True)
                    last.then_inc(s_logit, 1)

                pe.wait_ge(s_wr, 32)
                for g in range(GROUPS):
                    pe.wait_ge(s_ring, g + 1)
                    if g >= 2:
                        pe.wait_ge(s_Tc, g - 1)
                    for k in range(4):
                        last = pe.transpose(xnT_ps[:, g % 2, P * k:P * k + P], xn_ring[:, g % 2, k, :], ident[:])
                    last.then_inc(s_T, 1)
                    if g >= 1:
                        logits(g - 1)
                logits(GROUPS - 1)
                pe.wait_ge(s_mask, 1)
                m = mask_bf[:].rearrange("p t e -> p (t e)")
                pe.matmul(pre_ps[:, 0, 0:TILES * E], tri[:], m, start=True, stop=True)
                pe.matmul(pre_ps[:, 1, 0:TILES * E], ones_bf[:], m, start=True, stop=True).then_inc(s_pre, 1)

        with ExitStack() as expert_stack:
            pmem = Stage(nc, expert_stack, stage + "e")
            xsT_ps = pmem.ps("xsT_ps", [P, 512])
            up_ps = pmem.ps("up_ps", [P, 2, F])
            y_ps = pmem.ps("y_ps", [P, 2, 512])
            block = expert_stack.enter_context(nc.Block())
            PAIRS = (SLOTS - 2) // 2

            @block.sync
            def _(sp):
                def load(j, k, n, again):
                    if again:
                        sp.wait_ge(s_xsT, j - 1)
                    sp.dma_start(xs[:, k, :], x_slots[:, bass.ds(j, 1), :]).then_inc(s_xs[k], 16)

                load(0, 0, 0, False)
                load(1, 1, 0, False)
                with sp.Fori(0, PAIRS) as i:
                    for k in range(2):
                        load(2 * i + k + 2, k, i + 1, True)

            @block.scalar
            def _(act):
                def gelu(j, k):
                    act.wait_ge(s_up, j + 1)
                    act.activation(hT[:, k].rearrange("p q t -> p (q t)"), up_ps[:, k, :], ACT.Gelu).then_inc(s_gelu, 1)

                def store(j, k):
                    act.wait_ge(s_ys, j + 3)
                    act.dma_start(y_slots[:, bass.ds(j, 1), :], ys[:, k, :]).then_inc(s_out[k], 16)

                gelu(0, 0)
                gelu(1, 1)
                with act.Fori(0, PAIRS) as i:
                    for k in range(2):
                        gelu(2 * i + k + 2, k)
                        store(2 * i + k, k)
                store(SLOTS - 2, 0)
                store(SLOTS - 1, 1)
                for k in range(2):
                    act.wait_ge(s_out[k], 16 * (SLOTS // 2))

            @block.tensor
            def _(pe):
                def turn_x(k, n):
                    pe.wait_ge(s_xs[k], 16 * (n + 1))
                    pe.transpose(xsT_ps[:, 0:P], xs[:, k, :], ident[:]).then_inc(s_xsT, 1)

                def up(j, k):
                    pe.wait_ge(s_xsTc, j + 1)
                    pe.wait_ge(s_w1, j + 1)
                    for q in range(FB):
                        last = pe.matmul(up_ps[:, k, P * q:P * q + P], w1s[:, k, P * q:P * q + P], xsT[:, k, :],
                                         start=True, stop=True)
                    last.then_inc(s_up, 1)

                def down(j, k, e):
                    pe.wait_ge(s_ys, j + 1)
                    pe.wait_ge(s_gelu, j + 1)
                    for q in range(FB):
                        last = pe.matmul(y_ps[:, k, 0:C], hT[:, k, q, :], w2[:, bass.ds(e, 1), q, :],
                                         start=(q == 0), stop=(q == FB - 1))
                    last.then_inc(s_down, 1)

                def expert(j):
                    return pe.value_load(slot_i[0:1, bass.ds(j, 1)], min_val=0, max_val=E - 1)

                turn_x(0, 0)
                up(0, 0)
                turn_x(1, 0)
                with pe.Fori(0, PAIRS) as i:
                    for k in range(2):
                        j = 2 * i + k + 1
                        e = expert(j - 1)
                        up(j, 1 - k)
                        turn_x(k, i + 1)
                        down(j - 1, k, e)
                j = SLOTS - 1
                up(j, 1)
                down(j - 1, 0, expert(j - 1))
                down(j, 1, expert(j))

            @block.vector
            def _(v):
                def copy_x(j, k):
                    v.wait_ge(s_xsT, j + 1)
                    v.tensor_copy(xsT[:, k, :], xsT_ps[:, 0:P]).then_inc(s_xsTc, 1)

                def copy_y(j, k, stored):
                    v.wait_ge(s_down, j + 1)
                    if stored is not None:
                        v.wait_ge(s_out[k], 16 * stored)
                    v.tensor_copy(ys[:, k, :], y_ps[:, k, 0:C]).then_inc(s_ys, 1)

                v.sem_inc(s_ys, 2)
                copy_x(0, 0)
                copy_x(1, 1)
                for k in range(2):
                    copy_x(k + 2, k)
                    copy_y(k, k, None)
                with v.Fori(0, PAIRS - 2) as i:
                    for k in range(2):
                        j = 2 * i + k + 2
                        copy_x(j + 2, k)
                        copy_y(j, k, i + 1)
                for j in range(SLOTS - 4, SLOTS):
                    if j + 2 < SLOTS:
                        copy_x(j + 2, j % 2)
                    copy_y(j, j % 2, j // 2)
                for t in range(TILES):
                    if t % (TILES // 4) == 0:
                        v.wait_ge(s_gath[t // (TILES // 4)], 16 * (TILES // 4))
                    v.scalar_tensor_tensor(out=x_tok[:, t, :], in0=yg[:, t, :], scalar=best[:, t:t + 1],
                                           in1=x_tok[:, t, :], op0=ALU.mult, op1=ALU.add)

            @block.gpsimd
            def _(pool):
                def stage_w1(j, k, again):
                    e = pool.value_load(slot_i[0:1, bass.ds(j, 1)], min_val=0, max_val=E - 1)
                    if again:
                        pool.wait_ge(s_up, j - 1)
                    pool.tensor_copy(w1s[:, k, :], w1[:, bass.ds(e, 1), :]).then_inc(s_w1, 1)

                stage_w1(0, 0, False)
                stage_w1(1, 1, False)
                with pool.Fori(0, PAIRS) as i:
                    for k in range(2):
                        stage_w1(2 * i + k + 2, k, True)
                for k in range(2):
                    pool.wait_ge(s_out[k], 16 * (SLOTS // 2))
                for t in range(TILES):
                    pool.indirect_dma_start(yg[:, t, :], None, sorted_y,
                                            bass.IndirectOffsetOnAxis(pos_i[:, t:t + 1], 0)).then_inc(s_gath[t // (TILES // 4)], 16)


EDGE = 1 / 8
_NODES = (np.cos((2 * np.arange(5) + 1) * np.pi / 10) + 1) * EDGE / 2
LOG1P = [float(c) for c in np.polyfit(_NODES, np.log1p(_NODES) / _NODES, 4)]


def mamba_stage(nc, x_tok, ident, ln_w, ln_b, in_w, conv_w, conv_b, xp_w, dtp_w, dtp_b, A_log, D_skip, out_w,
                nf_w, nf_b):
    LAYERS, DI, N = A_log.shape
    TAPS = conv_w.shape[2]
    R = dtp_w.shape[2]
    HALVES = DI // P
    TILES = x_tok.shape[1]
    BT = 8
    L = BT * P
    BATCHES = TILES // BT
    CH = L // 512
    BC = 2 * N
    ROWS = 3 * BC + R
    with ExitStack() as stack:
        mem = Stage(nc, stack, "mamba")
        r_tok = mem.sb("r_tok", [P, TILES, C])
        nb = norm_buffers(mem, TILES)
        w_in = mem.sb("w_in", [P, 2 * HALVES, C])
        w_tap = mem.sb("w_tap", [P, 2, C])
        wT = mem.sb("wT", [P, HALVES * TAPS + HALVES, P])
        cw = mem.sb("cw", [P, HALVES, TAPS])
        cb = mem.sb("cb", [P, LAYERS, HALVES])
        dtb = mem.sb("dtb", [P, LAYERS, HALVES])
        dsk = mem.sb("dsk", [P, HALVES])
        diag = mem.sb("diag", [P, HALVES, P])
        xp_in = mem.sb("xp_in", [ROWS, DI])
        xpT = mem.sb("xpT", [P, HALVES, ROWS])
        dtp_in = mem.sb("dtp_in", [P, HALVES, ROWS])
        dtpT = mem.sb("dtpT", [ROWS, DI])
        ow_in = mem.sb("ow_in", [P, DI])
        owT = mem.sb("owT", [P, HALVES, C])
        alog = mem.sb("alog", [P, HALVES, N])
        aneg = mem.sb("aneg", [P, HALVES, N])
        lnw = mem.sb("lnw", [P, LAYERS, 2])
        nfw = mem.sb("nfw", [P, 2, C])
        sel = mem.sb("sel", [3 * BC, BC, P], BF16)
        hn = mem.sb("hn", [P, BT, C])
        hT = mem.sb("hT", [P, TAPS - 1 + L])
        xc = mem.sb("xc", [P, HALVES, L])
        zs = mem.sb("zs", [P, HALVES, L])
        dt = mem.sb("dt", [P, HALVES, L])
        u = mem.sb("u", [P, HALVES, L])
        dt8 = mem.sb("dt8", [ROWS, L])
        parts = mem.sb("parts", [3 * BC, L], BF16)
        mid = mem.sb("mid", [3 * BC, L], BF16)
        rest = mem.sb("rest", [3 * BC, L])
        dA = mem.sb("dA", [P, 2, HALVES, L])
        dBu = mem.sb("dBu", [P, 2, HALVES, L])
        Bs = mem.sb("Bs", [P, 2, L])
        hs = mem.sb("hs", [P, HALVES, L])
        hC = mem.sb("hC", [P, 2, HALVES, L])
        e_sp, ln_sp = dA[:, 0], dA[:, 1]
        t_sp, m_sp = hs, hC[:, 0]
        edge = mem.sb("edge", [P, 3])
        ln_edge = mem.sb("ln_edge", [P, 1])
        table = mem.sb("table", [P, 1])
        yz = dBu[:, 0]

        psB = mem.ps("psB", [P, CH, 512])
        psC = mem.ps("psC", [P, CH, 512])
        psY = mem.ps("psY", [P, HALVES, CH, 512])
        flatB = psB[:].rearrange("p a b -> p (a b)")
        flatC = psC[:].rearrange("p a b -> p (a b)")

        names = ("own once layer_done scan w_copied pool_own w_loaded w_cleared sel_made layer_free w_scaled w_turned "
                 "w_ready a_exp hn hT hT_copied xc_mm z_mm xc_silu z_silu dbl_mm parts dt8 dt_mm e_abs e_exp e_over "
                 "e_ln edge_set edge_ln poly dt_part u B_mm B_copied C_mm dA dBu hC y_mm yz out_mm nf_loaded "
                 "zero_pad").split()
        s = {n: mem.sem(n) for n in names}
        PREP = HALVES * TAPS
        TURNS = PREP + 4 * HALVES
        RING = 2 * HALVES
        B_AHEAD = 3
        LOADS = 10
        ONCE = 4

        def loaded(eng, l):
            eng.wait_ge(s["once"], 16 * ONCE)
            eng.wait_ge(s["w_loaded"], 16 * LOADS * (l + 1))
        block = stack.enter_context(nc.Block())

        @block.sync
        def _(sp):
            for k, w in enumerate((nf_w, nf_b)):
                sp.dma_start(nfw[:, k, :], w.rearrange("(a c) -> a c", a=1).broadcast_to([P, C])).then_inc(s["nf_loaded"], 16)
            with nc.allow_non_contiguous_dma(reason="one value per channel"):
                for dst, src in ((cb[:], conv_b.rearrange("l (h p) -> p l h", p=P)),
                                 (dtb[:], dtp_b.rearrange("l (h p) -> p l h", p=P)),
                                 (lnw[:, :, 0], ln_w.rearrange("l c -> c l")), (lnw[:, :, 1], ln_b.rearrange("l c -> c l"))):
                    sp.dma_start(dst, src).then_inc(s["once"], 16)
            sp.wait_ge(s["w_cleared"], 1)
            with sp.Fori(0, LAYERS) as l:
                sp.wait_ge(s["layer_free"], l + 1)
                one = bass.ds(l, 1)
                loads = [
                    (w_in[:], in_w[one].rearrange("a (k p) c -> p (a k) c", p=P)),
                    (cw[:], conv_w[one].rearrange("a (h p) t -> p (a h) t", p=P)),
                    (dsk[:], D_skip[one].rearrange("a (h p) -> p (a h)", p=P)),
                    (alog[:], A_log[one].rearrange("a (h p) n -> p (a h) n", p=P)),
                    (ow_in[:], out_w[one].rearrange("a d e -> d (a e)")),
                    (dtp_in[:, :, 3 * BC:ROWS], dtp_w[one].rearrange("a (h p) r -> p (a h) r", p=P)),
                    (xp_in[3 * BC:ROWS, :], xp_w[one, 0:R].rearrange("a r e -> r (a e)")),
                ] + [(xp_in[BC * k:BC * k + BC, :], xp_w[one, R:R + BC].rearrange("a r e -> r (a e)")) for k in range(3)]
                for dst, src in loads:
                    with nc.allow_non_contiguous_dma(reason="a few hundred values per channel"):
                        sp.dma_start(dst, src).then_inc(s["w_loaded"], 16)
            assert len(loads) == LOADS

        @block.gpsimd
        def _(pool):
            own = Tally(pool, s["pool_own"])
            pool.memset(dtp_in[:], 0.0).then_inc(s["w_cleared"], 1)
            for k, value in enumerate((-EDGE, 1 + EDGE, 0.0)):
                pool.memset(edge[:, k:k + 1], value).then_inc(s["edge_set"], 1)
                pool.wait_ge(s["edge_set"], k + 1)
            pool.memset(hT[:, 0:TAPS - 1], 0.0).then_inc(s["zero_pad"], 1)
            own.step(pool.memset(sel[:], 0.0))
            for q in range(3):
                own.step(pool.affine_select(out=sel[:], in_=sel[:], compare_op=ALU.not_equal, fill=1.0,
                                            base=-BC * q, pattern=[[-1, BC], [0, P]], channel_multiplier=1))
            pool.sem_inc(s["sel_made"], 1)
            pool.sem_inc(s["dBu"], RING)
            with pool.Fori(0, LAYERS * BATCHES) as g:
                for h in range(HALVES):
                    pool.wait_ge(s["poly"], HALVES * g + h + 1)
                    pool.tensor_tensor(dt[:, h, :], dt[:, h, :], t_sp[:, h, :], ALU.add).then_inc(s["dt_part"], 1)
                with pool.Fori(0, N // 2) as i:
                    for k in range(2):
                        m = g * N + i * 2 + k
                        pool.wait_ge(s["B_copied"], m + 2)
                        for h in range(HALVES):
                            pool.wait_ge(s["u"], HALVES * g + h + 1)
                            pool.wait_ge(s["scan"], HALVES * m + h + 1)
                            pool.tensor_tensor(dBu[:, k, h, :], u[:, h, :], Bs[:, k, :],
                                               ALU.mult).then_inc(s["dBu"], 1)

        @block.scalar
        def _(act):
            act.sem_inc(s["B_copied"], 1)
            act.wait_ge(s["edge_set"], 3)
            act.activation(ln_edge[:], edge[:, 2:3], ACT.Ln, bias=edge[:, 1:2]).then_inc(s["edge_ln"], 1)
            with act.Fori(0, LAYERS) as l:
                loaded(act, l)
                act.wait_ge(s["layer_done"], l + 1)
                act.activation(aneg[:].rearrange("p h n -> p (h n)"), alog[:].rearrange("p h n -> p (h n)"),
                               ACT.Exp).then_inc(s["a_exp"], 1)
                act.wait_ge(s["w_ready"], l + 1)
                with act.Fori(0, BATCHES) as b:
                    g = l * BATCHES + b
                    for h in range(HALVES):
                        act.wait_ge(s["xc_mm"], HALVES * g + h + 1)
                        act.activation(xc[:, h, :], psY[:, h].rearrange("p a b -> p (a b)"), ACT.Silu,
                                       bias=cb[:, bass.ds(l, 1), h]).then_inc(s["xc_silu"], 1)
                    act.activation(table[:], edge[:, 2:3], ACT.Exp)
                    for h, ps in enumerate((flatC, flatB)):
                        act.wait_ge(s["dt_mm"], HALVES * g + h + 1)
                        act.activation(dt[:, h, :], ps, ACT.Relu, bias=dtb[:, bass.ds(l, 1), h])
                        act.activation(e_sp[:, h, :], ps, ACT.Abs, bias=dtb[:, bass.ds(l, 1), h]).then_inc(s["e_abs"], 1)
                        act.wait_ge(s["e_abs"], HALVES * g + h + 1)
                        act.activation(e_sp[:, h, :], e_sp[:, h, :], ACT.Exp, scale=-1.0).then_inc(s["e_exp"], 1)
                        act.wait_ge(s["e_exp"], HALVES * g + h + 1)
                        act.activation(ln_sp[:, h, :], e_sp[:, h, :], ACT.Relu, bias=edge[:, 0:1]).then_inc(s["e_over"], 1)
                    for h in range(HALVES):
                        act.wait_ge(s["e_over"], HALVES * g + h + 1)
                        act.activation(ln_sp[:, h, :], ln_sp[:, h, :], ACT.Ln, bias=edge[:, 1:2]).then_inc(s["e_ln"], 1)
                    act.wait_ge(s["z_mm"], g + 1)
                    for h in range(HALVES):
                        last = act.activation(zs[:, h, :], psY[:, h].rearrange("p a b -> p (a b)"), ACT.Silu)
                    last.then_inc(s["z_silu"], 1)
                    with act.Fori(0, N // 2) as i:
                        for k in range(2):
                            m = g * N + i * 2 + k
                            act.wait_ge(s["dBu"], HALVES * m + HALVES)
                            act.wait_ge(s["B_mm"], m + 1)
                            act.activation(Bs[:, k, :], flatB, ACT.Copy).then_inc(s["B_copied"], 1)
                            for h in range(HALVES):
                                act.wait_ge(s["u"], HALVES * g + h + 1)
                                act.wait_ge(s["scan"], HALVES * m + h + 1)
                                act.activation(dA[:, k, h, :], dt[:, h, :], ACT.Exp,
                                               scale=aneg[:, h, bass.ds(i * 2 + k, 1)]).then_inc(s["dA"], 1)

        @block.tensor
        def _(pe):
            pe.sem_inc(s["y_mm"], 2)
            pe.wait_ge(s["sel_made"], 1)
            pe.wait_ge(s["zero_pad"], 1)
            with pe.Fori(0, LAYERS) as l:
                loaded(pe, l)
                turns = 0

                def turn(in_, rows):
                    nonlocal turns
                    out = psY[:, (turns % 4) // 2, turns % 2, 0:P]
                    if turns >= 4:
                        pe.wait_ge(s["w_copied"], l * TURNS + turns - 3)
                    pe.transpose(out[0:rows, 0:in_.shape[0]], in_, ident[0:in_.shape[0], 0:in_.shape[0]]).then_inc(s["w_turned"], 1)
                    turns += 1
                for q in range(PREP):
                    pe.wait_ge(s["w_scaled"], l * PREP + q + 1)
                    turn(w_tap[:, q % 2, :], P)
                for h in range(HALVES):
                    turn(w_in[:, HALVES + h, :], P)
                for h in range(HALVES):
                    turn(xp_in[:, P * h:P * h + P], P)
                for h in range(HALVES):
                    turn(dtp_in[:, h, :], ROWS)
                for h in range(HALVES):
                    turn(ow_in[:, P * h:P * h + P], P)
                assert turns == TURNS
                pe.wait_ge(s["w_ready"], l + 1)

                def turn_tokens(g):
                    pe.wait_ge(s["hn"], g + 1)
                    for t in range(BT):
                        last = pe.transpose(psC[:, t // 4, P * (t % 4):P * (t % 4) + P], hn[:, t, :], ident[:])
                    last.then_inc(s["hT"], 1)

                def batch(b, last_batch):
                    g = l * BATCHES + b
                    pe.wait_ge(s["hT_copied"], g + 1)
                    for h in range(HALVES):
                        for c in range(CH):
                            for k in range(TAPS):
                                last = pe.matmul(psY[:, h, c, :], wT[:, h * TAPS + k, :],
                                                 hT[:, 512 * c + k:512 * c + k + 512], start=(k == 0), stop=(k == TAPS - 1))
                        last.then_inc(s["xc_mm"], 1)
                    for h in range(HALVES):
                        pe.wait_ge(s["xc_silu"], HALVES * g + h + 1)
                        for c in range(CH):
                            last = pe.matmul(psY[0:ROWS, 0, c, :], xpT[:, h, :], xc[:, h, 512 * c:512 * c + 512],
                                             start=(h == 0), stop=(h == HALVES - 1))
                    last.then_inc(s["dbl_mm"], 1)
                    pe.wait_ge(s["dt8"], g + 1)
                    for h, ps in ((0, psC), (1, psB)):
                        for c in range(CH):
                            last = pe.matmul(ps[:, c, :], dtpT[3 * BC:ROWS, P * h:P * h + P],
                                             dt8[3 * BC:ROWS, 512 * c:512 * c + 512], start=True, stop=True)
                        last.then_inc(s["dt_mm"], 1)
                    pe.wait_ge(s["parts"], g + 1)
                    for h in range(HALVES):
                        for c in range(CH):
                            last = pe.matmul(psY[:, h, c, :], wT[:, PREP + h, :],
                                             hT[:, TAPS - 1 + 512 * c:TAPS - 1 + 512 * c + 512], start=True, stop=True)
                    last.then_inc(s["z_mm"], 1)
                    pe.wait_ge(s["e_abs"], HALVES * g + HALVES)

                    def spread(ps, row, sem):
                        for c in range(CH):
                            last = pe.matmul(ps[:, c, :], sel[:, bass.ds(row, 1), :],
                                             parts[:, 512 * c:512 * c + 512], start=True, stop=True)
                        last.then_inc(sem, 1)

                    def spread_B(n):
                        pe.wait_ge(s["B_copied"], g * N + n + 1)
                        spread(psB, n, s["B_mm"])

                    def spread_C(n):
                        pe.wait_ge(s["hC"], HALVES * (g * N + n) + HALVES)
                        spread(psC, n + N, s["C_mm"])

                    def step(n, k, left):
                        if left >= B_AHEAD:
                            spread_B(n + B_AHEAD)
                        for h in range(HALVES):
                            pe.wait_ge(s["hC"], HALVES * (g * N + n) + HALVES + h + 1)
                            if h == HALVES - 1 and left:
                                spread_C(n + 1)
                            for c in range(CH):
                                last = pe.matmul(psY[:, h, c, :], ident[:], hC[:, k, h, 512 * c:512 * c + 512],
                                                 start=False, stop=True, skip_group_check=True)
                        last.then_inc(s["y_mm"], 1)

                    spread_B(0)
                    pe.wait_ge(s["z_silu"], g + 1)
                    for h in range(HALVES):
                        for c in range(CH):
                            pe.matmul(psY[:, h, c, :], diag[:, h, :], xc[:, h, 512 * c:512 * c + 512],
                                      start=True, stop=True)
                    spread_C(0)
                    for n in range(1, B_AHEAD):
                        spread_B(n)
                    with pe.Fori(0, N // 2 - 2) as i:
                        for k in range(2):
                            step(i * 2 + k, k, B_AHEAD)
                    for n in range(N - 4, N):
                        step(n, n % 2, N - 1 - n)
                    if not last_batch:
                        turn_tokens(g + 1)
                    pe.wait_ge(s["yz"], g + 1)
                    for t in range(BT):
                        for h in range(HALVES):
                            last = pe.matmul(psB[:, t // 4, P * (t % 4):P * (t % 4) + P], yz[:, h, P * t:P * t + P],
                                             owT[:, h, :], start=(h == 0), stop=(h == HALVES - 1))
                    last.then_inc(s["out_mm"], 1)

                turn_tokens(l * BATCHES)
                with pe.Fori(0, BATCHES - 1) as b:
                    batch(b, False)
                batch(BATCHES - 1, True)

        @block.vector
        def _(v):
            own = Tally(v, s["own"])
            v.sem_inc(s["layer_free"], 1)
            v.sem_inc(s["layer_done"], 1)
            token_stats(v, own, nb, x_tok, TILES)
            norm_factors(v, own, nb, TILES)
            for t in range(TILES):
                own.count(v.tensor_scalar(r_tok[:, t, :], x_tok[:, t, :], nb["mean"][:, t:t + 1],
                                          nb["rstd"][:, t:t + 1], ALU.subtract, ALU.mult))
            own.wait()
            v.sem_inc(s["scan"], RING)
            v.sem_inc(s["hC"], HALVES)
            PER_BATCH = BT + NORM_STEPS + 17

            def normalize(b):
                for t in range(BT):
                    own.count(v.bn_stats(nb["bn"][:, t, :], r_tok[:, bass.ds(b * BT + t, 1), :]))
                norm_factors(v, own, nb, BT)
                for t in range(BT):
                    last = v.tensor_scalar(hn[:, t, :], r_tok[:, bass.ds(b * BT + t, 1), :], nb["mean"][:, t:t + 1],
                                           nb["rstd"][:, t:t + 1], ALU.subtract, ALU.mult)
                last.then_inc(s["hn"], 1)

            def copy_hT(g, l):
                v.wait_ge(s["hT"], g + 1)
                v.tensor_scalar(hT[:, TAPS - 1:], flatC, lnw[:, bass.ds(l, 1), 0], lnw[:, bass.ds(l, 1), 1], ALU.mult,
                                ALU.add).then_inc(s["hT_copied"], 1)

            normalize(0)
            v.wait_ge(s["edge_ln"], 1)
            with own.loop(LAYERS, HALVES + 1 + BATCHES * PER_BATCH) as l:
                loaded(v, l)
                turned = [wT[:, q, :] for q in range(PREP + HALVES)] + [xpT[:, h, :] for h in range(HALVES)] + \
                    [dtpT[3 * BC:ROWS, P * h:P * h + P] for h in range(HALVES)] + [owT[:, h, :] for h in range(HALVES)]

                def copy_turn(q):
                    dst = turned[q]
                    lo, n = (3 * BC, R) if PREP + 2 * HALVES <= q < PREP + 3 * HALVES else (0, P)
                    v.wait_ge(s["w_turned"], l * TURNS + q + 1)
                    v.tensor_copy(dst, psY[lo:lo + n, (q % 4) // 2, q % 2, 0:dst.shape[-1]]).then_inc(s["w_copied"], 1)

                for q in range(PREP):
                    h, k = q // TAPS, q % TAPS
                    if q >= 2:
                        v.wait_ge(s["w_turned"], l * TURNS + q - 1)
                    inst = v.tensor_scalar(w_tap[:, q % 2, :], w_in[:, h, :], cw[:, h, k:k + 1], None, ALU.mult)
                    inst.then_inc(s["w_scaled"], 1)
                    if q >= 2:
                        copy_turn(q - 2)
                for q in range(PREP - 2, TURNS):
                    copy_turn(q)
                for h in range(HALVES):
                    own.count(v.tensor_scalar(diag[:, h, :], ident[:], dsk[:, h:h + 1], None, ALU.mult))
                v.wait_ge(s["a_exp"], l + 1)
                own.count(v.tensor_scalar(aneg[:].rearrange("p h n -> p (h n)"), aneg[:].rearrange("p h n -> p (h n)"),
                                          -1.0, None, ALU.mult))
                own.wait()
                v.wait_ge(s["w_copied"], TURNS * (l + 1))
                v.sem_inc(s["w_ready"], 1)
                v.sem_inc(s["layer_free"], 1)
                copy_hT(l * BATCHES, l)

                def batch(b, last_batch):
                    g = l * BATCHES + b
                    normalize(0 if last_batch else b + 1)
                    v.wait_ge(s["dbl_mm"], g + 1)
                    dbl = psY[:, 0].rearrange("p a b -> p (a b)")
                    v.tensor_copy(dt8[3 * BC:ROWS, :], dbl[3 * BC:ROWS, :]).then_inc(s["dt8"], 1)
                    J = 3 * BC
                    own.step(v.tensor_copy(parts[:], dbl[0:J, :]))
                    own.step(v.tensor_tensor(rest[:], dbl[0:J, :], parts[:], ALU.subtract))
                    own.step(v.tensor_copy(mid[:], rest[:]))
                    own.step(v.tensor_tensor(rest[:], rest[:], mid[:], ALU.subtract))
                    v.tensor_copy(parts[BC:2 * BC, :], mid[BC:2 * BC, :])
                    v.tensor_copy(parts[2 * BC:J, :], rest[2 * BC:J, :]).then_inc(s["parts"], 1)
                    for h in range(HALVES):
                        e, m, t = e_sp[:, h, :], m_sp[:, h, :], t_sp[:, h, :]
                        v.wait_ge(s["e_exp"], HALVES * g + h + 1)
                        own.step(v.tensor_scalar(m, e, EDGE, None, ALU.min))
                        own.step(v.tensor_scalar(t, m, LOG1P[0], LOG1P[1], ALU.mult, ALU.add))
                        own.step(v.tensor_tensor(t, t, m, ALU.mult))
                        for c in LOG1P[2:-1]:
                            own.step(v.scalar_tensor_tensor(out=t, in0=t, scalar=c, in1=m, op0=ALU.add, op1=ALU.mult))
                        v.scalar_tensor_tensor(out=t, in0=t, scalar=LOG1P[-1], in1=m, op0=ALU.add,
                                               op1=ALU.mult).then_inc(s["poly"], 1)
                    for h in range(HALVES):
                        v.wait_ge(s["dt_part"], HALVES * g + h + 1)
                        v.wait_ge(s["e_ln"], HALVES * g + h + 1)
                        own.step(v.scalar_tensor_tensor(out=dt[:, h, :], in0=ln_sp[:, h, :], scalar=ln_edge[:, 0:1],
                                                        in1=dt[:, h, :], op0=ALU.subtract, op1=ALU.add))
                        v.tensor_tensor(u[:, h, :], dt[:, h, :], xc[:, h, :], ALU.mult).then_inc(s["u"], 1)
                    with v.Fori(0, N // 2) as i:
                        for k in range(2):
                            m = g * N + i * 2 + k
                            for h in range(HALVES):
                                v.wait_ge(s["dA"], HALVES * m + h + 1)
                                v.wait_ge(s["dBu"], HALVES * m + h + 1 + RING)
                                v.wait_ge(s["hC"], HALVES * m + h + 1)
                                v.tensor_tensor_scan(hs[:, h, :], dA[:, k, h, :], dBu[:, k, h, :], 0.0,
                                                     ALU.mult, ALU.add).then_inc(s["scan"], 1)
                            v.wait_ge(s["C_mm"], m + 1)
                            v.wait_ge(s["y_mm"], m + 1)
                            for h in range(HALVES):
                                v.wait_ge(s["scan"], HALVES * m + h + 1 + RING)
                                v.tensor_tensor(hC[:, k, h, :], hs[:, h, :], flatC, ALU.mult).then_inc(s["hC"], 1)
                    v.wait_ge(s["y_mm"], (g + 1) * N + 2)
                    for h in range(HALVES):
                        last = v.tensor_tensor(yz[:, h, :], zs[:, h, :], psY[:, h].rearrange("p a b -> p (a b)"), ALU.mult)
                    last.then_inc(s["yz"], 1)
                    if not last_batch:
                        copy_hT(g + 1, l)
                    v.wait_ge(s["out_mm"], g + 1)
                    tok = r_tok[:, bass.ds(b * BT, BT), :]
                    own.step(v.tensor_tensor(tok, tok, flatB.rearrange("p (t c) -> p t c", c=C), ALU.add))

                with own.loop(BATCHES - 1, PER_BATCH) as b:
                    batch(b, False)
                batch(BATCHES - 1, True)
                v.sem_inc(s["layer_done"], 1)
            token_stats(v, own, nb, r_tok, TILES)
            norm_factors(v, own, nb, TILES)
            for t in range(TILES):
                own.count(v.tensor_scalar(r_tok[:, t, :], r_tok[:, t, :], nb["mean"][:, t:t + 1],
                                          nb["rstd"][:, t:t + 1], ALU.subtract, ALU.mult))
            own.wait()
            v.wait_ge(s["nf_loaded"], 32)
            rows = [nfw[:, k:k + 1, :].broadcast_to([P, TILES, C]) for k in range(2)]
            own.step(v.tensor_tensor(r_tok[:], r_tok[:], rows[0], ALU.mult))
            own.step(v.tensor_tensor(r_tok[:], r_tok[:], rows[1], ALU.add))
            own.step(v.tensor_tensor(x_tok[:], x_tok[:], r_tok[:], ALU.add))


def lora_weight_stage(nc, ident, wT, b_row, ones_row, W, b, lora_down, lora_up, down_aux, up_aux):
    RANK, DD = lora_down.shape
    UD = lora_up.shape[0]
    with ExitStack() as stack:
        mem = Stage(nc, stack, "lora")
        w_in = mem.sb("w_in", [P, C])
        ld = mem.sb("ld", [RANK, DD])
        lu = mem.sb("lu", [UD, RANK])
        da = mem.sb("da", [DD, C])
        ua = mem.sb("ua", [P, UD])
        ldT = mem.sb("ldT", [DD, RANK])
        luT = mem.sb("luT", [RANK, UD])
        uaT = mem.sb("uaT", [UD, P])
        m1 = mem.sb("m1", [RANK, C])
        m2 = mem.sb("m2", [UD, C])
        ps = mem.ps("ps", [P, 6, 512])
        loaded, ones_set, done, copied = (mem.sem(n) for n in ("loaded", "ones_set", "mm", "copied"))
        block = stack.enter_context(nc.Block())

        @block.sync
        def _(sp):
            for dst, src in ((w_in, W), (ld, lora_down), (lu, lora_up), (da, down_aux), (ua, up_aux),
                             (b_row, b.rearrange("(a c) -> a c", a=1))):
                sp.dma_start(dst[:], src).then_inc(loaded, 16)

        @block.gpsimd
        def _(pool):
            pool.memset(ones_row[:], 1.0).then_inc(ones_set, 1)
            pool.wait_ge(ones_set, 1)

        @block.tensor
        def _(pe):
            pe.wait_ge(loaded, 96)
            pe.transpose(ps[0:DD, 0, 0:RANK], ld[:], ident[0:RANK, 0:RANK]).then_inc(done, 1)
            pe.transpose(ps[0:RANK, 1, 0:UD], lu[:], ident[0:UD, 0:UD]).then_inc(done, 1)
            pe.transpose(ps[0:UD, 2, 0:P], ua[:], ident[:]).then_inc(done, 1)
            pe.wait_ge(copied, 1)
            pe.matmul(ps[0:RANK, 3, 0:C], ldT[:], da[:], start=True, stop=True).then_inc(done, 1)
            pe.wait_ge(copied, 4)
            pe.matmul(ps[0:UD, 4, 0:C], luT[:], m1[:], start=True, stop=True).then_inc(done, 1)
            pe.wait_ge(copied, 5)
            pe.matmul(ps[:, 5, 0:C], w_in[:], ident[:], start=True, stop=False)
            pe.matmul(ps[:, 5, 0:C], m2[:], uaT[:], start=False, stop=True).then_inc(done, 1)

        @block.vector
        def _(v):
            for n, (dst, src) in enumerate(((ldT, ps[0:DD, 0, 0:RANK]), (luT, ps[0:RANK, 1, 0:UD]),
                                            (uaT, ps[0:UD, 2, 0:P]), (m1, ps[0:RANK, 3, 0:C]),
                                            (m2, ps[0:UD, 4, 0:C]), (wT, ps[:, 5, 0:C]))):
                v.wait_ge(done, n + 1)
                v.tensor_copy(dst[:], src).then_inc(copied, 1)
            v.wait_ge(copied, 6)


def linear_stage(nc, stage, x_tok, ident, wT, b_row, ones_row):
    TILES = x_tok.shape[1]
    GROUPS = TILES // 4
    with ExitStack() as stack:
        mem = Stage(nc, stack, stage)
        nb = norm_buffers(mem, TILES)
        xn = mem.sb("xn", [P, 2, 4, C])
        xnT = mem.sb("xnT", [P, 2, 512])
        ps_T = mem.ps("ps_T", [P, 2, 512])
        ps_y = mem.ps("ps_y", [P, 2, 512])
        s_own, s_xn, s_T, s_Tc, s_y, s_out = (mem.sem(n) for n in ("own", "xn", "turned", "copied", "y", "added"))
        block = stack.enter_context(nc.Block())

        @block.vector
        def _(v):
            own = Tally(v, s_own)
            token_stats(v, own, nb, x_tok, TILES)
            norm_factors(v, own, nb, TILES)

            def norm(n, k):
                for q in range(4):
                    t = n * 4 + q
                    last = v.tensor_scalar(xn[:, k, q, :], x_tok[:, bass.ds(t, 1), :], nb["mean"][:, bass.ds(t, 1)],
                                           nb["rstd"][:, bass.ds(t, 1)], ALU.subtract, ALU.mult)
                last.then_inc(s_xn, 1)

            def add(n, k):
                v.wait_ge(s_y, n + 1)
                tok = x_tok[:, bass.ds(n * 4, 4), :]
                v.scalar_tensor_tensor(out=tok, in0=ps_y[:, k].rearrange("p (q c) -> p q c", c=C), scalar=0.5,
                                       in1=tok, op0=ALU.mult, op1=ALU.add).then_inc(s_out, 1)

            norm(0, 0)
            norm(1, 1)
            with v.Fori(0, (GROUPS - 2) // 2) as i:
                for k in range(2):
                    add(2 * i + k, k)
                    norm(2 * i + k + 2, k)
            for k in range(2):
                add(GROUPS - 2 + k, k)
            v.wait_ge(s_out, GROUPS)

        @block.scalar
        def _(act):
            with act.Fori(0, GROUPS // 2) as i:
                for k in range(2):
                    act.wait_ge(s_T, 2 * i + k + 1)
                    act.activation(xnT[:, k, :], ps_T[:, k, :], ACT.Copy).then_inc(s_Tc, 1)

        @block.tensor
        def _(pe):
            def turn(n, k):
                pe.wait_ge(s_xn, n + 1)
                for q in range(4):
                    last = pe.transpose(ps_T[:, k, P * q:P * q + P], xn[:, k, q, :], ident[:])
                last.then_inc(s_T, 1)

            def product(n, k, again):
                pe.wait_ge(s_Tc, n + 1)
                if again:
                    pe.wait_ge(s_out, n - 1)
                for q in range(4):
                    o = ps_y[:, k, P * q:P * q + P]
                    pe.matmul(o, xnT[:, k, P * q:P * q + P], wT[:], start=True, stop=False)
                    last = pe.matmul(o, ones_row[:], b_row[:], start=False, stop=True)
                last.then_inc(s_y, 1)

            turn(0, 0)
            turn(1, 1)
            product(0, 0, False)
            turn(2, 0)
            product(1, 1, False)
            with pe.Fori(0, (GROUPS - 4) // 2) as i:
                for k in range(2):
                    turn(2 * i + k + 3, 1 - k)
                    product(2 * i + k + 2, k, True)
            turn(GROUPS - 1, 1)
            product(GROUPS - 2, 0, True)
            product(GROUPS - 1, 1, True)


Q_PARTS = (0, 0, 1, 1, 0, 2)
K_PARTS = (0, 1, 0, 1, 2, 0)
MAX_PARTS = 3


def attention_stage(nc, x_tok, ident, ones_row, w_qkv, b_qkv, w_proj, b_proj, q_dram, k_dram):
    TILES = x_tok.shape[1]
    BT = 8
    L = BT * P
    BATCHES = TILES // BT
    D = 8
    HEADS = C // D
    PAIRS = HEADS // 2
    SCALE = D ** -0.5
    QR = len(Q_PARTS) * D
    KR = QR + MAX_PARTS
    MAX_BANKS = 3
    VW = D + 1
    with ExitStack() as stack:
        mem = Stage(nc, stack, "attn")
        v_aug = mem.sb("v_aug", [P, BATCHES, BT, HEADS, VW])
        wqkv = mem.sb("wqkv", [P, 3, C])
        wp = mem.sb("wp", [P, C])
        bqk = mem.sb("bqk", [P, 2])
        bv = mem.sb("bv", [1, C])
        bp = mem.sb("bp", [1, C])

        q1 = mem.sb("q1", [P, 2, 2, L], BF16)
        k1 = mem.sb("k1", [P, 2, L], BF16)
        q2 = mem.sb("q2", [P, 2, L], BF16)
        k2 = mem.sb("k2", [P, 2, 2, L], BF16)
        ones = mem.sb("ones", [2 * BT, P])
        v_pair = mem.sb("v_pair", [P, BT, 2, 32])

        with ExitStack() as project_stack:
            pm = Stage(nc, project_stack, "qkv")
            nb = norm_buffers(pm, TILES)
            xn = pm.sb("xn", [P, BT, C])
            xnT = pm.sb("xnT", [P, L])
            full = pm.sb("full", [P, 2, L])
            part = pm.sb("part", [P, 2, 3, L], BF16)
            ps_T = pm.ps("ps_T", [P, L])
            ps_q = pm.ps("ps_q", [P, 2, L])
            ps_v = pm.ps("ps_v", [P, BT, C])
            names = "own xn turned copied q_mm v_mm biased split v_copied loaded set".split()
            s = {n: pm.sem(n) for n in names}
            stored = [pm.sem(n) for n in ("q_stored", "k_stored")]
            STORES = 16 * len(Q_PARTS)
            block = project_stack.enter_context(nc.Block())

            @block.sync
            def _(sp):
                with nc.allow_non_contiguous_dma(reason="one value per channel"):
                    for dst, src in ((wqkv[:], w_qkv.rearrange("c (k e) -> c k e", k=3)), (wp[:], w_proj),
                                     (bqk[:], b_qkv[0:2 * C].rearrange("(k e) -> e k", k=2)),
                                     (bv[:], b_qkv[2 * C:3 * C].rearrange("(a e) -> a e", a=1)),
                                     (bp[:], b_proj.rearrange("(a e) -> a e", a=1))):
                        sp.dma_start(dst, src).then_inc(s["loaded"], 16)
                for w in range(2):
                    sp.sem_inc(stored[w], STORES)
                with sp.Fori(0, BATCHES) as b:
                    for w, dram, parts_of in ((0, q_dram, Q_PARTS), (1, k_dram, K_PARTS)):
                        sp.wait_ge(s["split"], 2 * b + w + 3)
                        for c, p in enumerate(parts_of):
                            sp.dma_start(dram[bass.ds(b, 1), :, D * c:D * c + D, :].rearrange("a h d t -> (a h) d t"),
                                         part[:, w, p, :]).then_inc(stored[w], 16)
                for w in range(2):
                    sp.wait_ge(stored[w], STORES * (BATCHES + 1))

            @block.gpsimd
            def _(pool):
                own = Tally(pool, s["set"])
                own.step(pool.memset(v_aug[:, :, :, :, D:VW], 1.0))
                for rows in (q1, k1, q2, k2, v_pair):
                    own.step(pool.memset(rows[:], 0.0))
                for j in range(2):
                    own.step(pool.memset(k2[64 * j + 32:64 * j + 64, :, j, :], 1.0))
                own.step(pool.memset(ones[:], 1.0))

            @block.vector
            def _(v):
                own = Tally(v, s["own"])
                token_stats(v, own, nb, x_tok, TILES)
                norm_factors(v, own, nb, TILES)
                v.sem_inc(s["split"], 2)
                v.sem_inc(s["v_copied"], 1)

                def norm(b):
                    for q in range(BT):
                        t = b * BT + q
                        last = v.tensor_scalar(xn[:, q, :], x_tok[:, bass.ds(t, 1), :], nb["mean"][:, bass.ds(t, 1)],
                                               nb["rstd"][:, bass.ds(t, 1)], ALU.subtract, ALU.mult)
                    last.then_inc(s["xn"], 1)

                def split(b, again):
                    if again:
                        v.wait_ge(s["turned"], b + 1)
                        norm(b + 1)
                    v.wait_ge(s["v_mm"], b + 1)
                    v.tensor_copy(v_aug[:, bass.ds(b, 1), :, :, 0:D].rearrange("p a t h d -> p (a t) h d"),
                                  ps_v[:].rearrange("p t (h d) -> p t h d", d=D)).then_inc(s["v_copied"], 1)
                    for w in range(2):
                        v.wait_ge(s["biased"], 2 * b + w + 3)
                        v.wait_ge(stored[w], STORES * (b + 1))
                        own.step(v.tensor_copy(part[:, w, 0, :], full[:, w, :]))
                        own.step(v.tensor_tensor(full[:, w, :], full[:, w, :], part[:, w, 0, :], ALU.subtract))
                        own.step(v.tensor_copy(part[:, w, 1, :], full[:, w, :]))
                        v.tensor_tensor(part[:, w, 2, :], full[:, w, :], part[:, w, 1, :],
                                        ALU.subtract).then_inc(s["split"], 1)

                norm(0)
                with own.loop(BATCHES - 1, 6) as b:
                    split(b, True)
                split(BATCHES - 1, False)
                v.wait_ge(s["v_copied"], BATCHES + 1)

            @block.scalar
            def _(act):
                act.wait_ge(s["loaded"], 80)
                act.sem_inc(s["biased"], 2)
                with act.Fori(0, BATCHES) as b:
                    act.wait_ge(s["q_mm"], 2 * b + 2)
                    act.wait_ge(s["turned"], b + 1)
                    act.activation(xnT[:], ps_T[:], ACT.Copy).then_inc(s["copied"], 1)
                    for w in range(2):
                        act.wait_ge(s["split"], 2 * b + w + 1)
                        act.wait_ge(s["q_mm"], 2 * b + w + 3)
                        act.activation(full[:, w, :], ps_q[:, w, :], ACT.Identity,
                                       bias=bqk[:, w:w + 1]).then_inc(s["biased"], 1)

            @block.tensor
            def _(pe):
                pe.sem_inc(s["q_mm"], 2)
                pe.wait_ge(s["loaded"], 80)

                def turn(b):
                    pe.wait_ge(s["xn"], b + 1)
                    for q in range(BT):
                        last = pe.transpose(ps_T[:, P * q:P * q + P], xn[:, q, :], ident[:])
                    last.then_inc(s["turned"], 1)

                def project(b, again):
                    pe.wait_ge(s["copied"], b + 1)
                    pe.wait_ge(s["v_copied"], b + 1)
                    for q in range(BT):
                        pe.matmul(ps_v[:, q, :], xnT[:, P * q:P * q + P], wqkv[:, 2, :], start=True, stop=False)
                        last = pe.matmul(ps_v[:, q, :], ones_row[:], bv[:], start=False, stop=True)
                    last.then_inc(s["v_mm"], 1)
                    for w in range(2):
                        pe.wait_ge(s["biased"], 2 * b + w + 1)
                        for c in range(L // 512):
                            last = pe.matmul(ps_q[:, w, 512 * c:512 * c + 512], wqkv[:, w, :],
                                             xnT[:, 512 * c:512 * c + 512], start=True, stop=True)
                        last.then_inc(s["q_mm"], 1)
                    if again:
                        turn(b + 1)

                turn(0)
                with pe.Fori(0, BATCHES - 1) as b:
                    project(b, True)
                project(BATCHES - 1, False)

        with ExitStack() as main_stack:
            mm = Stage(nc, main_stack, "heads")
            top = mm.sb("top", [P, 2, 2, BT, 2])
            neg = mm.sb("neg", [P, 2, BT])
            neg_row = mm.sb("neg_row", [2 * BT, P])
            neg_part = mm.sb("neg_part", [2 * BT, MAX_PARTS, P], BF16)
            pT = mm.sb("pT", [P, 2, 2, L])
            oT = mm.sb("oT", [P, 512])
            recip = mm.sb("recip", [P, 4, 4])
            o_tok = mm.sb("o_tok", [P, TILES, C])
            oTa = mm.sb("oTa", [P, L])
            ps_s = mm.ps("ps_s", [P, 2, L])
            ps_m = mm.ps("ps_m", [P, MAX_BANKS, 512])
            ps_o = mm.ps("ps_o", [P, 512])
            ps_t = ps_o[:].rearrange("p (q a d) -> p q a d", q=4, a=4)
            names = ("own v_pair s_mm prob pv_step oT o_turned o_norm m_mm top neg neg_turned neg_copied "
                     "neg_work neg_split neg_stored a_turned a_copied out_mm added").split()
            s = {n: mm.sem(n) for n in names}
            first = [mm.sem(f"first{k}_loaded") for k in range(2)]
            second = [mm.sem(f"second{k}_loaded") for k in range(2)]
            block = main_stack.enter_context(nc.Block())
            MAXES = 4 * BT
            UNITS = 2 * BT
            LEAD = 2
            NEG_BANK = 2
            UNCOVERED = (0, 28, 31)
            NEG_STORES = 16 * 2

            def each_pair(loop, step):
                def pairs(b, rounds):
                    with loop(rounds, 2) as i:
                        for k in range(2):
                            step(b * PAIRS + i * 2 + k, b, i * 2 + k, k, True)

                with loop(BATCHES - 1, PAIRS) as b:
                    pairs(b, PAIRS // 2)
                b = BATCHES - 1
                pairs(b, (PAIRS - LEAD) // 2)
                for k in range(2):
                    pair = PAIRS - LEAD + k
                    step(b * PAIRS + pair, b, pair, k, False)

            @block.sync
            def _(sp):
                def rows(dram, g, n):
                    of_pair = dram.rearrange("b h r t -> (b h) r t")[bass.ds(g * 2, 2), 0:n, :]
                    return [of_pair[j] for j in range(2)]

                def load_first(g, k):
                    q_rows, k_rows = rows(q_dram, g, QR), rows(k_dram, g, QR)
                    sp.wait_ge(s["m_mm"], MAXES * (g + 1))
                    for j in range(2):
                        sp.dma_start(q1[64 * j:64 * j + QR, k, j, :], q_rows[j]).then_inc(first[k], 16)
                        sp.dma_start(k1[64 * j:64 * j + QR, k, :], k_rows[j]).then_inc(first[k], 16)

                def step(g, b, pair, k, with_first):
                    if with_first:
                        load_first(g + LEAD, k)

                    def head_rows(dram, j, n):
                        return dram[bass.ds(b, 1), bass.ds(pair * 2 + j, 1), 0:n, :].rearrange("b h r t -> (b h r) t")
                    sp.wait_ge(s["s_mm"], UNITS * (g + 1))
                    sp.wait_ge(s["neg_split"], g + 1)
                    for j in range(2):
                        sp.dma_start(head_rows(q_dram, j, KR)[QR:KR, :].rearrange("n (t c) -> t n c", c=P),
                                     neg_part[BT * j:BT * j + BT]).then_inc(s["neg_stored"], 16)
                    sp.wait_ge(s["neg_stored"], NEG_STORES * (g + 2))
                    for j in range(2):
                        sp.dma_start(k2[64 * j:64 * j + QR, k, j, :], head_rows(k_dram, j, QR)).then_inc(second[k], 16)
                    for j in range(2):
                        sp.dma_start(q2[64 * j:64 * j + KR, k, :], head_rows(q_dram, j, KR)).then_inc(second[k], 16)

                for k in range(LEAD):
                    load_first(k, k)
                each_pair(lambda n, pairs: sp.Fori(0, n), step)

            @block.gpsimd
            def _(pool):
                def split_neg(g):
                    pool.wait_ge(s["neg_stored"], NEG_STORES * (g + 1))
                    pool.wait_ge(s["neg_copied"], g + 1)
                    work = s["neg_work"]
                    pool.tensor_tensor(neg_part[:, 0, :], neg_row[:], ones[:], ALU.mult).then_inc(work, 1)
                    pool.wait_ge(work, 3 * g + 1)
                    pool.tensor_tensor(neg_row[:], neg_row[:], neg_part[:, 0, :], ALU.subtract).then_inc(work, 1)
                    pool.wait_ge(work, 3 * g + 2)
                    pool.tensor_tensor(neg_part[:, 1, :], neg_row[:], ones[:], ALU.mult).then_inc(work, 1)
                    pool.wait_ge(work, 3 * g + 3)
                    pool.tensor_tensor(neg_part[:, 2, :], neg_row[:], neg_part[:, 1, :],
                                       ALU.subtract).then_inc(s["neg_split"], 1)

                def step(g, b, pair, k, with_first):
                    pool.wait_ge(s["pv_step"], BT * g + 2)
                    pool.tensor_copy(v_pair[:, :, :, 0:VW],
                                     v_aug[:, bass.ds(b, 1), :, bass.ds(pair * 2, 2), :]
                                     .rearrange("p a t h d -> p (a t) h d")).then_inc(s["v_pair"], 1)
                    if with_first or k == 0:
                        split_neg(g + 1)

                pool.sem_inc(s["neg_stored"], NEG_STORES)
                split_neg(0)
                each_pair(lambda n, pairs: pool.Fori(0, n), step)

            @block.scalar
            def _(act):
                def copy_neg(g, again):
                    act.wait_ge(s["neg_turned"], g + 1)
                    if again:
                        act.wait_ge(s["neg_split"], g)
                    act.activation(neg_row[:], ps_m[0:2 * BT, NEG_BANK, 0:P], ACT.Copy).then_inc(s["neg_copied"], 1)

                def step(g, b, pair, k, with_first):
                    if with_first or k == 0:
                        copy_neg(g + 1, True)
                    for t in range(BT):
                        for j in range(2):
                            act.wait_ge(s["s_mm"], UNITS * (g + 2) + 2 * t + j + 1)
                            act.wait_ge(s["pv_step"], BT * g + t + 1)
                            act.activation(pT[:, t % 2, j, :], ps_s[:, j, :], ACT.Exp, scale=SCALE).then_inc(s["prob"], 1)
                    act.wait_ge(s["pv_step"], BT * (g + 1) + 2)
                    act.wait_ge(s["o_turned"], g + 1)
                    act.activation(oT[:], ps_o[:], ACT.Copy).then_inc(s["oT"], 1)

                copy_neg(0, False)
                each_pair(lambda n, pairs: act.Fori(0, n), step)
                for b in range(BATCHES):
                    act.wait_ge(s["a_turned"], b + 1)
                    if b:
                        act.wait_ge(s["out_mm"], b)
                    act.activation(oTa[:], ps_s[:, 0, :], ACT.Copy).then_inc(s["a_copied"], 1)

            @block.tensor
            def _(pe):
                pe.sem_inc(s["m_mm"], 2 * MAXES)
                pe.sem_inc(s["s_mm"], 2 * UNITS)
                pe.sem_inc(s["pv_step"], 2)

                def max_unit(g, k, n, turned):
                    q, j, c = n // 4, (n // 2) % 2, n % 2
                    pe.wait_ge(s["top"], MAXES * g + (n if n >= MAX_BANKS else min(n + 1, 2)))
                    if n == NEG_BANK and turned:
                        pe.wait_ge(s["neg_copied"], g)
                    pe.matmul(ps_m[:, n % MAX_BANKS, :], q1[:, k, j, P * q:P * q + P], k1[:, k, 512 * c:512 * c + 512],
                              start=True, stop=True).then_inc(s["m_mm"], 1)

                def turn_neg(g):
                    pe.wait_ge(s["neg"], g + 1)
                    pe.transpose(ps_m[0:2 * BT, NEG_BANK, 0:P], neg[:].rearrange("p j t -> p (j t)"),
                                 ident[:]).then_inc(s["neg_turned"], 1)

                def score(g, k, t, j, c):
                    if c == 0:
                        pe.wait_ge(s["prob"], UNITS * g + 2 * t + j + 1)
                    product = pe.matmul(ps_s[:, j, 512 * c:512 * c + 512], k2[:, k, j, P * t:P * t + P],
                                        q2[:, k, 512 * c:512 * c + 512], start=True, stop=True)
                    if c == L // 512 - 1:
                        product.then_inc(s["s_mm"], 1)

                def values(g, t):
                    pe.wait_ge(s["prob"], UNITS * g + 2 * t + 2 + 2)
                    if t == 0:
                        pe.wait_ge(s["v_pair"], g + 1)
                        pe.wait_ge(s["o_norm"], g + 1)
                    for j in range(2):
                        for c in range(2):
                            o = 32 * (2 * j + c)
                            last = pe.matmul(ps_o[o:o + 32, :], v_pair[:, t, j, :], pT[:, t % 2, j, 512 * c:512 * c + 512],
                                             start=(t == 0), stop=(t == BT - 1))
                    last.then_inc(s["pv_step"], 1)

                def step(g, b, pair, k, with_first):
                    units = iter(range(MAXES))

                    def cover(product=None):
                        if with_first and product not in UNCOVERED:
                            max_unit(g + LEAD, k, next(units), True)
                    pe.wait_ge(second[k], 32 * (g - k + 2))
                    if with_first:
                        pe.wait_ge(first[k], 32 * (g - k + LEAD + 2))
                    for t in range(BT):
                        for j in range(2):
                            score(g, k, t, j, 0)
                            cover(4 * t + 2 * j)
                            score(g, k, t, j, 1)
                            cover(4 * t + 2 * j + 1)
                            if (t, j) == (0, 0) and (with_first or k == 0):
                                turn_neg(g + 1)
                            if j == 1 and t:
                                values(g, t - 1)
                    cover()
                    cover()
                    values(g, BT - 1)
                    for _ in UNCOVERED[2:]:
                        cover()
                    pe.wait_ge(s["oT"], g + 1)
                    for q in range(4):
                        last = pe.transpose(ps_o[:, P * q:P * q + P], oT[:, P * q:P * q + P], ident[:])
                    last.then_inc(s["o_turned"], 1)

                def turn_out(b):
                    for q in range(BT):
                        last = pe.transpose(ps_s[:, 0, P * q:P * q + P], o_tok[:, b * BT + q, :], ident[:])
                    last.then_inc(s["a_turned"], 1)

                for k in range(LEAD):
                    pe.wait_ge(first[k], 64)
                    for n in range(MAXES):
                        if k and n == 0:
                            turn_neg(k - 1)
                        max_unit(k, k, n, k > 0)
                each_pair(lambda n, pairs: pe.Fori(0, n), step)
                pe.wait_ge(s["o_norm"], BATCHES * PAIRS + 1)
                turn_out(0)
                for b in range(BATCHES):
                    pe.wait_ge(s["a_copied"], b + 1)
                    if b + 1 < BATCHES:
                        turn_out(b + 1)
                    if b:
                        pe.wait_ge(s["added"], b)
                    for q in range(BT):
                        o = ps_s[:, 1, P * q:P * q + P]
                        pe.matmul(o, oTa[:, P * q:P * q + P], wp[:], start=True, stop=False)
                        last = pe.matmul(o, ones_row[:], bp[:], start=False, stop=True)
                    last.then_inc(s["out_mm"], 1)

            @block.vector
            def _(v):
                own = Tally(v, s["own"])
                v.sem_inc(s["top"], 2)
                v.sem_inc(s["prob"], 2)
                v.sem_inc(s["o_norm"], 1)
                v.sem_inc(s["o_turned"], 1)

                def negate(g, k):
                    v.wait_ge(s["top"], MAXES * (g + 1) + 2)
                    own.step(v.tensor_tensor(neg[:], top[:, k, :, :, 0], top[:, k, :, :, 1], ALU.max))
                    v.tensor_scalar(neg[:], neg[:], -1.0, None, ALU.mult).then_inc(s["neg"], 1)

                def first_pass(g, k):
                    for n in range(MAXES):
                        q, j, c = n // 4, (n // 2) % 2, n % 2
                        v.wait_ge(s["m_mm"], MAXES * (g + 2) + n + 1)
                        v.tensor_reduce(top[:, k, j, q, c:c + 1], ps_m[:, n % MAX_BANKS, :], AX.X,
                                        ALU.max).then_inc(s["top"], 1)
                    negate(g, k)

                def step(g, b, pair, k, with_first):
                    if with_first:
                        first_pass(g + LEAD, k)
                    v.wait_ge(s["o_turned"], g + 2)
                    own.step(v.reciprocal(recip[:], ps_t[:, :, :, D]))
                    for j in range(2):
                        for c in range(2):
                            last = v.tensor_tensor(
                                o_tok[:, bass.ds(b * BT + 4 * c, 4), bass.ds(pair * 2 * D + j * D, D)],
                                ps_t[:, :, 2 * j + c, 0:D],
                                recip[:, :, 2 * j + c:2 * j + c + 1].broadcast_to([P, 4, D]), ALU.mult)
                    last.then_inc(s["o_norm"], 1)

                def add(b):
                    v.wait_ge(s["out_mm"], b + 1)
                    tok = x_tok[:, b * BT:b * BT + BT, :]
                    v.tensor_tensor(tok, tok, ps_s[:, 1, :].rearrange("p (t c) -> p t c", c=C),
                                    ALU.add).then_inc(s["added"], 1)

                for k in range(LEAD):
                    first_pass(k, k)
                each_pair(lambda n, pairs: own.loop(n, 2 * pairs), step)
                for b in range(BATCHES):
                    add(b)
                v.wait_ge(s["added"], BATCHES)


def build_program(nc, x, ln_w, ln_b, in_w, conv_w, conv_b, xp_w, dtp_w, dtp_b, A_log, D_skip, out_w, nf_w, nf_b,
                  Wr, br, W1, W2, w_qkv, b_qkv, w_proj, b_proj, W, b, lora_down, lora_up, down_aux, up_aux, out):
    B, L, _ = x.shape
    TILES = B * L // P
    E = Wr.shape[1]
    HEADS, D = 16, C // 16
    with ExitStack() as stack:
        x_tok = stack.enter_context(nc.sbuf_tensor("x_tok", [P, TILES, C], F32))
        ident = stack.enter_context(nc.sbuf_tensor("ident", [P, P], F32))
        tri = stack.enter_context(nc.sbuf_tensor("tri", [P, P], BF16))
        ones_bf = stack.enter_context(nc.sbuf_tensor("ones_bf", [P, P], BF16))
        wT = stack.enter_context(nc.sbuf_tensor("wT", [P, C], F32))
        b_row = stack.enter_context(nc.sbuf_tensor("b_row", [1, C], F32))
        ones_row = stack.enter_context(nc.sbuf_tensor("ones_row", [1, C], F32))
        sorted_x = nc.dram_tensor("sorted_x", [(TILES + E) * P, C], F32, kind="Internal").ap()
        sorted_y = nc.dram_tensor("sorted_y", [(TILES + E) * P, C], F32, kind="Internal").ap()
        q_rows = nc.dram_tensor("q_rows", [B, HEADS, len(Q_PARTS) * D + MAX_PARTS, L], BF16, kind="Internal").ap()
        k_rows = nc.dram_tensor("k_rows", [B, HEADS, len(K_PARTS) * D, L], BF16, kind="Internal").ap()
        tokens = "b (t p) c -> p (b t) c"
        load_stage(nc, x.rearrange(tokens, p=P), x_tok, ident, tri, ones_bf)
        moe_stage(nc, "moe0", x_tok, ident, tri, ones_bf, Wr, br, W1, W2, sorted_x, sorted_y, True)
        mamba_stage(nc, x_tok, ident, ln_w, ln_b, in_w, conv_w, conv_b, xp_w, dtp_w, dtp_b, A_log, D_skip, out_w,
                    nf_w, nf_b)
        moe_stage(nc, "moe1", x_tok, ident, tri, ones_bf, Wr, br, W1, W2, sorted_x, sorted_y, False)
        lora_weight_stage(nc, ident, wT, b_row, ones_row, W, b, lora_down, lora_up, down_aux, up_aux)
        linear_stage(nc, "linear0", x_tok, ident, wT, b_row, ones_row)
        attention_stage(nc, x_tok, ident, ones_row, w_qkv, b_qkv, w_proj, b_proj, q_rows, k_rows)
        linear_stage(nc, "linear1", x_tok, ident, wT, b_row, ones_row)
        store_stage(nc, x_tok, out.rearrange(tokens, p=P))


_INS = ["L0_attn_x", "L0_attn_ln_w", "L0_attn_ln_b", "L0_attn_in_proj_w", "L0_attn_conv_w", "L0_attn_conv_b",
        "L0_attn_x_proj_w", "L0_attn_dt_proj_w", "L0_attn_dt_proj_b", "L0_attn_A_log", "L0_attn_D_skip",
        "L0_attn_out_proj_w", "L0_attn_norm_f_w", "L0_attn_norm_f_b", "L0_ffn_Wr", "L0_ffn_br", "L0_ffn_W1",
        "L0_ffn_W2", "L1_attn_w_qkv", "L1_attn_b_qkv", "L1_attn_w_proj", "L1_attn_b_proj", "L1_ffn_W", "L1_ffn_b",
        "L1_ffn_lora_down", "L1_ffn_lora_up", "L1_ffn_down_aux", "L1_ffn_up_aux"]
_OUTS = [((4, 1024, 128), "float32")]


def kernel(**inputs):
    import numpy as _np
    import concourse.bacc as _bacc
    from concourse import mybir as _mybir
    from concourse.bass_utils import run_bass_kernel_spmd as _run

    nc = _bacc.Bacc("TRN2", target_bir_lowering=False, num_devices=1)
    arrays, args = {}, []
    for name in _INS:
        a = _np.ascontiguousarray(inputs[name])
        arrays[f"in_{name}_dram"] = a
        args.append(nc.dram_tensor(f"in_{name}_dram", a.shape, _mybir.dt.from_np(a.dtype), kind="ExternalInput").ap())
    for i, (shape, dtype) in enumerate(_OUTS):
        dt = _mybir.dt.from_np(_np.dtype(dtype))
        args.append(nc.dram_tensor(f"out_{i}_dram", shape, dt, kind="ExternalOutput").ap())
    build_program(nc, *args)
    r = _run(nc, [arrays], core_ids=[0])
    got = tuple(r.results[0][f"out_{i}_dram"] for i in range(len(_OUTS)))
    return got[0]
```
